# Optimizing a Trainium2 kernel written in Bass

```python
import numpy as np
import jax
import jax.numpy as jnp

def _softmax(x, axis=-1):
    return jax.nn.softmax(x, axis=axis)

def _gelu(x):
    return jax.nn.gelu(x, approximate=True)

def _silu(x):
    return jax.nn.silu(x)

def _sigmoid(x):
    return jax.nn.sigmoid(x)

def _layernorm(x, axis=-1, eps=1e-05):
    m = jnp.mean(x, axis=axis, keepdims=True)
    v = jnp.var(x, axis=axis, keepdims=True)
    return (x - m) / jnp.sqrt(v + eps)

def _scatter_add(tgt, idx, src, axis=0):
    return tgt.at[idx].add(src)

def _segment_sum(src, seg, n):
    return jax.ops.segment_sum(src, seg, n)
kernel_name = 'mk_gnn_ffn_d1_gnn_r8_915514'

def setup_inputs(seed: int=0):
    np.random.seed(seed)
    _w = jnp.asarray

    def _rec_inputs():
        import jax
        import jax.numpy as jnp
        _gk = jax.random.key(seed)
        x = -0.0002117 + 1 * jax.random.normal(jax.random.fold_in(_gk, 1), (6250, 256), jnp.float32)
        _s = jax.random.randint(jax.random.fold_in(_gk, 2), (50000,), 0, 6250, jnp.int32)
        _d = jax.random.randint(jax.random.fold_in(_gk, 3), (50000,), 0, 6250, jnp.int32)
        _loop = jnp.arange(6250, dtype=jnp.int32)
        src = jnp.concatenate([_s, _d, _loop])
        dst = jnp.concatenate([_d, _s, _loop])
        _o = jnp.argsort(dst, stable=True)
        src = src[_o]
        dst = dst[_o]
        return (x, src, dst)
    x, src, dst = _rec_inputs()

    def _L0_gnn_setup():
        import jax, jax.numpy as jnp
        import numpy as np
        N_NODES = 12500
        NUM_FEATS = 256
        DIM = 256
        N_EDGES = 40000
        BN_EPS = 1e-05
        key = jax.random.key(seed)
        ks = jax.random.split(key, 16)
        x = jax.random.normal(ks[0], (N_NODES, NUM_FEATS), dtype=jnp.float32)
        edge_index = jax.random.randint(ks[1], (2, N_EDGES), 0, N_NODES, dtype=jnp.int64)
        s = 0.02
        inp = {'x': x, 'edge_index': edge_index}
        inp['W1a'] = jax.random.normal(ks[2], (NUM_FEATS, DIM), dtype=jnp.float32) * s
        inp['b1a'] = jnp.zeros((DIM,), jnp.float32)
        inp['W1b'] = jax.random.normal(ks[3], (DIM, DIM), dtype=jnp.float32) * s
        inp['b1b'] = jnp.zeros((DIM,), jnp.float32)
        inp['g1'] = jnp.ones((DIM,), jnp.float32)
        inp['be1'] = jnp.zeros((DIM,), jnp.float32)
        inp['W2a'] = jax.random.normal(ks[4], (DIM, DIM), dtype=jnp.float32) * s
        inp['b2a'] = jnp.zeros((DIM,), jnp.float32)
        inp['W2b'] = jax.random.normal(ks[5], (DIM, DIM), dtype=jnp.float32) * s
        inp['b2b'] = jnp.zeros((DIM,), jnp.float32)
        inp['g2'] = jnp.ones((DIM,), jnp.float32)
        inp['be2'] = jnp.zeros((DIM,), jnp.float32)
        inp['W3a'] = jax.random.normal(ks[6], (DIM, DIM), dtype=jnp.float32) * s
        inp['b3a'] = jnp.zeros((DIM,), jnp.float32)
        inp['W3b'] = jax.random.normal(ks[7], (DIM, DIM), dtype=jnp.float32) * s
        inp['b3b'] = jnp.zeros((DIM,), jnp.float32)
        inp['g3'] = jnp.ones((DIM,), jnp.float32)
        inp['be3'] = jnp.zeros((DIM,), jnp.float32)
        return inp
    _L0_gnn_all = _L0_gnn_setup()
    _L0_gnn_in = {k: v for k, v in _L0_gnn_all.items() if k in ('W1a', 'b1a', 'W1b', 'b1b', 'g1', 'be1', 'W2a', 'b2a', 'W2b', 'b2b', 'g2', 'be2', 'W3a', 'b3a', 'W3b', 'b3b', 'g3', 'be3')}
    del _L0_gnn_all

    def _L0_ffn_setup():
        import math
        import jax, jax.numpy as jnp
        import numpy as np
        CAPACITY_FACTOR = 1.25
        key = jax.random.key(seed)
        ks = jax.random.split(key, 5)
        B, L, D, F, E = (8, 1024, 256, 1024, 8)
        h = jax.random.normal(ks[0], (B, L, D), dtype=jnp.float32)
        gate_w = jax.random.normal(ks[1], (D, E), dtype=jnp.float32) * 0.02
        gate_b = jnp.zeros((E,), dtype=jnp.float32)
        w1 = jax.random.normal(ks[2], (E, D, F), dtype=jnp.float32) * (1.0 / math.sqrt(D))
        b1 = jnp.zeros((E, F), dtype=jnp.float32)
        w2 = jax.random.normal(ks[3], (E, F, D), dtype=jnp.float32) * (1.0 / math.sqrt(F))
        b2 = jnp.zeros((E, D), dtype=jnp.float32)
        return {'h': h, 'gate_w': gate_w, 'gate_b': gate_b, 'w1': w1, 'b1': b1, 'w2': w2, 'b2': b2}
    _L0_ffn_all = _L0_ffn_setup()
    _L0_ffn_in = {k: v for k, v in _L0_ffn_all.items() if k in ('gate_w', 'gate_b', 'w1', 'b1', 'w2', 'b2')}
    del _L0_ffn_all
    return {'x': x, 'src': src, 'dst': dst, 'L0_gnn_W1a': _L0_gnn_in['W1a'], 'L0_gnn_b1a': _L0_gnn_in['b1a'], 'L0_gnn_W1b': _L0_gnn_in['W1b'], 'L0_gnn_b1b': _L0_gnn_in['b1b'], 'L0_gnn_g1': _L0_gnn_in['g1'], 'L0_gnn_be1': _L0_gnn_in['be1'], 'L0_gnn_W2a': _L0_gnn_in['W2a'], 'L0_gnn_b2a': _L0_gnn_in['b2a'], 'L0_gnn_W2b': _L0_gnn_in['W2b'], 'L0_gnn_b2b': _L0_gnn_in['b2b'], 'L0_gnn_g2': _L0_gnn_in['g2'], 'L0_gnn_be2': _L0_gnn_in['be2'], 'L0_gnn_W3a': _L0_gnn_in['W3a'], 'L0_gnn_b3a': _L0_gnn_in['b3a'], 'L0_gnn_W3b': _L0_gnn_in['W3b'], 'L0_gnn_b3b': _L0_gnn_in['b3b'], 'L0_gnn_g3': _L0_gnn_in['g3'], 'L0_gnn_be3': _L0_gnn_in['be3'], 'L0_ffn_gate_w': _L0_ffn_in['gate_w'], 'L0_ffn_gate_b': _L0_ffn_in['gate_b'], 'L0_ffn_w1': _L0_ffn_in['w1'], 'L0_ffn_b1': _L0_ffn_in['b1'], 'L0_ffn_w2': _L0_ffn_in['w2'], 'L0_ffn_b2': _L0_ffn_in['b2']}

def reference(x, src, dst, L0_gnn_W1a, L0_gnn_b1a, L0_gnn_W1b, L0_gnn_b1b, L0_gnn_g1, L0_gnn_be1, L0_gnn_W2a, L0_gnn_b2a, L0_gnn_W2b, L0_gnn_b2b, L0_gnn_g2, L0_gnn_be2, L0_gnn_W3a, L0_gnn_b3a, L0_gnn_W3b, L0_gnn_b3b, L0_gnn_g3, L0_gnn_be3, L0_ffn_gate_w, L0_ffn_gate_b, L0_ffn_w1, L0_ffn_b1, L0_ffn_w2, L0_ffn_b2):
    import jax
    import jax.numpy as jnp

    def _L0_gnn_ref(x, edge_index, W1a, b1a, W1b, b1b, g1, be1, W2a, b2a, W2b, b2b, g2, be2, W3a, b3a, W3b, b3b, g3, be3):
        import jax, jax.numpy as jnp
        import numpy as np
        N_NODES = 12500
        NUM_FEATS = 256
        DIM = 256
        N_EDGES = 40000
        BN_EPS = 1e-05
        src, dst = (edge_index[0], edge_index[1])
        n = x.shape[0]

        def gin(h, Wa, ba, Wb, bb):
            agg = h + jax.ops.segment_sum(h[src], dst, num_segments=n)
            hid = jax.nn.relu(agg @ Wa + ba)
            return hid @ Wb + bb

        def bn(h, g, b):
            mu = h.mean(axis=0)
            var = h.var(axis=0)
            return (h - mu) * jax.lax.rsqrt(var + BN_EPS) * g + b
        h = bn(jax.nn.relu(gin(x, W1a, b1a, W1b, b1b)), g1, be1)
        h = bn(jax.nn.relu(gin(h, W2a, b2a, W2b, b2b)), g2, be2)
        h = bn(jax.nn.relu(gin(h, W3a, b3a, W3b, b3b)), g3, be3)
        return h

    def _L0_ffn_ref(h, gate_w, gate_b, w1, b1, w2, b2):
        import math
        import jax, jax.numpy as jnp
        import numpy as np
        CAPACITY_FACTOR = 1.25
        B, L, D = h.shape
        E = gate_w.shape[1]
        T = B * L
        C = max(1, math.ceil(CAPACITY_FACTOR * T / E))
        x = h.reshape(T, D)
        logits = x @ gate_w + gate_b
        probs = jax.nn.softmax(logits, axis=-1)
        idx = jnp.argmax(probs, axis=-1)
        prb = jnp.take_along_axis(probs, idx[:, None], axis=1)[:, 0]
        one_hot = jax.nn.one_hot(idx, E, dtype=jnp.float32)
        pos = (jnp.cumsum(one_hot, axis=0) * one_hot).sum(-1).astype(jnp.int32) - 1
        kept = pos < C
        pos_safe = jnp.where(kept, pos, C)
        buf = jnp.zeros((E, C, D), dtype=h.dtype).at[idx, pos_safe].set(x, mode='drop')
        hmid = jax.nn.relu(jnp.einsum('ecd,edf->ecf', buf, w1) + b1[:, None, :])
        ybuf = jnp.einsum('ecf,efd->ecd', hmid, w2) + b2[:, None, :]
        pos_g = jnp.minimum(pos, C - 1)
        y_tok = ybuf[idx, pos_g] * (prb * kept)[:, None]
        y = y_tok.reshape(B, L, D)
        y = jnp.nan_to_num(y, nan=0.0, posinf=10000.0, neginf=-10000.0)
        return y
    edge_index = jnp.stack([src, dst])
    x = x + _L0_gnn_ref(_layernorm(x, axis=-1), edge_index, L0_gnn_W1a, L0_gnn_b1a, L0_gnn_W1b, L0_gnn_b1b, L0_gnn_g1, L0_gnn_be1, L0_gnn_W2a, L0_gnn_b2a, L0_gnn_W2b, L0_gnn_b2b, L0_gnn_g2, L0_gnn_be2, L0_gnn_W3a, L0_gnn_b3a, L0_gnn_W3b, L0_gnn_b3b, L0_gnn_g3, L0_gnn_be3)
    x = x + _L0_ffn_ref(_layernorm(x, axis=-1)[None], L0_ffn_gate_w, L0_ffn_gate_b, L0_ffn_w1, L0_ffn_b1, L0_ffn_w2, L0_ffn_b2)[0]
    return x

_drawn_inputs = setup_inputs


def setup_inputs(seed=0):
    import zlib

    import numpy as np

    out = dict(_drawn_inputs(seed))
    spreads = {'L0_gnn_b1a': (0.0, 0.1),
     'L0_gnn_b1b': (0.0, 0.1),
     'L0_gnn_g1': (1.0, 0.2),
     'L0_gnn_be1': (0.0, 0.1),
     'L0_gnn_b2a': (0.0, 0.1),
     'L0_gnn_b2b': (0.0, 0.1),
     'L0_gnn_g2': (1.0, 0.2),
     'L0_gnn_be2': (0.0, 0.1),
     'L0_gnn_b3a': (0.0, 0.1),
     'L0_gnn_b3b': (0.0, 0.1),
     'L0_gnn_g3': (1.0, 0.2),
     'L0_gnn_be3': (0.0, 0.1),
     'L0_ffn_gate_b': (0.0, 0.1),
     'L0_ffn_b1': (0.0, 0.8),
     'L0_ffn_b2': (0.0, 0.631)}
    factors = {}
    for name, (base, spread) in spreads.items():
        noise = np.random.default_rng([zlib.crc32(name.encode()), seed]).standard_normal(out[name].shape)
        drawn = base * np.exp(spread * noise) if base else spread * noise
        out[name] = jnp.asarray(drawn.astype(out[name].dtype))
    for name, factor in factors.items():
        out[name] = (out[name] * factor).astype(out[name].dtype)
    return out
```

```python
from contextlib import ExitStack

import numpy as np

import concourse.bass as bass
from concourse import mybir

F32 = mybir.dt.float32
I32 = mybir.dt.int32
ALU = mybir.AluOpType
ACT = mybir.ActivationFunctionType
AX = mybir.AxisListType

P = 128
N = 6250
D = 256
HALVES = D // P
E_GNN = 106250
LAYERS = 3
EPS = 1e-5

TILES = -(-N // P)
NPAD = TILES * P
TAIL = N - (TILES - 1) * P
BATCH = 7
BATCHES = TILES // BATCH
AGW = NPAD + P

CHUNKS = 4
GE = CHUNKS * P
GROUPS = -(-E_GNN // GE)
HALF_GROUPS = 4
SLOTS = HALF_GROUPS * CHUNKS
LOOPS = GROUPS // (2 * HALF_GROUPS)
GROWS = GROUPS // 2
LAST_E = E_GNN - (GROUPS - 1) * GE

NODES_B = 500
BLOCKS = N // NODES_B
TAIL_B = N - BLOCKS * NODES_B

EXPERTS = 8
FF = 1024
FC = FF // P
CAP = -(-5 * N // (4 * EXPERTS))
CAPP = 1024
CT = CAPP // P
CAP_N = (CAP + 1) // 2
NO_SLOT = EXPERTS * CAPP
NEG_INF = float("-inf")

SLOW_STEPS = 2 + TILES * 6

assert TILES % BATCH == 0 and GROUPS % (2 * HALF_GROUPS) == 0 and BLOCKS % 2 == 0
assert 0 < LAST_E < GE and 2 * CAP_N <= CAPP and CAP <= CAPP and GROWS <= P


def gnn_moe_program(nc, t, out):
    with ExitStack() as ctx:
        def sb(name, shape, dt=F32):
            return ctx.enter_context(nc.sbuf_tensor(name, shape, dt))

        def sem(name):
            return ctx.enter_context(nc.semaphore(name))

        h_dram = [nc.dram_tensor(f"h_dram{i}", (NPAD, D), F32, kind="Internal").ap() for i in range(LAYERS)]
        dispatch_dram = nc.dram_tensor("dispatch_dram", (EXPERTS * CAPP, D), F32, kind="Internal").ap()
        answer_dram = nc.dram_tensor("answer_dram", (EXPERTS * CAPP, D), F32, kind="Internal").ap()

        agg = sb("agg", [P, HALVES, AGW])
        x_sb = sb("x_sb", [P, TILES, D])
        arena = sb("arena", [P, TILES * D])
        tokens = arena[:, :].rearrange("p (t d) -> p t d", d=D)

        at = 0

        def carve(words):
            nonlocal at
            at += words
            assert at <= TILES * D
            return arena[:, at - words:at]

        rows = carve(SLOTS * D).rearrange("p (s d) -> p s d", d=D)
        onehot = carve(2 * GE).rearrange("p (b c n) -> p b c n", b=2, c=CHUNKS)
        prep0 = at

        def carve_prep(dt=F32):
            return carve(2 * GE).bitcast(dt).rearrange("p (q e) -> p q e", q=2)

        src_i, dst_i = carve_prep(I32), carve_prep(I32)
        src_f, dst_f, key_f, rel_f, far_f = (carve_prep() for _ in range(5))
        hid = arena[:, prep0:prep0 + 2 * HALVES * NODES_B].rearrange("p (b m n) -> p b m n", b=2, m=HALVES)

        idx_cols = sb("idx_cols", [P, GROUPS * CHUNKS + SLOTS], I32)
        rel_cols = sb("rel_cols", [P, GROUPS * CHUNKS])
        far_cols = sb("far_cols", [P, GROUPS * CHUNKS])
        idx_now = sb("idx_now", [P, 2, SLOTS], I32)
        base = sb("base", [P, 2])
        any_far = sb("any_far", [P, 1])
        base_row = sb("base_row", [1, GROUPS], I32)
        far_flag_f = sb("far_flag_f", [1, 1])
        far_flag = sb("far_flag", [1, 1], I32)
        slow_idx = sb("slow_idx", [P, 1], I32)
        slow_rel = sb("slow_rel", [P, 1])

        ident = sb("ident", [P, P])
        ones = sb("ones", [P, P])
        upto = sb("upto", [P, P])
        zeros = sb("zeros", [P, D])
        iota_i = sb("iota_i", [P, P], I32)
        iota = sb("iota", [P, P])
        eps_col = sb("eps_col", [P, 1])

        w_gnn = sb("w_gnn", [P, LAYERS, 2, HALVES, D])
        gate_w = sb("gate_w", [P, HALVES, EXPERTS])
        gate_b = sb("gate_b", [P, EXPERTS])
        b2_all = sb("b2_all", [P, EXPERTS, D])
        VEC0 = EXPERTS * FC
        PARAMS = 1 + LAYERS * 6 + 3
        NVEC = VEC0 + LAYERS * 4 * HALVES
        vec_rows = sb("vec_rows", [NVEC, P])
        vecs = sb("vecs", [P, NVEC])

        partial = sb("partial", [P, 2, D])
        nm = sb("nm", [P, BATCH, D])
        fm = sb("fm", [P, BATCH, HALVES, P])
        bn_st = sb("bn_st", [P, HALVES, BLOCKS + 1, 6])
        bn_mv = sb("bn_mv", [P, HALVES, 2])
        bn_w = sb("bn_w", [P, 6, HALVES])
        ln_st = sb("ln_st", [P, BATCH, 6])
        ln_w = sb("ln_w", [P, 10, BATCH])

        TE = TILES * EXPERTS
        tok_i = sb("tok_i", [P, TILES], I32)
        exp_i = sb("exp_i", [P, TE], I32)
        route = sb("route", [P, 14, TILES])
        scatter_idx = sb("scatter_idx", [P, TILES], I32)
        gather_idx = sb("gather_idx", [P, TILES], I32)

        agg_flat = agg[:, :, :].rearrange("p m n -> p (m n)")
        WX = 2 * FC * D
        w_exp = agg_flat[:, 0:2 * WX].rearrange("p (s w) -> p s w", s=2)
        bufT = agg_flat[:, 2 * WX:2 * WX + HALVES * CAPP].rearrange("p (k n) -> p k n", k=HALVES)
        y_out = agg_flat[:, 2 * WX + 2 * CAPP:2 * WX + 2 * CAPP + CT * D].rearrange("p (c d) -> p c d", c=CT)
        hmid = arena[:, 0:FC * CAPP].rearrange("p (f n) -> p f n", f=FC)
        buf = arena[:, FC * CAPP:FC * CAPP + 2 * CT * D].rearrange("p (s c d) -> p s c d", s=2, c=CT)

        nm_flat = nm[:, :, :].rearrange("p a b -> p (a b)")
        fm_flat = fm[:, :, :, :].rearrange("p a m b -> p (a m b)")
        r_exp, r_a, r_b, r_c = (nm_flat[:, i * TE:(i + 1) * TE] for i in range(4))
        r_d, r_e, r_f, r_g = (fm_flat[:, i * TE:(i + 1) * TE] for i in range(4))

        bank = [ctx.enter_context(nc.psum_tensor(f"bank{i}", [P, 512], F32)) for i in range(8)]

        cleared = sem("cleared")
        consts = sem("consts")
        edges_in = sem("edges_in")
        x_in = sem("x_in")
        params_in = sem("params_in")
        prep = sem("prep")
        edges_ready = sem("edges_ready")
        prep_turned = sem("prep_turned")
        vecs_turned = sem("vecs_turned")
        vecs_ready = sem("vecs_ready")
        tables_ready = sem("tables_ready")
        gate_passed = sem("gate_passed")
        ln_steps = sem("ln_steps")
        ln_var = sem("ln_var")
        ln_std = sem("ln_std")
        ln_ready = sem("ln_ready")
        x_normed, x_turned, x_in_agg = sem("x_normed"), sem("x_turned"), sem("x_in_agg")
        stored = [sem(f"stored{i}") for i in range(BATCH)]
        h_normed, h_turned, h_read, agg_set = sem("h_normed"), sem("h_turned"), sem("h_read"), sem("agg_set")
        idx_staged = sem("idx_staged")
        landed = [sem(f"landed{i}") for i in range(SLOTS)]
        onehot_ready = sem("onehot_ready")
        summed = sem("summed")
        partial_copied = sem("partial_copied")
        sums_turned = sem("sums_turned")
        added = sem("added")
        turn = sem("turn")
        slow_landed = sem("slow_landed")
        hid_summed = sem("hid_summed")
        hid_ready = sem("hid_ready")
        out_summed = sem("out_summed")
        out_stored = sem("out_stored")
        bn_seen = sem("bn_seen")
        bn_var = sem("bn_var")
        bn_std = sem("bn_std")
        bn_ready = sem("bn_ready")
        tok_normed, tok_turned, tok_copied = sem("tok_normed"), sem("tok_turned"), sem("tok_copied")
        tok_kept, tok_scored = sem("tok_kept"), sem("tok_scored")
        exp_in = sem("exp_in")
        exp_done = sem("exp_done")
        chosen = sem("chosen")
        counted = sem("counted")
        routed = sem("routed")
        zero_filled = sem("zero_filled")
        scattered = sem("scattered")
        w_in = [sem(f"w_in{i}") for i in range(2)]
        buf_in = [sem(f"buf_in{i}") for i in range(2)]
        bufT_turned = sem("bufT_turned")
        bufT_copied = sem("bufT_copied")
        f_summed = sem("f_summed")
        f_ready = sem("f_ready")
        y_summed = sem("y_summed")
        y_added = sem("y_added")
        y_stored = [sem(f"y_stored{i}") for i in range(CT // 2)]
        y_back = [sem(f"y_back{i}") for i in range(2 * BATCH)]
        hmid_padded = sem("hmid_padded")
        y_scaled = sem("y_scaled")
        y_done = sem("y_done")
        out_done = sem("out_done")

        def gate(eng, semaphore, value):
            eng.wait_ge(semaphore, value)
            eng.sem_inc(gate_passed, 1)

        def y_slot(i):
            return nm[:, i % BATCH, :] if i // BATCH % 2 else fm[:, i % BATCH].rearrange("p m n -> p (m n)")

        def wgt(layer, which, k, m):
            return w_gnn[:, layer, which, k, m * P:(m + 1) * P]

        def vec(layer, which, m):
            c = VEC0 + (layer * 4 + which) * HALVES + m
            return vecs[:, c:c + 1]

        block = ctx.enter_context(nc.Block())

        @block.sync
        def _(sp):
            sp.wait_ge(cleared, 2)
            for flat, dst in ((t["dst"], dst_i), (t["src"], src_i)):
                sp.dma_start(dst[0:GROWS, 0, :],
                             flat[0:GROWS * GE].rearrange("(p e) -> p e", e=GE)).then_inc(edges_in, 16)
                sp.dma_start(dst[0:GROWS - 1, 1, :],
                             flat[GROWS * GE:(GROUPS - 1) * GE].rearrange("(p e) -> p e", e=GE)).then_inc(edges_in, 16)
                sp.dma_start(dst[GROWS - 1:GROWS, 1, 0:LAST_E],
                             flat[(GROUPS - 1) * GE:E_GNN].rearrange("(p e) -> p e", p=1)).then_inc(edges_in, 16)
            sp.wait_ge(cleared, 3)
            for i in range(BATCHES):
                lo, hi = i * BATCH, (i + 1) * BATCH if i < BATCHES - 1 else TILES - 1
                sp.dma_start(x_sb[:, lo:hi, :],
                             t["x"][lo * P:hi * P, :].rearrange("(t p) d -> p t d", p=P)).then_inc(x_in, 16)
            sp.dma_start(x_sb[0:TAIL, TILES - 1, :], t["x"][(TILES - 1) * P:N, :]).then_inc(x_in, 16)

            for layer in range(LAYERS):
                with sp.Fori(0, BATCHES) as i:
                    for j in range(BATCH):
                        if layer == 0:
                            sp.wait_ge(x_normed, i * BATCH + j + 1)
                        else:
                            sp.wait_ge(h_read, (layer - 1) * TILES + i * BATCH + j + 1 + BATCH)
                        sp.dma_start(h_dram[layer][bass.ds((i * BATCH + j) * P, P), :], nm[:, j, :]).then_inc(stored[j], 16)
                if layer == 0:
                    sp.wait_ge(consts, 1)
                    for e in range(EXPERTS):
                        sp.dma_start(dispatch_dram[e * CAPP:(e + 1) * CAPP, :].rearrange("(p c) d -> p c d", p=P),
                                     zeros[:, :].unsqueeze(1).to_broadcast([P, CT, D])).then_inc(zero_filled, 16)

            def load_weights(e, s):
                for which, src, at0 in ((0, "L0_ffn_w1", 0), (1, "L0_ffn_w2", FC * D)):
                    src = t[src][bass.ds(e, 1)] if not isinstance(e, int) else t[src][e:e + 1]
                    c = HALVES if which == 0 else FC
                    sp.dma_start(w_exp[:, s, at0:at0 + FC * D].rearrange("p (c n) -> p c n", c=c),
                                 src.rearrange("o (c p) n -> (o p) c n", p=P)).then_inc(w_in[s], 16)

            def load_buf(e, s):
                sp.dma_start(buf[:, s], dispatch_dram[bass.ds(e * CAPP, CAPP), :].rearrange(
                    "(c p) d -> p c d", p=P)).then_inc(buf_in[s], 16)

            sp.wait_ge(h_normed, TILES * LAYERS)
            load_weights(0, 0)
            load_weights(1, 1)
            sp.wait_ge(scattered, 16 * TILES)
            load_buf(0, 0)
            load_buf(1, 1)

            def store_answers(e):
                for c in range(CT // 2):
                    sp.wait_ge(y_added, e * CT + 2 * c + 2 + 2)
                    sp.dma_start(answer_dram[bass.ds(e * CAPP + 2 * c * P, 2 * P), :].rearrange("(c p) d -> p c d", p=P),
                                 y_out[:, 2 * c:2 * c + 2, :]).then_inc(y_stored[c], 16)

            with sp.Fori(0, EXPERTS // 2 - 1) as i:
                for s in range(2):
                    store_answers(i * 2 + s)
                    load_weights(i * 2 + s + 2, s)
                    load_buf(i * 2 + s + 2, s)
            for e in range(EXPERTS - 2, EXPERTS):
                store_answers(e)

            for i in range(BATCHES):
                lo, hi = i * BATCH, (i + 1) * BATCH if i < BATCHES - 1 else TILES - 1
                sp.wait_ge(y_done, i + 1)
                sp.dma_start(out[lo * P:hi * P, :].rearrange("(t p) d -> p t d", p=P),
                             x_sb[:, lo:hi, :]).then_inc(out_done, 16)
            sp.dma_start(out[(TILES - 1) * P:N, :], x_sb[0:TAIL, TILES - 1, :]).then_inc(out_done, 16)
            sp.wait_ge(out_done, 16 * (BATCHES + 1))

        @block.gpsimd
        def _(pool):
            pool.memset(dst_i, -1).then_inc(cleared, 1)
            pool.memset(src_i, 0).then_inc(cleared, 1)
            pool.memset(x_sb[:, TILES - 1, :], 0.0).then_inc(cleared, 1)
            pool.memset(zeros[:, :], 0.0).then_inc(consts, 1)
            pool.memset(ones[:, :], 1.0).then_inc(consts, 1)
            pool.memset(eps_col[:, :], EPS).then_inc(consts, 1)
            pool.memset(idx_cols[:, GROUPS * CHUNKS:], 0).then_inc(consts, 1)
            pool.memset(agg[:, :, NPAD:AGW], 0.0).then_inc(consts, 1)
            pool.iota(iota_i[:, :], [[1, P]], base=0, channel_multiplier=0).then_inc(consts, 1)
            pool.iota(tok_i[:, :], [[P, TILES]], base=0, channel_multiplier=1).then_inc(consts, 1)
            pool.iota(exp_i[:, :], [[0, TILES], [1, EXPERTS]], base=0, channel_multiplier=0).then_inc(consts, 1)
            pool.sem_inc(agg_set, BATCH)
            pool.sem_inc(tok_kept, BATCH)
            pool.wait_ge(consts, 8)
            pool.affine_select(out=ident[:, :], in_=ones[:, :], pattern=[[-1, P]], compare_op=ALU.is_equal, fill=0.0,
                               base=0, channel_multiplier=1).then_inc(consts, 1)
            pool.affine_select(out=upto[:, :], in_=ones[:, :], pattern=[[1, P]], compare_op=ALU.is_ge, fill=0.0,
                               base=0, channel_multiplier=-1).then_inc(consts, 1)

            for layer in range(LAYERS):
                h = h_dram[layer]
                if layer > 0:
                    with pool.Fori(0, BATCHES) as i:
                        for j in range(BATCH):
                            gate(pool, h_normed, (layer - 1) * TILES + i * BATCH + j + 1)
                            pool.tensor_copy(agg[:, :, bass.ds((i * BATCH + j) * P, P)], fm[:, j]).then_inc(agg_set, 1)
                for j in range(BATCH):
                    pool.wait_ge(stored[j], 16 * BATCHES * (layer + 1))
                with pool.Fori(0, LOOPS) as i:
                    for half in range(2):
                        gate(pool, idx_staged, layer * (2 * LOOPS + 1) + 2 * i + half + 1)
                        for k in range(HALF_GROUPS):
                            gate(pool, summed, layer * GROUPS + (2 * i + half) * HALF_GROUPS + k + 1)
                            for c in range(CHUNKS):
                                s = k * CHUNKS + c
                                pool.indirect_dma_start(
                                    rows[:, s, :], None, h,
                                    bass.IndirectOffsetOnAxis(ap=idx_now[:, half, s:s + 1], axis=0),
                                ).then_inc(landed[s], 16)

                pool.wait_ge(tables_ready, 2)
                far = pool.value_load(far_flag[0:1, 0:1], min_val=0, max_val=1)
                with pool.If(far > 0):
                    with pool.Fori(0, GROUPS * CHUNKS) as c:
                        gate(pool, turn, (layer * GROUPS * CHUNKS + c) * SLOW_STEPS + 3)
                        pool.indirect_dma_start(
                            rows[:, 0, :], None, h,
                            bass.IndirectOffsetOnAxis(ap=slow_idx[:, 0:1], axis=0)).then_inc(slow_landed, 16)
                pool.end_ifs()

            with pool.Fori(0, BATCHES) as i:
                for j in range(BATCH):
                    gate(pool, tok_normed, i * BATCH + j + 1)
                    pool.tensor_copy(tokens[:, bass.ds(i * BATCH + j, 1), :], nm[:, j:j + 1, :]).then_inc(tok_kept, 1)

            pool.wait_ge(zero_filled, 16 * EXPERTS)
            pool.wait_ge(routed, 1)
            pool.wait_ge(tok_kept, TILES + BATCH)
            for i in range(TILES):
                pool.indirect_dma_start(
                    dispatch_dram, bass.IndirectOffsetOnAxis(ap=scatter_idx[:, i:i + 1], axis=0), tokens[:, i, :], None,
                    bounds_check=EXPERTS * CAPP - 1, oob_is_err=False).then_inc(scattered, 16)

            pool.wait_ge(scattered, 16 * TILES)
            pool.memset(hmid[:, :, 2 * CAP_N:], 0.0).then_inc(hmid_padded, 1)

            for c in range(CT // 2):
                pool.wait_ge(y_stored[c], 16 * EXPERTS)
            for i in range(TILES):
                if i >= 2 * BATCH and i % BATCH == 0:
                    pool.wait_ge(y_done, i // BATCH - 1)
                pool.indirect_dma_start(
                    y_slot(i), None, answer_dram,
                    bass.IndirectOffsetOnAxis(ap=gather_idx[:, i:i + 1], axis=0)).then_inc(y_back[i % (2 * BATCH)], 16)

        @block.scalar
        def _(act):
            act.dma_start(vec_rows[0:VEC0, :], t["L0_ffn_b1"].rearrange("e (f p) -> (e f) p", p=P)).then_inc(params_in, 16)
            for layer in range(LAYERS):
                n = layer + 1
                for w, name in enumerate((f"b{n}a", f"b{n}b", f"g{n}", f"be{n}")):
                    r = VEC0 + (layer * 4 + w) * HALVES
                    act.dma_start(vec_rows[r:r + HALVES, :],
                                  t["L0_gnn_" + name].rearrange("(k p) -> k p", p=P)).then_inc(params_in, 16)
                for w, name in enumerate((f"W{n}a", f"W{n}b")):
                    act.dma_start(w_gnn[:, layer, w],
                                  t["L0_gnn_" + name].rearrange("(k p) n -> p k n", p=P)).then_inc(params_in, 16)
            act.dma_start(gate_w[:, :, :], t["L0_ffn_gate_w"].rearrange("(k p) e -> p k e", p=P)).then_inc(params_in, 16)
            act.dma_start(gate_b[:, :], t["L0_ffn_gate_b"].partition_broadcast(P)).then_inc(params_in, 16)
            act.dma_start(b2_all[:, :, :], t["L0_ffn_b2"].partition_broadcast(P)).then_inc(params_in, 16)

            act.sem_inc(partial_copied, 2)
            act.sem_inc(hid_ready, 4)
            act.sem_inc(f_ready, 4)

            def layer_norm_batch(i, nth, source, slot_free, done):
                act.wait_ge(ln_var, nth * BATCHES + i + 1)
                nc.scalar.activation(ln_w[:, 6, :], ln_w[:, 5, :], ACT.Sqrt).then_inc(ln_std, 1)
                gate(act, ln_ready, nth * BATCHES + i + 1)
                for j in range(BATCH):
                    slot_free(j)
                    nc.scalar.activation(nm[:, j:j + 1, :], source[:, bass.ds(i * BATCH + j, 1), :], ACT.Identity,
                                         bias=ln_w[:, 8, j:j + 1], scale=ln_w[:, 7, j:j + 1]).then_inc(done, 1)

            layer_norm_batch(0, 0, x_sb, lambda j: None, x_normed)
            with act.Fori(1, BATCHES) as i:
                def slot_free(j):
                    gate(act, stored[j], 16 * i)
                    gate(act, x_turned, (i - 1) * BATCH + j + 1)
                layer_norm_batch(i, 0, x_sb, slot_free, x_normed)

            for layer in range(LAYERS):
                with act.Fori(0, LOOPS) as i:
                    for k in range(2 * HALF_GROUPS):
                        g = layer * GROUPS + i * 2 * HALF_GROUPS + k
                        gate(act, sums_turned, g + 1)
                        act.wait_ge(summed, g + 1 + 4)
                        nc.scalar.copy(partial[:, k % 2, :], bank[k % 2][:, 0:D]).then_inc(partial_copied, 1)

                act.wait_ge(tables_ready, 2)
                far = act.value_load(far_flag[0:1, 0:1], min_val=0, max_val=1)
                with act.If(far > 0):
                    with act.Fori(0, GROUPS * CHUNKS) as c:
                        with act.Fori(0, TILES) as w:
                            act.wait_ge(turn, (c + layer * GROUPS * CHUNKS) * SLOW_STEPS + w * 6 + 5)
                            nc.scalar.copy(partial[:, 0, :], bank[0][:, 0:D]).then_inc(turn, 1)
                    act.wait_ge(turn, (layer + 1) * GROUPS * CHUNKS * SLOW_STEPS + 1)
                act.end_ifs()

                def hidden(b, par, size):
                    for m in range(HALVES):
                        act.wait_ge(out_summed, 2 * b + 2)
                        act.sem_inc(gate_passed, 1)
                        act.wait_ge(hid_summed, 2 * b + m + 1)
                        nc.scalar.activation(hid[:, par, m, 0:size], bank[2 * par + m][:, 0:size], ACT.Relu,
                                             bias=vec(layer, 0, m)).then_inc(hid_ready, 1)

                act.wait_ge(vecs_ready, 1)
                b0 = layer * (BLOCKS + 1)
                with act.Fori(0, BLOCKS // 2) as i:
                    for par in range(2):
                        hidden(b0 + 2 * i + par, par, NODES_B)
                hidden(b0 + BLOCKS, 0, TAIL_B)

                act.wait_ge(bn_var, layer + 1)
                nc.scalar.activation(bn_w[:, 1, :], bn_w[:, 0, :], ACT.Sqrt).then_inc(bn_std, 1)
                act.wait_ge(bn_ready, layer + 1)
                if layer == LAYERS - 1:
                    act.wait_ge(h_turned, layer * TILES + BATCH)
                    act.wait_ge(agg_set, layer * TILES + BATCH)
                    for j in range(BATCH):
                        act.wait_ge(stored[j], 16 * BATCHES * LAYERS)
                with act.Fori(0, BATCHES) as i:
                    for j in range(BATCH):
                        tile = i * BATCH + j
                        if layer < LAYERS - 1:
                            gate(act, h_turned, layer * TILES + tile + 1)
                            gate(act, agg_set, layer * TILES + tile + 1)
                        else:
                            gate(act, tok_scored, tile + 1)
                        for m in range(HALVES):
                            ins = nc.scalar.activation(fm[:, j, m, :], agg[:, m, bass.ds(tile * P, P)],
                                                       ACT.Identity, bias=bn_w[:, 4, m:m + 1], scale=bn_w[:, 3, m:m + 1])
                        ins.then_inc(h_normed, 1)
                    if layer == LAYERS - 1:
                        def slot_free(j):
                            gate(act, tok_turned, i * BATCH + j + 1)
                            gate(act, tok_kept, i * BATCH + j + 1)
                        layer_norm_batch(i, 1, x_sb, slot_free, tok_normed)

            act.wait_ge(exp_in, 1)
            nc.scalar.activation(r_c, r_b, ACT.Exp).then_inc(exp_done, 1)

            act.wait_ge(hmid_padded, 1)
            with act.Fori(0, EXPERTS // 2) as i:
                for s in range(2):
                    e = 2 * i + s
                    gate(act, y_summed, e * CT + CT)
                    for q in range(2 * FC):
                        f, n = q // 2, q % 2
                        gate(act, f_summed, e * 2 * FC + q + 1)
                        nc.scalar.activation(hmid[:, f, n * CAP_N:(n + 1) * CAP_N], bank[q % 4][:, 0:CAP_N], ACT.Relu,
                                             bias=vecs[:, bass.ds(e * FC + f, 1)]).then_inc(f_ready, 1)

            for i in range(TILES):
                act.wait_ge(y_back[i % (2 * BATCH)], 16 * (i // (2 * BATCH) + 1))
                slot = y_slot(i)
                nc.scalar.activation(slot, slot, ACT.Copy, scale=route[:, 13, i:i + 1]).then_inc(y_scaled, 1)

        @block.tensor
        def _(pe):
            pe.sem_inc(summed, 4)
            pe.sem_inc(sums_turned, 2)
            pe.sem_inc(out_summed, 4)
            pe.sem_inc(h_turned, BATCH)
            pe.sem_inc(tok_turned, BATCH)
            pe.sem_inc(tok_scored, BATCH)
            pe.sem_inc(y_summed, CT)

            pe.wait_ge(consts, 10)
            pe.wait_ge(edges_ready, 1)
            for a, src in enumerate((src_f, rel_f, far_f)):
                for q in range(2):
                    for c in range(CHUNKS):
                        ins = pe.transpose(bank[2 * a + q][:, c * GROWS:(c + 1) * GROWS],
                                           src[0:GROWS, q, c * P:(c + 1) * P], ident[0:GROWS, 0:GROWS])
                    ins.then_inc(prep_turned, 1)
            for n, col in enumerate((base[0:GROWS, 0:1], base[0:GROWS, 1:2], any_far[0:GROWS, :])):
                ins = pe.transpose(bank[6][0:1, n * GROWS:(n + 1) * GROWS], col, ident[0:GROWS, 0:GROWS])
            ins.then_inc(prep_turned, 1)
            pe.wait_ge(params_in, 16 * PARAMS)
            pe.transpose(bank[7][:, 0:NVEC], vec_rows[:, :], ident[0:NVEC, 0:NVEC]).then_inc(vecs_turned, 1)
            pe.wait_ge(tables_ready, 2)
            pe.wait_ge(vecs_ready, 1)

            def turn_tile(src, j, done):
                for m in range(HALVES):
                    ins = pe.transpose(bank[j][:, m * P:(m + 1) * P], src(m), ident[:, :])
                ins.then_inc(done, 1)

            with pe.Fori(0, BATCHES) as i:
                for j in range(BATCH):
                    pe.wait_ge(x_in_agg, i * BATCH + j + 1)
                    pe.sem_inc(gate_passed, 1)
                    pe.wait_ge(x_normed, i * BATCH + j + 1)
                    turn_tile(lambda m: nm[:, j, m * P:(m + 1) * P], j, x_turned)
            pe.wait_ge(x_in_agg, TILES + BATCH)

            for layer in range(LAYERS):
                def turn_sums(g, par):
                    pe.wait_ge(partial_copied, g + 1 + 2)
                    pe.sem_inc(gate_passed, 1)
                    pe.wait_ge(added, g + 1)
                    for m in range(HALVES):
                        ins = pe.transpose(bank[2 + par][:, m * P:(m + 1) * P], partial[:, par, m * P:(m + 1) * P], ident[:, :])
                    ins.then_inc(sums_turned, 1)

                with pe.Fori(0, LOOPS) as i:
                    for half in range(2):
                        for k in range(HALF_GROUPS):
                            g = layer * GROUPS + (2 * i + half) * HALF_GROUPS + k
                            pe.wait_ge(onehot_ready, g + 1)
                            pe.sem_inc(gate_passed, 1)
                            pe.wait_ge(partial_copied, g + 1)
                            pe.sem_inc(gate_passed, 1)
                            for c in range(CHUNKS):
                                pe.wait_ge(landed[k * CHUNKS + c], 16 * (layer * 2 * LOOPS + 2 * i + half + 1))
                                ins = pe.matmul(bank[k % 2][:, 0:D], onehot[:, k % 2, c, :], rows[:, k * CHUNKS + c, :],
                                                start=(c == 0), stop=(c == CHUNKS - 1))
                            ins.then_inc(summed, 1)
                            if k > 0:
                                turn_sums(g - 1, (k - 1) % 2)
                        turn_sums(g, k % 2)

                far = pe.value_load(far_flag[0:1, 0:1], min_val=0, max_val=1)
                with pe.If(far > 0):
                    with pe.Fori(0, GROUPS * CHUNKS) as c:
                        step = (c + layer * GROUPS * CHUNKS) * SLOW_STEPS
                        pe.wait_ge(slow_landed, 16 * (c + layer * GROUPS * CHUNKS + 1))
                        pe.sem_inc(gate_passed, 1)
                        with pe.Fori(0, TILES) as w:
                            pe.wait_ge(turn, step + w * 6 + 4)
                            pe.matmul(bank[0][:, 0:D], onehot[:, 0, 0, :], rows[:, 0, :], start=True, stop=True).then_inc(turn, 1)
                            pe.wait_ge(turn, step + w * 6 + 6)
                            for m in range(HALVES):
                                ins = pe.transpose(bank[2][:, m * P:(m + 1) * P], partial[:, 0, m * P:(m + 1) * P], ident[:, :])
                            ins.then_inc(turn, 1)
                    pe.wait_ge(turn, (layer + 1) * GROUPS * CHUNKS * SLOW_STEPS + 1)
                pe.end_ifs()

                pe.wait_ge(added, (layer + 1) * GROUPS + 2)

                def first(b, par, lo, size):
                    for m in range(HALVES):
                        pe.wait_ge(hid_ready, 2 * b + m + 1)
                        for k in range(HALVES):
                            ins = pe.matmul(bank[2 * par + m][:, 0:size], wgt(layer, 0, k, m), agg[:, k, bass.ds(lo, size)],
                                            start=(k == 0), stop=(k == HALVES - 1))
                        ins.then_inc(hid_summed, 1)

                def second(b, par, size):
                    for m in range(HALVES):
                        if m == 0:
                            pe.wait_ge(hid_ready, 2 * b + 2 + 4)
                            pe.sem_inc(gate_passed, 1)
                        pe.wait_ge(out_stored, 2 * b + m + 1)
                        for k in range(HALVES):
                            ins = pe.matmul(bank[4 + 2 * par + m][:, 0:size], wgt(layer, 1, k, m), hid[:, par, k, 0:size],
                                            start=(k == 0), stop=(k == HALVES - 1))
                        ins.then_inc(out_summed, 1)

                b0 = layer * (BLOCKS + 1)
                with pe.Fori(0, BLOCKS // 2) as i:
                    for par in range(2):
                        first(b0 + 2 * i + par, par, (2 * i + par) * NODES_B, NODES_B)
                    for par in range(2):
                        second(b0 + 2 * i + par, par, NODES_B)
                first(b0 + BLOCKS, 0, BLOCKS * NODES_B, TAIL_B)
                second(b0 + BLOCKS, 0, TAIL_B)

                pe.wait_ge(out_stored, 2 * (b0 + BLOCKS + 1) + 4)
                with pe.Fori(0, BATCHES) as i:
                    for j in range(BATCH):
                        tile = i * BATCH + j
                        if layer == LAYERS - 1:
                            pe.wait_ge(tok_copied, tile + 1)
                        else:
                            pe.wait_ge(h_read, layer * TILES + tile + 1)
                        pe.sem_inc(gate_passed, 1)
                        pe.wait_ge(h_normed, layer * TILES + tile + 1)
                        turn_tile(lambda m: fm[:, j, m, :], j, h_turned)
                    if layer == LAYERS - 1:
                        for j in range(BATCH):
                            tile = i * BATCH + j
                            pe.wait_ge(h_read, layer * TILES + tile + 1 + BATCH)
                            pe.sem_inc(gate_passed, 1)
                            pe.wait_ge(tok_normed, tile + 1)
                            turn_tile(lambda m: nm[:, j, m * P:(m + 1) * P], j, tok_turned)
                        for j in range(BATCH):
                            tile = i * BATCH + j
                            pe.wait_ge(tok_copied, tile + 1 + BATCH)
                            for m in range(HALVES):
                                ins = pe.matmul(bank[7][:, bass.ds(tile * EXPERTS, EXPERTS)], fm[:, j, m, :], gate_w[:, m, :],
                                                start=(m == 0), stop=(m == HALVES - 1))
                            ins.then_inc(tok_scored, 1)
                if layer < LAYERS - 1:
                    pe.wait_ge(h_read, (layer + 1) * TILES + BATCH)

            pe.wait_ge(chosen, 1)
            pe.matmul(bank[0][:, 0:TE], upto[:, :], r_e, start=True, stop=True).then_inc(counted, 1)
            pe.matmul(bank[1][:, 0:TE], ones[:, :], r_e, start=True, stop=True).then_inc(counted, 1)
            pe.wait_ge(routed, 1)

            with pe.Fori(0, EXPERTS // 2) as i:
                for s in range(2):
                    e = 2 * i + s
                    w1 = w_exp[:, s, 0:FC * D].rearrange("p (k n) -> p k n", k=HALVES)
                    w2 = w_exp[:, s, FC * D:2 * FC * D].rearrange("p (f n) -> p f n", f=FC)
                    pe.wait_ge(buf_in[s], 16 * (i + 1))
                    pe.sem_inc(gate_passed, 1)
                    for c in range(CT):
                        pe.wait_ge(bufT_copied, e * CT + c + 1)
                        for k in range(HALVES):
                            ins = pe.transpose(bank[6 + c % 2][:, k * P:(k + 1) * P], buf[:, s, c, k * P:(k + 1) * P], ident[:, :])
                        ins.then_inc(bufT_turned, 1)
                    pe.wait_ge(w_in[s], 32 * (i + 1))
                    pe.sem_inc(gate_passed, 1)
                    pe.wait_ge(bufT_copied, (e + 1) * CT + 2)
                    pe.sem_inc(gate_passed, 1)
                    for q in range(2 * FC):
                        f, n = q // 2, q % 2
                        pe.wait_ge(f_ready, e * 2 * FC + q + 1)
                        for k in range(HALVES):
                            ins = pe.matmul(bank[q % 4][:, 0:CAP_N], w1[:, k, f * P:(f + 1) * P],
                                            bufT[:, k, n * CAP_N:(n + 1) * CAP_N], start=(k == 0), stop=(k == HALVES - 1))
                        ins.then_inc(f_summed, 1)
                    pe.wait_ge(f_ready, (e + 1) * 2 * FC + 4)
                    pe.sem_inc(gate_passed, 1)
                    for c in range(CT):
                        pe.wait_ge(y_added, e * CT + c + 1)
                        for f in range(FC):
                            ins = pe.matmul(bank[4 + c % 2][:, 0:D], hmid[:, f, c * P:(c + 1) * P], w2[:, f, :],
                                            start=(f == 0), stop=(f == FC - 1))
                        ins.then_inc(y_summed, 1)

        @block.vector
        def _(dve):
            steps = 0

            def link(ins):
                nonlocal steps
                steps += 1
                ins.then_inc(prep, 1)
                dve.wait_ge(prep, steps)

            dve.sem_inc(added, 2)
            dve.sem_inc(out_stored, 4)
            dve.sem_inc(x_in_agg, BATCH)
            dve.sem_inc(h_read, BATCH)
            dve.sem_inc(tok_copied, BATCH)
            dve.sem_inc(bufT_copied, 2)
            dve.sem_inc(y_added, 2)

            G = slice(0, GROWS)
            dve.wait_ge(edges_in, 16 * 6)
            dve.tensor_copy(src_f[G], src_i[G])
            link(dve.tensor_copy(dst_f[G], dst_i[G]))
            link(dve.tensor_scalar(key_f[G], dst_f[G], 0.0, 65536.0, ALU.is_lt, ALU.mult))
            link(dve.tensor_tensor(key_f[G], key_f[G], dst_f[G], ALU.add))
            link(dve.tensor_reduce(base[G, :], key_f[G], AX.X, ALU.min))
            for q in range(2):
                link(dve.tensor_scalar(rel_f[G, q], dst_f[G, q], base[G, q:q + 1], None, ALU.subtract))
            link(dve.tensor_scalar(key_f[G], rel_f[G], float(P), None, ALU.is_ge))
            link(dve.tensor_reduce(any_far[G, :], key_f[G], AX.XY, ALU.max))
            link(dve.scalar_tensor_tensor(out=far_f[G], in0=dst_f[G], scalar=1.0, in1=key_f[G], op0=ALU.add, op1=ALU.mult))
            dve.tensor_scalar(far_f[G], far_f[G], 1.0, None, ALU.subtract).then_inc(edges_ready, 1)
            dve.wait_ge(edges_ready, 1)
            dve.wait_ge(consts, 10)
            link(dve.tensor_copy(iota[:, :], iota_i[:, :]))
            for a, cols in enumerate((idx_cols, rel_cols, far_cols)):
                for q in range(2):
                    dve.wait_ge(prep_turned, 2 * a + q + 1)
                    to = cols[:, 0:GROUPS * CHUNKS].rearrange("p (g c) -> p c g", c=CHUNKS)[:, :, q * GROWS:(q + 1) * GROWS]
                    link(dve.tensor_copy(to, bank[2 * a + q][:, 0:CHUNKS * GROWS].rearrange("p (c g) -> p c g", c=CHUNKS)))
            dve.wait_ge(prep_turned, 7)
            dve.tensor_copy(base_row[:, :], bank[6][0:1, 0:GROUPS]).then_inc(tables_ready, 1)
            link(dve.tensor_reduce(far_flag_f[:, :], bank[6][0:1, GROUPS:GROUPS + GROWS], AX.X, ALU.max))
            dve.tensor_copy(far_flag[:, :], far_flag_f[:, :]).then_inc(tables_ready, 1)
            dve.wait_ge(vecs_turned, 1)
            dve.tensor_copy(vecs[:, :], bank[7][:, 0:NVEC]).then_inc(vecs_ready, 1)
            dve.wait_ge(tables_ready, 2)

            LN_STEPS = BATCH + 6

            def ln_stats(nb, j, tile):
                dve.bn_stats(ln_st[:, j, :], tile).then_inc(ln_steps, 1)

            def ln_finish(nb):
                s0 = nb * LN_STEPS
                col = lambda c: ln_st[:, :, c]
                w = lambda r: ln_w[:, r, :]
                gate(dve, ln_steps, s0 + BATCH)
                dve.tensor_tensor(w(0), col(1), col(4), ALU.add).then_inc(ln_steps, 1)
                dve.tensor_tensor(w(1), col(1), col(4), ALU.subtract).then_inc(ln_steps, 1)
                dve.tensor_tensor(w(2), col(2), col(5), ALU.add).then_inc(ln_steps, 1)
                gate(dve, ln_steps, s0 + BATCH + 3)
                dve.tensor_tensor(w(3), w(1), w(1), ALU.mult).then_inc(ln_steps, 1)
                dve.tensor_scalar(w(4), w(2), 1.0 / D, EPS, ALU.mult, ALU.add).then_inc(ln_steps, 1)
                gate(dve, ln_steps, s0 + BATCH + 5)
                dve.scalar_tensor_tensor(out=w(5), in0=w(3), scalar=0.25, in1=w(4), op0=ALU.mult, op1=ALU.add).then_inc(ln_var, 1)
                gate(dve, ln_std, nb + 1)
                dve.reciprocal(w(7), w(6)).then_inc(ln_steps, 1)
                gate(dve, ln_steps, s0 + BATCH + 6)
                dve.scalar_tensor_tensor(out=w(8), in0=w(0), scalar=-0.5, in1=w(7), op0=ALU.mult, op1=ALU.mult).then_inc(ln_ready, 1)

            dve.wait_ge(x_in, 16 * (BATCHES + 1))
            with dve.Fori(0, BATCHES) as i:
                for j in range(BATCH):
                    ln_stats(i, j, x_sb[:, bass.ds(i * BATCH + j, 1), :].rearrange("p a d -> p (a d)"))
                ln_finish(i)
                for j in range(BATCH):
                    gate(dve, x_turned, i * BATCH + j + 1)
                    dve.tensor_copy(agg[:, :, bass.ds((i * BATCH + j) * P, P)],
                                    bank[j][:, 0:D].rearrange("p (m n) -> p m n", m=HALVES)).then_inc(x_in_agg, 1)
            dve.wait_ge(x_in_agg, TILES + BATCH)

            for layer in range(LAYERS):
                if layer > 0:
                    dve.wait_ge(agg_set, layer * TILES + BATCH)
                dve.tensor_copy(idx_now[:, 0, :], idx_cols[:, 0:SLOTS]).then_inc(idx_staged, 1)

                def one_hots(g, gl, par):
                    dve.wait_ge(summed, g - 2 + 1 + 4)
                    dve.tensor_tensor(onehot[:, par], iota[:, :].unsqueeze(1).to_broadcast([P, CHUNKS, P]),
                                      rel_cols[:, bass.ds(gl * CHUNKS, CHUNKS)].unsqueeze(2).to_broadcast([P, CHUNKS, P]),
                                      ALU.is_equal).then_inc(onehot_ready, 1)

                def add_sums(g, gl, par):
                    first = dve.value_load(base_row[0:1, bass.ds(gl, 1)], min_val=0, max_val=N - 1)
                    window = agg[:, :, bass.ds(first, P)]
                    gate(dve, added, g + 2)
                    dve.wait_ge(sums_turned, g + 1 + 2)
                    dve.tensor_tensor(window, window, bank[2 + par][:, 0:D].rearrange("p (m n) -> p m n", m=HALVES),
                                      ALU.add).then_inc(added, 1)

                with dve.Fori(0, LOOPS) as i:
                    for half in range(2):
                        dve.tensor_copy(idx_now[:, 1 - half, :],
                                        idx_cols[:, bass.ds((2 * i + half + 1) * SLOTS, SLOTS)]).then_inc(idx_staged, 1)
                        for k in range(HALF_GROUPS):
                            gl = (2 * i + half) * HALF_GROUPS + k
                            one_hots(layer * GROUPS + gl, gl, k % 2)
                            if k > 0:
                                add_sums(layer * GROUPS + gl - 1, gl - 1, (k - 1) % 2)
                        add_sums(layer * GROUPS + gl, gl, k % 2)

                far = dve.value_load(far_flag[0:1, 0:1], min_val=0, max_val=1)
                dve.wait_ge(added, (layer + 1) * GROUPS + 2)
                with dve.If(far > 0):
                    if layer == 0:
                        dve.sem_inc(turn, 1)
                    with dve.Fori(0, GROUPS * CHUNKS) as c:
                        step = (c + layer * GROUPS * CHUNKS) * SLOW_STEPS
                        gate(dve, turn, step + 1)
                        dve.tensor_copy(slow_idx[:, :], idx_cols[:, bass.ds(c, 1)]).then_inc(turn, 1)
                        dve.tensor_copy(slow_rel[:, :], far_cols[:, bass.ds(c, 1)]).then_inc(turn, 1)
                        with dve.Fori(0, TILES) as w:
                            dve.wait_ge(turn, step + w * 6 + 3)
                            dve.tensor_scalar(onehot[:, 0, 0, :], iota[:, :], slow_rel[:, 0:1], None, ALU.is_equal).then_inc(turn, 1)
                            block_cols = agg[:, :, bass.ds(w * P, P)]
                            dve.wait_ge(turn, step + w * 6 + 7)
                            dve.tensor_tensor(block_cols, block_cols, bank[2][:, 0:D].rearrange("p (m n) -> p m n", m=HALVES),
                                              ALU.add).then_inc(turn, 1)
                            dve.wait_ge(turn, step + w * 6 + 8)
                            dve.tensor_scalar(slow_rel[:, :], slow_rel[:, :], float(P), None, ALU.subtract).then_inc(turn, 1)
                    dve.wait_ge(turn, (layer + 1) * GROUPS * CHUNKS * SLOW_STEPS + 1)
                dve.end_ifs()

                def output(b, par, lo, blk, size):
                    for m in range(HALVES):
                        dve.wait_ge(out_summed, 2 * b + m + 1 + 4)
                        dve.tensor_scalar(agg[:, m, bass.ds(lo, size)], bank[4 + 2 * par + m][:, 0:size], vec(layer, 1, m), 0.0,
                                          ALU.add, ALU.max).then_inc(out_stored, 1)
                    for m in range(HALVES):
                        gate(dve, out_stored, 2 * b + m + 1 + 4)
                        dve.bn_stats(bn_st[:, m, bass.ds(blk, 1), :].rearrange("p a s -> p (a s)"),
                                     agg[:, m, bass.ds(lo, size)]).then_inc(bn_seen, 1)

                b0 = layer * (BLOCKS + 1)
                with dve.Fori(0, BLOCKS // 2) as i:
                    for par in range(2):
                        output(b0 + 2 * i + par, par, (2 * i + par) * NODES_B, 2 * i + par, NODES_B)
                output(b0 + BLOCKS, 0, BLOCKS * NODES_B, BLOCKS, TAIL_B)

                dve.wait_ge(bn_seen, 2 * (b0 + BLOCKS + 1))
                for m in range(HALVES):
                    link(dve.bn_aggr(bn_mv[:, m, :], bn_st[:, m, :, :].rearrange("p b s -> p (b s)")))
                c = VEC0 + (layer * 4 + 2) * HALVES
                gamma, beta = vecs[:, c:c + HALVES], vecs[:, c + HALVES:c + 2 * HALVES]
                dve.tensor_scalar(bn_w[:, 0, :], bn_mv[:, :, 1], EPS, None, ALU.add).then_inc(bn_var, 1)
                dve.wait_ge(bn_std, layer + 1)
                link(dve.reciprocal(bn_w[:, 2, :], bn_w[:, 1, :]))
                link(dve.tensor_tensor(bn_w[:, 3, :], bn_w[:, 2, :], gamma, ALU.mult))
                link(dve.tensor_tensor(bn_w[:, 5, :], bn_mv[:, :, 0], bn_w[:, 3, :], ALU.mult))
                dve.tensor_tensor(bn_w[:, 4, :], beta, bn_w[:, 5, :], ALU.subtract).then_inc(bn_ready, 1)

                if layer < LAYERS - 1:
                    with dve.Fori(0, BATCHES) as i:
                        for j in range(BATCH):
                            gate(dve, stored[j], 16 * (BATCHES * (layer + 1) + i))
                            dve.wait_ge(h_turned, layer * TILES + i * BATCH + j + 1 + BATCH)
                            dve.tensor_copy(nm[:, j, :], bank[j][:, 0:D]).then_inc(h_read, 1)
                    continue

                with dve.Fori(0, BATCHES) as i:
                    nb = BATCHES + i
                    for j in range(BATCH):
                        tile = i * BATCH + j
                        x_tile = x_sb[:, bass.ds(tile, 1), :].rearrange("p a d -> p (a d)")
                        dve.wait_ge(h_turned, layer * TILES + tile + 1 + BATCH)
                        dve.tensor_tensor(x_tile, x_tile, bank[j][:, 0:D], ALU.add).then_inc(h_read, 1)
                    for j in range(BATCH):
                        tile = i * BATCH + j
                        gate(dve, h_read, layer * TILES + tile + 1 + BATCH)
                        ln_stats(nb, j, x_sb[:, bass.ds(tile, 1), :].rearrange("p a d -> p (a d)"))
                    ln_finish(nb)
                    for j in range(BATCH):
                        tile = i * BATCH + j
                        dve.wait_ge(tok_turned, tile + 1 + BATCH)
                        dve.tensor_copy(fm[:, j].rearrange("p m n -> p (m n)"), bank[j][:, 0:D]).then_inc(tok_copied, 1)

            def by_tile(flat):
                return flat.rearrange("p (t e) -> p t e", e=EXPERTS)

            def wide(row):
                return route[:, row, :].unsqueeze(2).to_broadcast([P, TILES, EXPERTS])

            def row(r):
                return route[:, r, :]

            SHIFTED_MAX, SUM, INV, PROB, CHOICE_8, CHOICE, REAL, PLACE, KEPT, SENT, ROW_S, ROW_T, ROW_G, WEIGHT = range(14)
            dve.wait_ge(tok_scored, TILES + BATCH)
            dve.wait_ge(tok_kept, TILES + BATCH)
            link(dve.tensor_tensor(by_tile(r_a), by_tile(bank[7][:, 0:TE]),
                                   gate_b[:, :].unsqueeze(1).to_broadcast([P, TILES, EXPERTS]), ALU.add))
            link(dve.tensor_reduce(row(SHIFTED_MAX), by_tile(r_a), AX.X, ALU.max))
            dve.tensor_tensor(by_tile(r_b), by_tile(r_a), wide(SHIFTED_MAX), ALU.subtract).then_inc(exp_in, 1)
            dve.wait_ge(exp_done, 1)
            link(dve.tensor_reduce(row(SUM), by_tile(r_c), AX.X, ALU.add))
            link(dve.reciprocal(row(INV), row(SUM)))
            link(dve.tensor_tensor(by_tile(r_a), by_tile(r_c), wide(INV), ALU.mult))
            link(dve.tensor_reduce(row(PROB), by_tile(r_a), AX.X, ALU.max))
            link(dve.tensor_tensor(by_tile(r_b), by_tile(r_a), wide(PROB), ALU.is_equal))
            link(dve.tensor_copy(r_g, exp_i[:, :]))
            link(dve.scalar_tensor_tensor(out=r_d, in0=r_b, scalar=-float(EXPERTS), in1=r_g, op0=ALU.mult, op1=ALU.add))
            link(dve.tensor_reduce(row(CHOICE_8), by_tile(r_d), AX.X, ALU.min))
            link(dve.tensor_scalar(row(CHOICE), row(CHOICE_8), float(EXPERTS), None, ALU.add))
            link(dve.tensor_copy(row(ROW_S), tok_i[:, :]))
            link(dve.tensor_scalar(row(REAL), row(ROW_S), float(N), None, ALU.is_lt))
            link(dve.tensor_tensor(by_tile(r_d), by_tile(r_g), wide(CHOICE), ALU.is_equal))
            dve.tensor_tensor(by_tile(r_e), by_tile(r_d), wide(REAL), ALU.mult).then_inc(chosen, 1)
            dve.wait_ge(counted, 2)
            link(dve.tensor_copy(r_f, bank[1][:, 0:TE]))
            for e in range(EXPERTS):
                link(dve.tensor_tensor_scan(r_a[:, e:TE:EXPERTS], ones[:, 0:TILES], r_f[:, e:TE:EXPERTS], 0.0, ALU.mult, ALU.add))
            link(dve.tensor_tensor(r_a, r_a, r_f, ALU.subtract))
            link(dve.tensor_tensor(r_a, r_a, bank[0][:, 0:TE], ALU.add))
            link(dve.tensor_tensor(r_a, r_a, r_e, ALU.mult))
            link(dve.tensor_reduce(row(PLACE), by_tile(r_a), AX.X, ALU.add))
            link(dve.tensor_scalar(row(KEPT), row(PLACE), float(CAP), None, ALU.is_le))
            link(dve.tensor_tensor(row(SENT), row(KEPT), row(REAL), ALU.mult))
            link(dve.scalar_tensor_tensor(out=row(ROW_S), in0=row(CHOICE), scalar=float(CAPP), in1=row(PLACE), op0=ALU.mult, op1=ALU.add))
            link(dve.scalar_tensor_tensor(out=row(ROW_T), in0=row(ROW_S), scalar=-float(NO_SLOT + 1), in1=row(SENT), op0=ALU.add, op1=ALU.mult))
            link(dve.tensor_scalar(scatter_idx[:, :], row(ROW_T), float(NO_SLOT), None, ALU.add))
            link(dve.tensor_scalar(row(ROW_G), row(PLACE), float(CAP), 1.0, ALU.min, ALU.max))
            link(dve.scalar_tensor_tensor(out=row(ROW_S), in0=row(CHOICE), scalar=float(CAPP), in1=row(ROW_G), op0=ALU.mult, op1=ALU.add))
            link(dve.tensor_scalar(gather_idx[:, :], row(ROW_S), 1.0, None, ALU.subtract))
            dve.tensor_tensor(row(WEIGHT), row(PROB), row(KEPT), ALU.mult).then_inc(routed, 1)

            def expert(e, s, first):
                for c in range(CT):
                    gate(dve, bufT_turned, e * CT + c + 1)
                    dve.tensor_copy(bufT[:, :, c * P:(c + 1) * P],
                                    bank[6 + c % 2][:, 0:D].rearrange("p (k n) -> p k n", k=HALVES)).then_inc(bufT_copied, 1)
                for c in range(CT):
                    if not first and c % 2 == 0:
                        gate(dve, y_stored[c // 2], 16 * e)
                    dve.wait_ge(y_summed, e * CT + c + 1 + CT)
                    dve.tensor_tensor(y_out[:, c:c + 1, :], bank[4 + c % 2][:, 0:D].unsqueeze(1), b2_all[:, bass.ds(e, 1), :],
                                      ALU.add).then_inc(y_added, 1)

            expert(0, 0, True)
            expert(1, 1, False)
            with dve.Fori(1, EXPERTS // 2) as i:
                for s in range(2):
                    expert(2 * i + s, s, False)

            W7 = BATCH * D
            safe, finite = arena[:, 0:W7], arena[:, W7:2 * W7].bitcast(I32)
            for i in range(BATCHES):
                y7 = nm_flat if i % 2 else fm_flat
                dve.wait_ge(y_scaled, (i + 1) * BATCH)
                dve.tensor_scalar(finite, y7, 0.0, 0.0, ALU.mult, ALU.is_equal)
                link(dve.tensor_scalar(safe, y7, 1e4, -1e4, ALU.min, ALU.max))
                link(dve.scalar_tensor_tensor(out=safe, in0=y7, scalar=NEG_INF, in1=safe, op0=ALU.is_ge, op1=ALU.mult))
                link(dve.copy_predicated(safe, finite, y7))
                x7 = x_sb[:, i * BATCH:(i + 1) * BATCH, :].rearrange("p a d -> p (a d)")
                dve.tensor_tensor(x7, x7, safe, ALU.add).then_inc(y_done, 1)
                dve.wait_ge(y_done, i + 1)


_INS = ["x", "src", "dst"] + [f"L0_gnn_{n}" for l in (1, 2, 3) for n in
                              (f"W{l}a", f"b{l}a", f"W{l}b", f"b{l}b", f"g{l}", f"be{l}")] + \
       [f"L0_ffn_{n}" for n in ("gate_w", "gate_b", "w1", "b1", "w2", "b2")]


def kernel(**inputs):
    import numpy as _np
    import concourse.bacc as _bacc
    from concourse import mybir as _mybir
    from concourse.bass_utils import run_bass_kernel_spmd as _run

    nc = _bacc.Bacc("TRN2", target_bir_lowering=False, num_devices=1)
    arrays, args = {}, {}
    for name in _INS:
        a = _np.ascontiguousarray(inputs[name])
        arrays[f"in_{name}_dram"] = a
        args[name] = nc.dram_tensor(f"in_{name}_dram", a.shape, _mybir.dt.from_np(a.dtype), kind="ExternalInput").ap()
    out = nc.dram_tensor("out_dram", (N, D), _mybir.dt.float32, kind="ExternalOutput").ap()
    gnn_moe_program(nc, args, out)
    r = _run(nc, [arrays], core_ids=[0])
    return r.results[0]["out_dram"]
```

```python
from contextlib import ExitStack

import numpy as np

import concourse.bass as bass
from concourse import mybir

F32 = mybir.dt.float32
I32 = mybir.dt.int32
ALU = mybir.AluOpType
ACT = mybir.ActivationFunctionType
AX = mybir.AxisListType

P = 128
N = 6250
D = 256
HALVES = D // P
E_GNN = 106250
LAYERS = 3
EPS = 1e-5

TILES = -(-N // P)
NPAD = TILES * P
TAIL = N - (TILES - 1) * P
BATCH = 7
BATCHES = TILES // BATCH

CHUNKS = 4
GE = CHUNKS * P
GROUPS = -(-E_GNN // GE)
HALF_GROUPS = 4
SLOTS = HALF_GROUPS * CHUNKS
LOOPS = GROUPS // (2 * HALF_GROUPS)
HID_AT, OUT_AT, TURN_AT, KEEP_AT, ROWS_AT = 1, 3, 5, 4, 6
GROWS = GROUPS // 2
LAST_E = E_GNN - (GROUPS - 1) * GE

NODES_B = 2 * P
LAG = 3
FRONT = LAG * NODES_B
BLOCKS = LOOPS + 2
COLS = FRONT + NPAD + P

EXPERTS = 8
FF = 1024
FC = FF // P
CAP = -(-5 * N // (4 * EXPERTS))
CAPP = 1024
CT = CAPP // P
CAP_N = (CAP + 1) // 2
NO_SLOT = EXPERTS * CAPP
NEG_INF = float("-inf")

SLOW_STEPS = 2 + TILES * 6

assert TILES % BATCH == 0 and GROUPS % (2 * HALF_GROUPS) == 0
assert FRONT + N == (BLOCKS - 1) * NODES_B + TAIL
assert 0 < LAST_E < GE and 2 * CAP_N <= CAPP and CAP <= CAPP and GROWS <= P


def gnn_moe_program(nc, t, out):
    with ExitStack() as ctx:
        def sb(name, shape, dt=F32):
            return ctx.enter_context(nc.sbuf_tensor(name, shape, dt))

        def sem(name):
            return ctx.enter_context(nc.semaphore(name))

        h_dram = [nc.dram_tensor(f"h_dram{i}", (FRONT + NPAD, D), F32, kind="Internal").ap() for i in range(LAYERS)]
        dispatch_dram = nc.dram_tensor("dispatch_dram", (EXPERTS * CAPP, D), F32, kind="Internal").ap()
        answer_dram = nc.dram_tensor("answer_dram", (EXPERTS * CAPP, D), F32, kind="Internal").ap()

        agg = sb("agg", [P, HALVES, COLS])
        x_sb = sb("x_sb", [P, TILES, D])
        arena = sb("arena", [P, TILES * D])
        tokens = arena[:, :].rearrange("p (t d) -> p t d", d=D)

        at = 0

        def carve(words):
            nonlocal at
            at += words
            assert at <= TILES * D
            return arena[:, at - words:at]

        rows = carve(SLOTS * (D + 1)).rearrange("p (s d) -> p s d", d=D + 1)
        onehot = carve(2 * GE).rearrange("p (b c n) -> p b c n", b=2, c=CHUNKS)
        prep0 = at

        def carve_prep(dt=F32):
            return carve(2 * GE).bitcast(dt).rearrange("p (q e) -> p q e", q=2)

        src_i, dst_i = carve_prep(I32), carve_prep(I32)
        src_f, dst_f, key_f, rel_f = (carve_prep() for _ in range(4))
        deg_row = arena[0:1, prep0:prep0 + COLS]

        idx_cols = sb("idx_cols", [P, GROUPS * CHUNKS + SLOTS], I32)
        rel_cols = sb("rel_cols", [P, (GROUPS + 1) * CHUNKS])
        dst_cols = sb("dst_cols", [P, GROUPS * CHUNKS])
        idx_now = sb("idx_now", [P, 2, SLOTS], I32)
        base = sb("base", [P, 2])
        any_far = sb("any_far", [P, 1])
        base_row = sb("base_row", [1, GROUPS], I32)
        least_i = sb("least_i", [1, GROUPS], I32)
        late_row = sb("late_row", [1, 3, GROUPS])
        general_f = sb("general_f", [1, 3])
        general_flag = sb("general_flag", [1, 1], I32)
        c_row = sb("c_row", [1, D])
        slow_idx = sb("slow_idx", [P, 1], I32)
        slow_rel = sb("slow_rel", [P, 1])

        ident = sb("ident", [P, P])
        ones = sb("ones", [P, P])
        upto = sb("upto", [P, P])
        zeros = sb("zeros", [P, D])
        iota_i = agg[:, 0, FRONT:FRONT + P].bitcast(I32)
        iota = sb("iota", [P, P])
        eps_col = sb("eps_col", [P, 1])

        w_gnn = sb("w_gnn", [P, LAYERS, 2, HALVES, D])
        gate_w = sb("gate_w", [P, HALVES, EXPERTS])
        gate_b = sb("gate_b", [P, EXPERTS])
        VEC0 = EXPERTS * FC
        PARAMS = 1 + LAYERS * 6 + 2
        CONSTS = 13
        NVEC = VEC0 + LAYERS * 4 * HALVES
        vec_rows = arena[0:NVEC, TILES * D - P:]
        assert prep0 + COLS <= TILES * D - P and at <= TILES * D - P
        vecs = sb("vecs", [P, NVEC])

        partial = sb("partial", [P, 2, D + 1])
        nm = sb("nm", [P, BATCH, D])
        fm = sb("fm", [P, BATCH, HALVES, P])
        hid = fm[:, 0:2].rearrange("p a m b -> p (a m b)").rearrange("p (m n) -> p m n", m=HALVES)
        u_stage = fm[:, 2:4].rearrange("p a m b -> p (a m b)").rearrange("p (m n) -> p m n", m=HALVES)
        bn_st = sb("bn_st", [P, HALVES, BLOCKS, 6])
        bn_mv = sb("bn_mv", [P, HALVES, 2])
        bn_w = sb("bn_w", [P, 6, HALVES])
        ln_st = sb("ln_st", [P, BATCH, 6])
        ln_w = sb("ln_w", [P, 10, BATCH])

        TE = TILES * EXPERTS
        tok_i = sb("tok_i", [P, TILES], I32)
        exp_i = sb("exp_i", [P, TE], I32)
        route = sb("route", [P, 14, TILES])
        scatter_idx = sb("scatter_idx", [P, TILES], I32)
        gather_idx = sb("gather_idx", [P, TILES], I32)

        agg_flat = agg[:, :, :].rearrange("p m n -> p (m n)")
        WX = 2 * FC * D
        WS = WX + D
        w_exp = agg_flat[:, 0:2 * WS].rearrange("p (s w) -> p s w", s=2)
        bufT = agg_flat[:, 2 * WS:2 * WS + HALVES * CAPP].rearrange("p (k n) -> p k n", k=HALVES)
        y_out = agg_flat[:, 2 * WS + 2 * CAPP:2 * WS + 2 * CAPP + CT * D].rearrange("p (c d) -> p c d", c=CT)
        hmid = arena[:, 0:FC * CAPP].rearrange("p (f n) -> p f n", f=FC)
        buf = arena[:, FC * CAPP:FC * CAPP + 2 * CT * D].rearrange("p (s c d) -> p s c d", s=2, c=CT)

        nm_flat = nm[:, :, :].rearrange("p a b -> p (a b)")
        fm_flat = fm[:, :, :, :].rearrange("p a m b -> p (a m b)")
        r_exp, r_a, r_b, r_c = (nm_flat[:, i * TE:(i + 1) * TE] for i in range(4))
        r_d, r_e, r_f, r_g = (fm_flat[:, i * TE:(i + 1) * TE] for i in range(4))

        bank = [ctx.enter_context(nc.psum_tensor(f"bank{i}", [P, 512], F32)) for i in range(8)]

        cleared = sem("cleared")
        consts = sem("consts")
        edges_in = sem("edges_in")
        x_in = sem("x_in")
        params_in = sem("params_in")
        prep = sem("prep")
        edges_ready = sem("edges_ready")
        prep_turned = sem("prep_turned")
        vecs_turned = sem("vecs_turned")
        vecs_ready = sem("vecs_ready")
        tables_ready = sem("tables_ready")
        gate_passed = sem("gate_passed")
        ln_steps = sem("ln_steps")
        ln_var = sem("ln_var")
        ln_std = sem("ln_std")
        ln_ready = sem("ln_ready")
        x_normed, x_turned, x_in_agg = sem("x_normed"), sem("x_turned"), sem("x_in_agg")
        stored = [sem(f"stored{i}") for i in range(BATCH)]
        h_normed, h_turned, h_read = sem("h_normed"), sem("h_turned"), sem("h_read")
        idx_staged = sem("idx_staged")
        landed = [sem(f"landed{i}") for i in range(SLOTS)]
        onehot_ready = sem("onehot_ready")
        summed = sem("summed")
        partial_copied = sem("partial_copied")
        sums_turned = sem("sums_turned")
        added = sem("added")
        turn = sem("turn")
        slow_landed = sem("slow_landed")
        hid_summed = sem("hid_summed")
        hid_ready = sem("hid_ready")
        out_summed = sem("out_summed")
        u_ready = sem("u_ready")
        u_kept = sem("u_kept")
        u_turned = sem("u_turned")
        u_read = sem("u_read")
        bn_var = sem("bn_var")
        bn_std = sem("bn_std")
        bn_ready = sem("bn_ready")
        c_summed = sem("c_summed")
        wa_scaled = sem("wa_scaled")
        tok_normed, tok_turned, tok_copied = sem("tok_normed"), sem("tok_turned"), sem("tok_copied")
        tok_kept, tok_scored = sem("tok_kept"), sem("tok_scored")
        exp_in = sem("exp_in")
        exp_done = sem("exp_done")
        chosen = sem("chosen")
        counted = sem("counted")
        routed = sem("routed")
        front_filled = sem("front_filled")
        zero_filled = sem("zero_filled")
        scattered = sem("scattered")
        w_in = [sem(f"w_in{i}") for i in range(2)]
        buf_in = [sem(f"buf_in{i}") for i in range(2)]
        bufT_turned = sem("bufT_turned")
        bufT_copied = sem("bufT_copied")
        f_summed = sem("f_summed")
        f_ready = sem("f_ready")
        y_summed = sem("y_summed")
        y_added = sem("y_added")
        y_stored = [sem(f"y_stored{i}") for i in range(CT // 2)]
        y_back = [sem(f"y_back{i}") for i in range(2 * BATCH)]
        hmid_padded = sem("hmid_padded")
        y_scaled = sem("y_scaled")
        y_done = sem("y_done")
        out_done = sem("out_done")

        def gate(eng, semaphore, value):
            eng.wait_ge(semaphore, value)
            eng.sem_inc(gate_passed, 1)

        def y_slot(i):
            return nm[:, i % BATCH, :] if i // BATCH % 2 else fm[:, i % BATCH].rearrange("p m n -> p (m n)")

        def wgt(layer, which, k, m):
            return w_gnn[:, layer, which, k, m * P:(m + 1) * P]

        def vec(layer, which, m):
            c = VEC0 + (layer * 4 + which) * HALVES + m
            return vecs[:, c:c + 1]

        block = ctx.enter_context(nc.Block())

        @block.sync
        def _(sp):
            sp.wait_ge(cleared, 2)
            for flat, dst in ((t["dst"], dst_i), (t["src"], src_i)):
                sp.dma_start(dst[0:GROWS, 0, :],
                             flat[0:GROWS * GE].rearrange("(p e) -> p e", e=GE)).then_inc(edges_in, 16)
                sp.dma_start(dst[0:GROWS - 1, 1, :],
                             flat[GROWS * GE:(GROUPS - 1) * GE].rearrange("(p e) -> p e", e=GE)).then_inc(edges_in, 16)
                sp.dma_start(dst[GROWS - 1:GROWS, 1, 0:LAST_E],
                             flat[(GROUPS - 1) * GE:E_GNN].rearrange("(p e) -> p e", p=1)).then_inc(edges_in, 16)
            sp.wait_ge(cleared, 3)
            for i in range(BATCHES):
                lo, hi = i * BATCH, (i + 1) * BATCH if i < BATCHES - 1 else TILES - 1
                sp.dma_start(x_sb[:, lo:hi, :],
                             t["x"][lo * P:hi * P, :].rearrange("(t p) d -> p t d", p=P)).then_inc(x_in, 16)
            sp.dma_start(x_sb[0:TAIL, TILES - 1, :], t["x"][(TILES - 1) * P:N, :]).then_inc(x_in, 16)

            sp.wait_ge(consts, 1)
            sp.dma_start(h_dram[0][0:FRONT, :].rearrange("(p c) d -> p c d", p=P),
                         zeros[:, :].unsqueeze(1).to_broadcast([P, FRONT // P, D])).then_inc(front_filled, 16)
            with sp.Fori(0, BATCHES) as i:
                for j in range(BATCH):
                    sp.wait_ge(x_normed, i * BATCH + j + 1)
                    sp.dma_start(h_dram[0][bass.ds(FRONT + (i * BATCH + j) * P, P), :], nm[:, j, :]).then_inc(stored[j], 16)
            for e in range(EXPERTS):
                sp.dma_start(dispatch_dram[e * CAPP:(e + 1) * CAPP, :].rearrange("(p c) d -> p c d", p=P),
                             zeros[:, :].unsqueeze(1).to_broadcast([P, CT, D])).then_inc(zero_filled, 16)
            for layer in range(LAYERS - 1):
                with sp.Fori(0, BLOCKS - 1) as i:
                    sp.wait_ge(u_read, layer * BLOCKS + i + 2)
                    sp.dma_start(h_dram[layer + 1][bass.ds(i * NODES_B, NODES_B), :].rearrange("(c p) d -> p c d", p=P),
                                 nm[:, 0:2, :]).then_inc(stored[0], 16)
                sp.wait_ge(u_read, (layer + 1) * BLOCKS + 1)
                sp.dma_start(h_dram[layer + 1][(BLOCKS - 1) * NODES_B:(BLOCKS - 1) * NODES_B + P, :], nm[:, 0, :]).then_inc(stored[0], 16)

            def load_weights(e, s):
                for which, src, at0 in ((0, "L0_ffn_w1", 0), (1, "L0_ffn_w2", FC * D)):
                    src = t[src][bass.ds(e, 1)] if not isinstance(e, int) else t[src][e:e + 1]
                    c = HALVES if which == 0 else FC
                    sp.dma_start(w_exp[:, s, at0:at0 + FC * D].rearrange("p (c n) -> p c n", c=c),
                                 src.rearrange("o (c p) n -> (o p) c n", p=P)).then_inc(w_in[s], 16)
                src = t["L0_ffn_b2"][bass.ds(e, 1), :] if not isinstance(e, int) else t["L0_ffn_b2"][e:e + 1, :]
                sp.dma_start(w_exp[:, s, WX:WS], src.rearrange("o d -> (o d)").partition_broadcast(P)).then_inc(w_in[s], 16)

            def load_buf(e, s):
                sp.dma_start(buf[:, s], dispatch_dram[bass.ds(e * CAPP, CAPP), :].rearrange(
                    "(c p) d -> p c d", p=P)).then_inc(buf_in[s], 16)

            sp.wait_ge(h_normed, BATCHES)
            load_weights(0, 0)
            load_weights(1, 1)
            sp.wait_ge(scattered, 16 * TILES)
            load_buf(0, 0)
            load_buf(1, 1)

            def store_answers(e):
                for c in range(CT // 2):
                    sp.wait_ge(y_added, e * CT + 2 * c + 2 + 2)
                    sp.dma_start(answer_dram[bass.ds(e * CAPP + 2 * c * P, 2 * P), :].rearrange("(c p) d -> p c d", p=P),
                                 y_out[:, 2 * c:2 * c + 2, :]).then_inc(y_stored[c], 16)

            with sp.Fori(0, EXPERTS // 2 - 1) as i:
                for s in range(2):
                    store_answers(i * 2 + s)
                    load_weights(i * 2 + s + 2, s)
                    load_buf(i * 2 + s + 2, s)
            for e in range(EXPERTS - 2, EXPERTS):
                store_answers(e)

            for i in range(BATCHES):
                lo, hi = i * BATCH, (i + 1) * BATCH if i < BATCHES - 1 else TILES - 1
                sp.wait_ge(y_done, i + 1)
                sp.dma_start(out[lo * P:hi * P, :].rearrange("(t p) d -> p t d", p=P),
                             x_sb[:, lo:hi, :]).then_inc(out_done, 16)
            sp.dma_start(out[(TILES - 1) * P:N, :], x_sb[0:TAIL, TILES - 1, :]).then_inc(out_done, 16)
            sp.wait_ge(out_done, 16 * (BATCHES + 1))

        @block.gpsimd
        def _(pool):
            pool.memset(dst_i, -1).then_inc(cleared, 1)
            pool.memset(src_i, 0).then_inc(cleared, 1)
            pool.memset(x_sb[:, TILES - 1, :], 0.0).then_inc(cleared, 1)
            pool.memset(zeros[:, :], 0.0).then_inc(consts, 1)
            pool.memset(ones[:, :], 1.0).then_inc(consts, 1)
            pool.memset(eps_col[:, :], EPS).then_inc(consts, 1)
            pool.memset(idx_cols[:, GROUPS * CHUNKS:], 0).then_inc(consts, 1)
            pool.memset(agg[:, :, 0:FRONT], 0.0).then_inc(consts, 1)
            pool.memset(agg[:, :, FRONT + NPAD:COLS], 0.0).then_inc(consts, 1)
            pool.memset(rows[:, :, D:D + 1], 1.0).then_inc(consts, 1)
            pool.iota(least_i[:, :], [[NODES_B, LOOPS], [0, 2 * HALF_GROUPS]], base=NODES_B - FRONT, channel_multiplier=0).then_inc(consts, 1)
            pool.iota(iota_i[:, :], [[1, P]], base=0, channel_multiplier=0).then_inc(consts, 1)
            pool.iota(tok_i[:, :], [[P, TILES]], base=0, channel_multiplier=1).then_inc(consts, 1)
            pool.iota(exp_i[:, :], [[0, TILES], [1, EXPERTS]], base=0, channel_multiplier=0).then_inc(consts, 1)
            pool.sem_inc(tok_kept, BATCH)
            pool.wait_ge(consts, CONSTS - 2)
            pool.affine_select(out=ident[:, :], in_=ones[:, :], pattern=[[-1, P]], compare_op=ALU.is_equal, fill=0.0,
                               base=0, channel_multiplier=1).then_inc(consts, 1)
            pool.affine_select(out=upto[:, :], in_=ones[:, :], pattern=[[1, P]], compare_op=ALU.is_ge, fill=0.0,
                               base=0, channel_multiplier=-1).then_inc(consts, 1)

            pool.wait_ge(tables_ready, 2)
            general = pool.value_load(general_flag[0:1, 0:1], min_val=0, max_val=1)
            for layer in range(LAYERS):
                h = h_dram[layer]
                if layer == 0:
                    pool.wait_ge(front_filled, 16)
                    for j in range(BATCH):
                        pool.wait_ge(stored[j], 16 * BATCHES)
                else:
                    pool.wait_ge(stored[0], 16 * (BATCHES + layer * BLOCKS))
                with pool.If(general > 0):
                    with pool.Fori(0, GROUPS * CHUNKS) as c:
                        gate(pool, turn, (c + layer * GROUPS * CHUNKS) * SLOW_STEPS + 3)
                        pool.indirect_dma_start(
                            rows[:, 0, 0:D], None, h,
                            bass.IndirectOffsetOnAxis(ap=slow_idx[:, 0:1], axis=0)).then_inc(slow_landed, 16)
                with pool.Else():
                    with pool.Fori(0, LOOPS) as i:
                        for half in range(2):
                            gate(pool, idx_staged, layer * (2 * LOOPS + 1) + 2 * i + half + 1)
                            for k in range(HALF_GROUPS):
                                gate(pool, summed, layer * GROUPS + (2 * i + half) * HALF_GROUPS + k + 1)
                                for c in range(CHUNKS):
                                    s = k * CHUNKS + c
                                    pool.indirect_dma_start(
                                        rows[:, s, 0:D], None, h,
                                        bass.IndirectOffsetOnAxis(ap=idx_now[:, half, s:s + 1], axis=0),
                                    ).then_inc(landed[s], 16)
                pool.end_ifs()

            with pool.Fori(0, BATCHES) as i:
                for j in range(BATCH):
                    gate(pool, tok_normed, i * BATCH + j + 1)
                    pool.tensor_copy(tokens[:, bass.ds(i * BATCH + j, 1), :], nm[:, j:j + 1, :]).then_inc(tok_kept, 1)

            pool.wait_ge(zero_filled, 16 * EXPERTS)
            pool.wait_ge(routed, 1)
            pool.wait_ge(tok_kept, TILES + BATCH)
            for i in range(TILES):
                pool.indirect_dma_start(
                    dispatch_dram, bass.IndirectOffsetOnAxis(ap=scatter_idx[:, i:i + 1], axis=0), tokens[:, i, :], None,
                    bounds_check=EXPERTS * CAPP - 1, oob_is_err=False).then_inc(scattered, 16)

            pool.wait_ge(scattered, 16 * TILES)
            pool.memset(hmid[:, :, 2 * CAP_N:], 0.0).then_inc(hmid_padded, 1)

            for c in range(CT // 2):
                pool.wait_ge(y_stored[c], 16 * EXPERTS)
            for i in range(TILES):
                if i >= 2 * BATCH and i % BATCH == 0:
                    pool.wait_ge(y_done, i // BATCH - 1)
                pool.indirect_dma_start(
                    y_slot(i), None, answer_dram,
                    bass.IndirectOffsetOnAxis(ap=gather_idx[:, i:i + 1], axis=0)).then_inc(y_back[i % (2 * BATCH)], 16)

        @block.scalar
        def _(act):
            act.dma_start(vec_rows[0:VEC0, :], t["L0_ffn_b1"].rearrange("e (f p) -> (e f) p", p=P)).then_inc(params_in, 16)
            for layer in range(LAYERS):
                n = layer + 1
                for w, name in enumerate((f"b{n}a", f"b{n}b", f"g{n}", f"be{n}")):
                    r = VEC0 + (layer * 4 + w) * HALVES
                    act.dma_start(vec_rows[r:r + HALVES, :],
                                  t["L0_gnn_" + name].rearrange("(k p) -> k p", p=P)).then_inc(params_in, 16)
                for w, name in enumerate((f"W{n}a", f"W{n}b")):
                    act.dma_start(w_gnn[:, layer, w],
                                  t["L0_gnn_" + name].rearrange("(k p) n -> p k n", p=P)).then_inc(params_in, 16)
            act.dma_start(gate_w[:, :, :], t["L0_ffn_gate_w"].rearrange("(k p) e -> p k e", p=P)).then_inc(params_in, 16)
            act.dma_start(gate_b[:, :], t["L0_ffn_gate_b"].partition_broadcast(P)).then_inc(params_in, 16)

            act.sem_inc(partial_copied, 2)
            act.sem_inc(hid_ready, 1)
            act.sem_inc(u_ready, 1)
            act.sem_inc(f_ready, 4)

            def layer_norm_batch(i, nth, source, slot_free, done):
                act.wait_ge(ln_var, nth * BATCHES + i + 1)
                nc.scalar.activation(ln_w[:, 6, :], ln_w[:, 5, :], ACT.Sqrt).then_inc(ln_std, 1)
                gate(act, ln_ready, nth * BATCHES + i + 1)
                for j in range(BATCH):
                    slot_free(j)
                    nc.scalar.activation(nm[:, j:j + 1, :], source[:, bass.ds(i * BATCH + j, 1), :], ACT.Identity,
                                         bias=ln_w[:, 8, j:j + 1], scale=ln_w[:, 7, j:j + 1]).then_inc(done, 1)

            layer_norm_batch(0, 0, x_sb, lambda j: None, x_normed)
            with act.Fori(1, BATCHES) as i:
                def slot_free(j):
                    gate(act, stored[j], 16 * i)
                    gate(act, x_turned, (i - 1) * BATCH + j + 1)
                layer_norm_batch(i, 0, x_sb, slot_free, x_normed)

            act.wait_ge(vecs_ready, 1)
            act.wait_ge(tables_ready, 2)
            general = act.value_load(general_flag[0:1, 0:1], min_val=0, max_val=1)
            for layer in range(LAYERS):
                width = D + 1 if layer == 0 else D

                def mlp_hid(b, size):
                    gate(act, out_summed, b + 1)
                    gate(act, hid_summed, b + 1)
                    for m in range(HALVES):
                        ins = nc.scalar.activation(hid[:, m, 0:size], bank[4][:, m * NODES_B:m * NODES_B + size], ACT.Relu,
                                                   bias=vec(layer, 0, m))
                    ins.then_inc(hid_ready, 1)

                def mlp_u(b, size):
                    gate(act, u_kept, b + 1)
                    if layer < LAYERS - 1:
                        gate(act, u_turned, b + 1)
                    gate(act, out_summed, b + 2)
                    for m in range(HALVES):
                        ins = nc.scalar.activation(u_stage[:, m, 0:size], bank[5][:, m * NODES_B:m * NODES_B + size], ACT.Relu,
                                                   bias=vec(layer, 1, m))
                    ins.then_inc(u_ready, 1)

                if layer > 0:
                    act.wait_ge(c_summed, layer)
                    nc.scalar.copy(c_row[:, :], bank[7][0:1, 0:D])
                    for k in range(HALVES):
                        w = w_gnn[:, layer, 0, k, :]
                        ins = nc.scalar.mul(w, w, bn_w[:, 3, k:k + 1])
                    ins.then_inc(wa_scaled, 1)
                if layer == LAYERS - 1:
                    act.wait_ge(u_turned, layer * BLOCKS + 1)

                with act.If(general > 0):
                    with act.Fori(0, GROUPS * CHUNKS) as c:
                        with act.Fori(0, TILES) as w:
                            act.wait_ge(turn, (c + layer * GROUPS * CHUNKS) * SLOW_STEPS + w * 6 + 5)
                            nc.scalar.copy(partial[:, 0, 0:width], bank[0][:, 0:width]).then_inc(turn, 1)
                    with act.Fori(0, LOOPS) as i:
                        mlp_hid(i + layer * BLOCKS, NODES_B)
                        mlp_u(i + layer * BLOCKS, NODES_B)
                with act.Else():
                    with act.Fori(0, LOOPS) as i:
                        for k in range(2 * HALF_GROUPS):
                            g = layer * GROUPS + i * 2 * HALF_GROUPS + k
                            gate(act, sums_turned, g + 1)
                            act.wait_ge(summed, g + 1 + 4)
                            nc.scalar.copy(partial[:, k % 2, 0:width], bank[k % 2][:, 0:width]).then_inc(partial_copied, 1)
                            if k == HID_AT:
                                mlp_hid(i + layer * BLOCKS, NODES_B)
                            if k == OUT_AT:
                                mlp_u(i + layer * BLOCKS, NODES_B)
                act.end_ifs()
                for b, size in ((LOOPS, NODES_B), (LOOPS + 1, P)):
                    mlp_hid(layer * BLOCKS + b, size)
                    mlp_u(layer * BLOCKS + b, size)

                act.wait_ge(bn_var, layer + 1)
                nc.scalar.activation(bn_w[:, 1, :], bn_w[:, 0, :], ACT.Sqrt).then_inc(bn_std, 1)

            act.wait_ge(bn_ready, LAYERS)
            act.wait_ge(u_kept, LAYERS * BLOCKS + 1)
            for j in range(BATCH):
                act.wait_ge(stored[j], 16 * (BATCHES + (0 if j else (LAYERS - 1) * BLOCKS)))
            with act.Fori(0, BATCHES) as i:
                gate(act, tok_scored, (i + 1) * BATCH)
                for m in range(HALVES):
                    ins = nc.scalar.activation(fm[:, :, m, :],
                                               agg[:, m, bass.ds(FRONT + i * BATCH * P, BATCH * P)].rearrange("p (j n) -> p j n", n=P),
                                               ACT.Identity, bias=bn_w[:, 4, m:m + 1], scale=bn_w[:, 3, m:m + 1])
                ins.then_inc(h_normed, 1)

                def slot_free(j):
                    gate(act, tok_turned, i * BATCH + j + 1)
                    gate(act, tok_kept, i * BATCH + j + 1)
                layer_norm_batch(i, 1, x_sb, slot_free, tok_normed)

            act.wait_ge(exp_in, 1)
            nc.scalar.activation(r_c, r_b, ACT.Exp).then_inc(exp_done, 1)

            act.wait_ge(hmid_padded, 1)
            with act.Fori(0, EXPERTS // 2) as i:
                for s in range(2):
                    e = 2 * i + s
                    gate(act, y_summed, e * CT + CT)
                    for q in range(2 * FC):
                        f, n = q // 2, q % 2
                        gate(act, f_summed, e * 2 * FC + q + 1)
                        nc.scalar.activation(hmid[:, f, n * CAP_N:(n + 1) * CAP_N], bank[q % 4][:, 0:CAP_N], ACT.Relu,
                                             bias=vecs[:, bass.ds(e * FC + f, 1)]).then_inc(f_ready, 1)

            for i in range(TILES):
                act.wait_ge(y_back[i % (2 * BATCH)], 16 * (i // (2 * BATCH) + 1))
                slot = y_slot(i)
                nc.scalar.activation(slot, slot, ACT.Copy, scale=route[:, 13, i:i + 1]).then_inc(y_scaled, 1)

        @block.tensor
        def _(pe):
            pe.sem_inc(summed, 4)
            pe.sem_inc(sums_turned, 2)
            pe.sem_inc(out_summed, 1)
            pe.sem_inc(u_turned, 1)
            pe.sem_inc(tok_turned, BATCH)
            pe.sem_inc(tok_scored, BATCH)
            pe.sem_inc(y_summed, CT)

            pe.wait_ge(consts, CONSTS)
            pe.wait_ge(edges_ready, 1)
            for a, src in enumerate((src_f, rel_f, dst_f)):
                for q in range(2):
                    for c in range(CHUNKS):
                        ins = pe.transpose(bank[2 * a + q][:, c * GROWS:(c + 1) * GROWS],
                                           src[0:GROWS, q, c * P:(c + 1) * P], ident[0:GROWS, 0:GROWS])
                    ins.then_inc(prep_turned, 1)
            for n, col in enumerate((base[0:GROWS, 0:1], base[0:GROWS, 1:2], any_far[0:GROWS, :])):
                ins = pe.transpose(bank[6][0:1, n * GROWS:(n + 1) * GROWS], col, ident[0:GROWS, 0:GROWS])
            ins.then_inc(prep_turned, 1)
            pe.wait_ge(params_in, 16 * PARAMS)
            pe.transpose(bank[7][:, 0:NVEC], vec_rows[:, :], ident[0:NVEC, 0:NVEC]).then_inc(vecs_turned, 1)
            pe.wait_ge(tables_ready, 2)
            pe.wait_ge(vecs_ready, 1)

            def turn_tile(src, j, done):
                for m in range(HALVES):
                    ins = pe.transpose(bank[j][:, m * P:(m + 1) * P], src(m), ident[:, :])
                ins.then_inc(done, 1)

            with pe.Fori(0, BATCHES) as i:
                for j in range(BATCH):
                    pe.wait_ge(x_in_agg, i * BATCH + j + 1)
                    pe.sem_inc(gate_passed, 1)
                    pe.wait_ge(x_normed, i * BATCH + j + 1)
                    turn_tile(lambda m: nm[:, j, m * P:(m + 1) * P], j, x_turned)
            pe.wait_ge(x_in_agg, TILES + BATCH)

            general = pe.value_load(general_flag[0:1, 0:1], min_val=0, max_val=1)
            for layer in range(LAYERS):
                width = D + 1 if layer == 0 else D

                def turn_partial(par, done):
                    if layer == 0:
                        pe.transpose(bank[2 + par][0:1, D:D + P], partial[:, par, D:D + 1], ident[:, :])
                    for m in range(HALVES):
                        ins = pe.transpose(bank[2 + par][:, m * P:(m + 1) * P], partial[:, par, m * P:(m + 1) * P], ident[:, :])
                    ins.then_inc(done, 1)

                def turn_sums(g, par):
                    pe.wait_ge(partial_copied, g + 1 + 2)
                    pe.sem_inc(gate_passed, 1)
                    gate(pe, added, g + 1)
                    turn_partial(par, sums_turned)

                def mlp_first(idx, size):
                    b = layer * BLOCKS + idx
                    pe.wait_ge(hid_ready, b + 1)
                    for m in range(HALVES):
                        to = bank[4][:, m * NODES_B:m * NODES_B + size]
                        for k in range(HALVES):
                            ins = pe.matmul(to, wgt(layer, 0, k, m), agg[:, k, bass.ds(idx * NODES_B, size)],
                                            start=(k == 0), stop=(layer == 0 and k == HALVES - 1))
                        if layer > 0:
                            ins = pe.matmul(to, c_row[0:1, m * P:(m + 1) * P], deg_row[0:1, bass.ds(idx * NODES_B, size)],
                                            start=False, stop=True)
                    ins.then_inc(hid_summed, 1)

                def mlp_second(idx, size):
                    b = layer * BLOCKS + idx
                    gate(pe, hid_ready, b + 2)
                    gate(pe, u_ready, b + 1)
                    for m in range(HALVES):
                        for k in range(HALVES):
                            ins = pe.matmul(bank[5][:, m * NODES_B:m * NODES_B + size], wgt(layer, 1, k, m), hid[:, k, 0:size],
                                            start=(k == 0), stop=(k == HALVES - 1))
                    ins.then_inc(out_summed, 1)

                def mlp_turn(idx, size):
                    b = layer * BLOCKS + idx
                    if layer < LAYERS - 1:
                        gate(pe, u_ready, b + 2)
                        gate(pe, u_read, b + 1)
                        for c in range(size // P):
                            for m in range(HALVES):
                                ins = pe.transpose(bank[6][:, c * D + m * P:c * D + (m + 1) * P],
                                                   u_stage[:, m, c * P:(c + 1) * P], ident[:, :])
                        ins.then_inc(u_turned, 1)

                if layer > 0:
                    pe.wait_ge(bn_ready, layer)
                    for k in range(HALVES):
                        ins = pe.matmul(bank[7][0:1, 0:D], bn_w[:, 4, k:k + 1], w_gnn[:, layer, 0, k, :],
                                        start=(k == 0), stop=(k == HALVES - 1))
                    ins.then_inc(c_summed, 1)
                    pe.wait_ge(wa_scaled, layer)

                with pe.If(general > 0):
                    with pe.Fori(0, GROUPS * CHUNKS) as c:
                        step = (c + layer * GROUPS * CHUNKS) * SLOW_STEPS
                        gate(pe, slow_landed, 16 * (c + layer * GROUPS * CHUNKS + 1))
                        with pe.Fori(0, TILES) as w:
                            pe.wait_ge(turn, step + w * 6 + 4)
                            pe.matmul(bank[0][:, 0:width], onehot[:, 0, 0, :], rows[:, 0, 0:width], start=True, stop=True).then_inc(turn, 1)
                            gate(pe, turn, step + w * 6 + 6)
                            turn_partial(0, turn)
                    pe.wait_ge(turn, (layer + 1) * GROUPS * CHUNKS * SLOW_STEPS + 1)
                    with pe.Fori(0, LOOPS) as i:
                        mlp_first(i, NODES_B)
                        mlp_second(i, NODES_B)
                        mlp_turn(i, NODES_B)
                with pe.Else():
                    with pe.Fori(0, LOOPS) as i:
                        for k in range(2 * HALF_GROUPS):
                            g = layer * GROUPS + 2 * i * HALF_GROUPS + k
                            gate(pe, onehot_ready, g + 1)
                            gate(pe, partial_copied, g + 1)
                            for c in range(CHUNKS):
                                s = k % HALF_GROUPS * CHUNKS + c
                                pe.wait_ge(landed[s], 16 * (layer * 2 * LOOPS + 2 * i + k // HALF_GROUPS + 1))
                                ins = pe.matmul(bank[k % 2][:, 0:width], onehot[:, k % 2, c, :], rows[:, s, 0:width],
                                                start=(c == 0), stop=(c == CHUNKS - 1))
                            ins.then_inc(summed, 1)
                            if k > 0:
                                turn_sums(g - 1, (k - 1) % 2)
                            if k == HID_AT:
                                gate(pe, added, layer * GROUPS + i * 2 * HALF_GROUPS + 2)
                                mlp_first(i, NODES_B)
                            if k == OUT_AT:
                                mlp_second(i, NODES_B)
                            if k == TURN_AT:
                                mlp_turn(i, NODES_B)
                        turn_sums(g, k % 2)
                    pe.wait_ge(added, (layer + 1) * GROUPS + 2)
                    pe.sem_inc(gate_passed, 1)
                pe.end_ifs()
                for b, size in ((LOOPS, NODES_B), (LOOPS + 1, P)):
                    mlp_first(b, size)
                    mlp_second(b, size)
                    mlp_turn(b, size)

            pe.wait_ge(u_ready, LAYERS * BLOCKS + 1)
            pe.wait_ge(u_read, (LAYERS - 1) * BLOCKS + 1)
            pe.wait_ge(wa_scaled, LAYERS - 1)
            with pe.Fori(0, BATCHES) as i:
                gate(pe, h_normed, i + 1)
                for j in range(BATCH):
                    pe.wait_ge(tok_copied, i * BATCH + j + 1)
                    turn_tile(lambda m: fm[:, j, m, :], j, h_turned)
                for j in range(BATCH):
                    gate(pe, h_read, i * BATCH + j + 1)
                    pe.wait_ge(tok_normed, i * BATCH + j + 1)
                    turn_tile(lambda m: nm[:, j, m * P:(m + 1) * P], j, tok_turned)
                for j in range(BATCH):
                    tile = i * BATCH + j
                    pe.wait_ge(tok_copied, tile + 1 + BATCH)
                    for m in range(HALVES):
                        ins = pe.matmul(bank[7][:, bass.ds(tile * EXPERTS, EXPERTS)], fm[:, j, m, :], gate_w[:, m, :],
                                        start=(m == 0), stop=(m == HALVES - 1))
                    ins.then_inc(tok_scored, 1)

            pe.wait_ge(chosen, 1)
            pe.matmul(bank[0][:, 0:TE], upto[:, :], r_e, start=True, stop=True).then_inc(counted, 1)
            pe.matmul(bank[1][:, 0:TE], ones[:, :], r_e, start=True, stop=True).then_inc(counted, 1)
            pe.wait_ge(routed, 1)

            with pe.Fori(0, EXPERTS // 2) as i:
                for s in range(2):
                    e = 2 * i + s
                    w1 = w_exp[:, s, 0:FC * D].rearrange("p (k n) -> p k n", k=HALVES)
                    w2 = w_exp[:, s, FC * D:2 * FC * D].rearrange("p (f n) -> p f n", f=FC)
                    pe.wait_ge(buf_in[s], 16 * (i + 1))
                    pe.sem_inc(gate_passed, 1)
                    for c in range(CT):
                        pe.wait_ge(bufT_copied, e * CT + c + 1)
                        for k in range(HALVES):
                            ins = pe.transpose(bank[6 + c % 2][:, k * P:(k + 1) * P], buf[:, s, c, k * P:(k + 1) * P], ident[:, :])
                        ins.then_inc(bufT_turned, 1)
                    pe.wait_ge(w_in[s], 48 * (i + 1))
                    pe.sem_inc(gate_passed, 1)
                    pe.wait_ge(bufT_copied, (e + 1) * CT + 2)
                    pe.sem_inc(gate_passed, 1)
                    for q in range(2 * FC):
                        f, n = q // 2, q % 2
                        pe.wait_ge(f_ready, e * 2 * FC + q + 1)
                        for k in range(HALVES):
                            ins = pe.matmul(bank[q % 4][:, 0:CAP_N], w1[:, k, f * P:(f + 1) * P],
                                            bufT[:, k, n * CAP_N:(n + 1) * CAP_N], start=(k == 0), stop=(k == HALVES - 1))
                        ins.then_inc(f_summed, 1)
                    pe.wait_ge(f_ready, (e + 1) * 2 * FC + 4)
                    pe.sem_inc(gate_passed, 1)
                    for c in range(CT):
                        pe.wait_ge(y_added, e * CT + c + 1)
                        for f in range(FC):
                            ins = pe.matmul(bank[4 + c % 2][:, 0:D], hmid[:, f, c * P:(c + 1) * P], w2[:, f, :],
                                            start=(f == 0), stop=(f == FC - 1))
                        ins.then_inc(y_summed, 1)

        @block.vector
        def _(dve):
            steps = 0

            def link(ins):
                nonlocal steps
                steps += 1
                ins.then_inc(prep, 1)
                dve.wait_ge(prep, steps)

            dve.sem_inc(added, 2)
            dve.sem_inc(u_kept, 1)
            dve.sem_inc(u_read, 1)
            dve.sem_inc(x_in_agg, BATCH)
            dve.sem_inc(tok_copied, BATCH)
            dve.sem_inc(bufT_copied, 2)
            dve.sem_inc(y_added, 2)

            G = slice(0, GROWS)
            dve.wait_ge(edges_in, 16 * 6)
            dve.tensor_copy(src_f[G], src_i[G])
            link(dve.tensor_copy(dst_f[G], dst_i[G]))
            link(dve.tensor_scalar(key_f[G], dst_f[G], 0.0, 65536.0, ALU.is_lt, ALU.mult))
            link(dve.tensor_tensor(key_f[G], key_f[G], dst_f[G], ALU.add))
            link(dve.tensor_reduce(base[G, :], key_f[G], AX.X, ALU.min))
            for q in range(2):
                link(dve.tensor_scalar(rel_f[G, q], dst_f[G, q], base[G, q:q + 1], None, ALU.subtract))
            link(dve.tensor_scalar(key_f[G], rel_f[G], float(P), None, ALU.is_ge))
            link(dve.tensor_reduce(any_far[G, :], key_f[G], AX.XY, ALU.max))
            dve.sem_inc(edges_ready, 1)
            dve.wait_ge(consts, CONSTS)
            link(dve.tensor_copy(iota[:, :], iota_i[:, :]))
            for a, cols in enumerate((idx_cols, rel_cols, dst_cols)):
                for q in range(2):
                    dve.wait_ge(prep_turned, 2 * a + q + 1)
                    to = cols[:, 0:GROUPS * CHUNKS].rearrange("p (g c) -> p c g", c=CHUNKS)[:, :, q * GROWS:(q + 1) * GROWS]
                    turned_edges = bank[2 * a + q][:, 0:CHUNKS * GROWS].rearrange("p (c g) -> p c g", c=CHUNKS)
                    link(dve.tensor_scalar(to, turned_edges, float(FRONT if a == 0 else 0), None, ALU.add))
            link(dve.tensor_copy(rel_cols[:, GROUPS * CHUNKS:], rel_cols[:, 0:CHUNKS]))
            dve.wait_ge(prep_turned, 7)
            dve.tensor_copy(base_row[:, :], bank[6][0:1, 0:GROUPS]).then_inc(tables_ready, 1)
            link(dve.memset(deg_row, 1.0))
            link(dve.tensor_copy(late_row[:, 0, :], least_i[:, :]))
            link(dve.tensor_copy(late_row[:, 1, :], bank[6][0:1, 0:GROUPS]))
            link(dve.tensor_tensor(late_row[:, 2, :], late_row[:, 1, :], late_row[:, 0, :], ALU.is_lt))
            link(dve.tensor_reduce(general_f[:, 0:1], late_row[:, 2, :], AX.X, ALU.max))
            link(dve.tensor_reduce(general_f[:, 1:2], bank[6][0:1, GROUPS:GROUPS + GROWS], AX.X, ALU.max))
            link(dve.tensor_tensor(general_f[:, 2:3], general_f[:, 0:1], general_f[:, 1:2], ALU.max))
            dve.tensor_copy(general_flag[:, :], general_f[:, 2:3]).then_inc(tables_ready, 1)
            dve.wait_ge(vecs_turned, 1)
            dve.tensor_copy(vecs[:, :], bank[7][:, 0:NVEC]).then_inc(vecs_ready, 1)
            dve.wait_ge(tables_ready, 2)

            LN_STEPS = BATCH + 6

            def ln_stats(nb, j, tile):
                dve.bn_stats(ln_st[:, j, :], tile).then_inc(ln_steps, 1)

            def ln_finish(nb):
                s0 = nb * LN_STEPS
                col = lambda c: ln_st[:, :, c]
                w = lambda r: ln_w[:, r, :]
                gate(dve, ln_steps, s0 + BATCH)
                dve.tensor_tensor(w(0), col(1), col(4), ALU.add).then_inc(ln_steps, 1)
                dve.tensor_tensor(w(1), col(1), col(4), ALU.subtract).then_inc(ln_steps, 1)
                dve.tensor_tensor(w(2), col(2), col(5), ALU.add).then_inc(ln_steps, 1)
                gate(dve, ln_steps, s0 + BATCH + 3)
                dve.tensor_tensor(w(3), w(1), w(1), ALU.mult).then_inc(ln_steps, 1)
                dve.tensor_scalar(w(4), w(2), 1.0 / D, EPS, ALU.mult, ALU.add).then_inc(ln_steps, 1)
                gate(dve, ln_steps, s0 + BATCH + 5)
                dve.scalar_tensor_tensor(out=w(5), in0=w(3), scalar=0.25, in1=w(4), op0=ALU.mult, op1=ALU.add).then_inc(ln_var, 1)
                gate(dve, ln_std, nb + 1)
                dve.reciprocal(w(7), w(6)).then_inc(ln_steps, 1)
                gate(dve, ln_steps, s0 + BATCH + 6)
                dve.scalar_tensor_tensor(out=w(8), in0=w(0), scalar=-0.5, in1=w(7), op0=ALU.mult, op1=ALU.mult).then_inc(ln_ready, 1)

            dve.wait_ge(x_in, 16 * (BATCHES + 1))
            with dve.Fori(0, BATCHES) as i:
                for j in range(BATCH):
                    ln_stats(i, j, x_sb[:, bass.ds(i * BATCH + j, 1), :].rearrange("p a d -> p (a d)"))
                ln_finish(i)
                for j in range(BATCH):
                    gate(dve, x_turned, i * BATCH + j + 1)
                    dve.tensor_copy(agg[:, :, bass.ds(FRONT + (i * BATCH + j) * P, P)],
                                    bank[j][:, 0:D].rearrange("p (m n) -> p m n", m=HALVES)).then_inc(x_in_agg, 1)
            dve.wait_ge(x_in_agg, TILES + BATCH)

            general = dve.value_load(general_flag[0:1, 0:1], min_val=0, max_val=1)
            for j in range(2):
                dve.wait_ge(stored[j], 16 * BATCHES)
            for layer in range(LAYERS):
                def add_window(first, par, done):
                    if layer == 0:
                        counts = deg_row[0:1, bass.ds(first, P)]
                        dve.tensor_tensor(counts, counts, bank[2 + par][0:1, D:D + P], ALU.add)
                    window = agg[:, :, bass.ds(first, P)]
                    dve.tensor_tensor(window, window, bank[2 + par][:, 0:D].rearrange("p (m n) -> p m n", m=HALVES),
                                      ALU.add).then_inc(done, 1)

                def one_hots(g, gl, par):
                    dve.wait_ge(summed, g - 2 + 1 + 4)
                    dve.tensor_tensor(onehot[:, par], iota[:, :].unsqueeze(1).to_broadcast([P, CHUNKS, P]),
                                      rel_cols[:, bass.ds(gl * CHUNKS, CHUNKS)].unsqueeze(2).to_broadcast([P, CHUNKS, P]),
                                      ALU.is_equal).then_inc(onehot_ready, 1)

                def add_sums(g, gl, par):
                    first = dve.value_load(base_row[0:1, bass.ds(gl, 1)], min_val=0, max_val=N - 1)
                    gate(dve, added, g + 2)
                    gate(dve, sums_turned, g + 1 + 2)
                    add_window(FRONT + first, par, added)

                def mlp_keep(idx, size, real):
                    b = layer * BLOCKS + idx
                    gate(dve, u_ready, b + 2)
                    for m in range(HALVES):
                        dve.bn_stats(bn_st[:, m, bass.ds(idx, 1), :].rearrange("p a s -> p (a s)"), u_stage[:, m, 0:real])
                    dve.tensor_copy(agg[:, :, bass.ds(idx * NODES_B, size)], u_stage[:, :, 0:size]).then_inc(u_kept, 1)

                def mlp_rows(idx, size):
                    b = layer * BLOCKS + idx
                    if layer < LAYERS - 1:
                        gate(dve, stored[0], 16 * (b + BATCHES))
                        gate(dve, u_turned, b + 2)
                        c = size // P
                        dve.tensor_copy(nm[:, 0:c, :].rearrange("p c d -> p (c d)"), bank[6][:, 0:c * D]).then_inc(u_read, 1)

                with dve.If(general > 0):
                    if layer == 0:
                        dve.sem_inc(turn, 1)
                    with dve.Fori(0, GROUPS * CHUNKS) as c:
                        step = (c + layer * GROUPS * CHUNKS) * SLOW_STEPS
                        gate(dve, turn, step + 1)
                        dve.tensor_copy(slow_idx[:, :], idx_cols[:, bass.ds(c, 1)]).then_inc(turn, 1)
                        dve.tensor_copy(slow_rel[:, :], dst_cols[:, bass.ds(c, 1)]).then_inc(turn, 1)
                        with dve.Fori(0, TILES) as w:
                            dve.wait_ge(turn, step + w * 6 + 3)
                            dve.tensor_scalar(onehot[:, 0, 0, :], iota[:, :], slow_rel[:, 0:1], None, ALU.is_equal).then_inc(turn, 1)
                            gate(dve, turn, step + w * 6 + 7)
                            add_window(FRONT + w * P, 0, turn)
                            dve.wait_ge(turn, step + w * 6 + 8)
                            dve.tensor_scalar(slow_rel[:, :], slow_rel[:, :], float(P), None, ALU.subtract).then_inc(turn, 1)
                    dve.wait_ge(turn, (layer + 1) * GROUPS * CHUNKS * SLOW_STEPS + 1)
                    with dve.Fori(0, LOOPS) as i:
                        mlp_keep(i, NODES_B, NODES_B)
                        mlp_rows(i, NODES_B)
                with dve.Else():
                    dve.tensor_copy(idx_now[:, 0, :], idx_cols[:, 0:SLOTS]).then_inc(idx_staged, 1)
                    if layer == 0:
                        one_hots(0, 0, 0)
                    with dve.Fori(0, LOOPS) as i:
                        for k in range(2 * HALF_GROUPS):
                            gl = 2 * i * HALF_GROUPS + k
                            if k == 0:
                                dve.tensor_copy(idx_now[:, 1, :],
                                                idx_cols[:, bass.ds((2 * i + 1) * SLOTS, SLOTS)]).then_inc(idx_staged, 1)
                            one_hots(layer * GROUPS + gl + 1, gl + 1, (k + 1) % 2)
                            if k > 0:
                                add_sums(layer * GROUPS + gl - 1, gl - 1, (k - 1) % 2)
                            if k == HALF_GROUPS:
                                dve.tensor_copy(idx_now[:, 0, :],
                                                idx_cols[:, bass.ds((2 * i + 2) * SLOTS, SLOTS)]).then_inc(idx_staged, 1)
                            if k == KEEP_AT:
                                mlp_keep(i, NODES_B, NODES_B)
                            if k == ROWS_AT:
                                mlp_rows(i, NODES_B)
                        add_sums(layer * GROUPS + gl, gl, k % 2)
                dve.end_ifs()
                for b, size, real in ((LOOPS, NODES_B, NODES_B), (LOOPS + 1, P, TAIL)):
                    mlp_keep(b, size, real)
                    mlp_rows(b, size)

                dve.wait_ge(u_kept, (layer + 1) * BLOCKS + 1)
                for m in range(HALVES):
                    link(dve.bn_aggr(bn_mv[:, m, :], bn_st[:, m, LAG:, :].rearrange("p b s -> p (b s)")))
                c = VEC0 + (layer * 4 + 2) * HALVES
                gamma, beta = vecs[:, c:c + HALVES], vecs[:, c + HALVES:c + 2 * HALVES]
                if layer > 0:
                    dve.wait_ge(wa_scaled, layer)
                dve.tensor_scalar(bn_w[:, 0, :], bn_mv[:, :, 1], EPS, None, ALU.add).then_inc(bn_var, 1)
                dve.wait_ge(bn_std, layer + 1)
                link(dve.reciprocal(bn_w[:, 2, :], bn_w[:, 1, :]))
                link(dve.tensor_tensor(bn_w[:, 3, :], bn_w[:, 2, :], gamma, ALU.mult))
                link(dve.tensor_tensor(bn_w[:, 5, :], bn_mv[:, :, 0], bn_w[:, 3, :], ALU.mult))
                dve.tensor_tensor(bn_w[:, 4, :], beta, bn_w[:, 5, :], ALU.subtract).then_inc(bn_ready, 1)

            with dve.Fori(0, BATCHES) as i:
                nb = i + BATCHES
                for j in range(BATCH):
                    tile = i * BATCH + j
                    x_tile = x_sb[:, bass.ds(tile, 1), :].rearrange("p a d -> p (a d)")
                    dve.wait_ge(h_turned, tile + 1)
                    dve.tensor_tensor(x_tile, x_tile, bank[j][:, 0:D], ALU.add).then_inc(h_read, 1)
                for j in range(BATCH):
                    tile = i * BATCH + j
                    gate(dve, h_read, tile + 1)
                    ln_stats(nb, j, x_sb[:, bass.ds(tile, 1), :].rearrange("p a d -> p (a d)"))
                ln_finish(nb)
                for j in range(BATCH):
                    dve.wait_ge(tok_turned, i * BATCH + j + 1 + BATCH)
                    dve.tensor_copy(fm[:, j].rearrange("p m n -> p (m n)"), bank[j][:, 0:D]).then_inc(tok_copied, 1)

            def by_tile(flat):
                return flat.rearrange("p (t e) -> p t e", e=EXPERTS)

            def wide(row):
                return route[:, row, :].unsqueeze(2).to_broadcast([P, TILES, EXPERTS])

            def row(r):
                return route[:, r, :]

            SHIFTED_MAX, SUM, INV, PROB, CHOICE_8, CHOICE, REAL, PLACE, KEPT, SENT, ROW_S, ROW_T, ROW_G, WEIGHT = range(14)
            dve.wait_ge(tok_scored, TILES + BATCH)
            dve.wait_ge(tok_kept, TILES + BATCH)
            link(dve.tensor_tensor(by_tile(r_a), by_tile(bank[7][:, 0:TE]),
                                   gate_b[:, :].unsqueeze(1).to_broadcast([P, TILES, EXPERTS]), ALU.add))
            link(dve.tensor_reduce(row(SHIFTED_MAX), by_tile(r_a), AX.X, ALU.max))
            dve.tensor_tensor(by_tile(r_b), by_tile(r_a), wide(SHIFTED_MAX), ALU.subtract).then_inc(exp_in, 1)
            dve.wait_ge(exp_done, 1)
            link(dve.tensor_reduce(row(SUM), by_tile(r_c), AX.X, ALU.add))
            link(dve.reciprocal(row(INV), row(SUM)))
            link(dve.tensor_tensor(by_tile(r_a), by_tile(r_c), wide(INV), ALU.mult))
            link(dve.tensor_reduce(row(PROB), by_tile(r_a), AX.X, ALU.max))
            link(dve.tensor_tensor(by_tile(r_b), by_tile(r_a), wide(PROB), ALU.is_equal))
            link(dve.tensor_copy(r_g, exp_i[:, :]))
            link(dve.scalar_tensor_tensor(out=r_d, in0=r_b, scalar=-float(EXPERTS), in1=r_g, op0=ALU.mult, op1=ALU.add))
            link(dve.tensor_reduce(row(CHOICE_8), by_tile(r_d), AX.X, ALU.min))
            link(dve.tensor_scalar(row(CHOICE), row(CHOICE_8), float(EXPERTS), None, ALU.add))
            link(dve.tensor_copy(row(ROW_S), tok_i[:, :]))
            link(dve.tensor_scalar(row(REAL), row(ROW_S), float(N), None, ALU.is_lt))
            link(dve.tensor_tensor(by_tile(r_d), by_tile(r_g), wide(CHOICE), ALU.is_equal))
            dve.tensor_tensor(by_tile(r_e), by_tile(r_d), wide(REAL), ALU.mult).then_inc(chosen, 1)
            dve.wait_ge(counted, 2)
            link(dve.tensor_copy(r_f, bank[1][:, 0:TE]))
            for e in range(EXPERTS):
                link(dve.tensor_tensor_scan(r_a[:, e:TE:EXPERTS], ones[:, 0:TILES], r_f[:, e:TE:EXPERTS], 0.0, ALU.mult, ALU.add))
            link(dve.tensor_tensor(r_a, r_a, r_f, ALU.subtract))
            link(dve.tensor_tensor(r_a, r_a, bank[0][:, 0:TE], ALU.add))
            link(dve.tensor_tensor(r_a, r_a, r_e, ALU.mult))
            link(dve.tensor_reduce(row(PLACE), by_tile(r_a), AX.X, ALU.add))
            link(dve.tensor_scalar(row(KEPT), row(PLACE), float(CAP), None, ALU.is_le))
            link(dve.tensor_tensor(row(SENT), row(KEPT), row(REAL), ALU.mult))
            link(dve.scalar_tensor_tensor(out=row(ROW_S), in0=row(CHOICE), scalar=float(CAPP), in1=row(PLACE), op0=ALU.mult, op1=ALU.add))
            link(dve.scalar_tensor_tensor(out=row(ROW_T), in0=row(ROW_S), scalar=-float(NO_SLOT + 1), in1=row(SENT), op0=ALU.add, op1=ALU.mult))
            link(dve.tensor_scalar(scatter_idx[:, :], row(ROW_T), float(NO_SLOT), None, ALU.add))
            link(dve.tensor_scalar(row(ROW_G), row(PLACE), float(CAP), 1.0, ALU.min, ALU.max))
            link(dve.scalar_tensor_tensor(out=row(ROW_S), in0=row(CHOICE), scalar=float(CAPP), in1=row(ROW_G), op0=ALU.mult, op1=ALU.add))
            link(dve.tensor_scalar(gather_idx[:, :], row(ROW_S), 1.0, None, ALU.subtract))
            dve.tensor_tensor(row(WEIGHT), row(PROB), row(KEPT), ALU.mult).then_inc(routed, 1)

            def expert(e, s, first):
                if first:
                    dve.wait_ge(w_in[0], 48)
                else:
                    gate(dve, w_in[s], 48 * (e // 2 + 1) if isinstance(e, int) else 24 * (e - s) + 48)
                for c in range(CT):
                    gate(dve, bufT_turned, e * CT + c + 1)
                    dve.tensor_copy(bufT[:, :, c * P:(c + 1) * P],
                                    bank[6 + c % 2][:, 0:D].rearrange("p (k n) -> p k n", k=HALVES)).then_inc(bufT_copied, 1)
                for c in range(CT):
                    if not first and c % 2 == 0:
                        gate(dve, y_stored[c // 2], 16 * e)
                    dve.wait_ge(y_summed, e * CT + c + 1 + CT)
                    dve.tensor_tensor(y_out[:, c:c + 1, :], bank[4 + c % 2][:, 0:D].unsqueeze(1), w_exp[:, s:s + 1, WX:WS],
                                      ALU.add).then_inc(y_added, 1)

            expert(0, 0, True)
            expert(1, 1, False)
            with dve.Fori(1, EXPERTS // 2) as i:
                for s in range(2):
                    expert(2 * i + s, s, False)

            W7 = BATCH * D
            safe, finite = arena[:, 0:W7], arena[:, W7:2 * W7].bitcast(I32)
            for i in range(BATCHES):
                y7 = nm_flat if i % 2 else fm_flat
                dve.wait_ge(y_scaled, (i + 1) * BATCH)
                dve.tensor_scalar(finite, y7, 0.0, 0.0, ALU.mult, ALU.is_equal)
                link(dve.tensor_scalar(safe, y7, 1e4, -1e4, ALU.min, ALU.max))
                link(dve.scalar_tensor_tensor(out=safe, in0=y7, scalar=NEG_INF, in1=safe, op0=ALU.is_ge, op1=ALU.mult))
                link(dve.copy_predicated(safe, finite, y7))
                x7 = x_sb[:, i * BATCH:(i + 1) * BATCH, :].rearrange("p a d -> p (a d)")
                dve.tensor_tensor(x7, x7, safe, ALU.add).then_inc(y_done, 1)
                dve.wait_ge(y_done, i + 1)


_INS = ["x", "src", "dst"] + [f"L0_gnn_{n}" for l in (1, 2, 3) for n in
                              (f"W{l}a", f"b{l}a", f"W{l}b", f"b{l}b", f"g{l}", f"be{l}")] + \
       [f"L0_ffn_{n}" for n in ("gate_w", "gate_b", "w1", "b1", "w2", "b2")]


def kernel(**inputs):
    import numpy as _np
    import concourse.bacc as _bacc
    from concourse import mybir as _mybir
    from concourse.bass_utils import run_bass_kernel_spmd as _run

    nc = _bacc.Bacc("TRN2", target_bir_lowering=False, num_devices=1)
    arrays, args = {}, {}
    for name in _INS:
        a = _np.ascontiguousarray(inputs[name])
        arrays[f"in_{name}_dram"] = a
        args[name] = nc.dram_tensor(f"in_{name}_dram", a.shape, _mybir.dt.from_np(a.dtype), kind="ExternalInput").ap()
    out = nc.dram_tensor("out_dram", (N, D), _mybir.dt.float32, kind="ExternalOutput").ap()
    gnn_moe_program(nc, args, out)
    r = _run(nc, [arrays], core_ids=[0])
    return r.results[0]["out_dram"]
```

```python
from contextlib import ExitStack

import concourse.bass as bass
from concourse import mybir

F32 = mybir.dt.float32
F32R = mybir.dt.float32r
I32 = mybir.dt.int32
ALU = mybir.AluOpType
ACT = mybir.ActivationFunctionType
AX = mybir.AxisListType

P = 128
N = 6250
D = 256
HALVES = D // P
E_GNN = 106250
LAYERS = 3
EPS = 1e-5

TILES = -(-N // P)
NPAD = TILES * P
TAIL = N - (TILES - 1) * P
BATCH = 7
BATCHES = TILES // BATCH
SPLIT = BATCHES - 2
ROUTED = ((0, SPLIT * BATCH), (SPLIT * BATCH, TILES))
PAIRS = (BATCH + 1) // 2

CHUNKS = 4
GE = CHUNKS * P
GROUPS = -(-E_GNN // GE)
HALF_GROUPS = 4
SLOTS = HALF_GROUPS * CHUNKS
LOOPS = GROUPS // (2 * HALF_GROUPS)
HID_AT, OUT_AT, TURN_AT, KEEP_AT, ROWS_AT = 1, 3, 5, 4, 6
GROWS = GROUPS // 2
LAST_E = E_GNN - (GROUPS - 1) * GE

NODES_B = 2 * P
LAG = 3
FRONT = LAG * NODES_B
BLOCKS = LOOPS + 2
COLS = FRONT + NPAD + P

ARENA = TILES * (D + 2)

EXPERTS = 8
FF = 1024
FC = FF // P
CAP = -(-5 * N // (4 * EXPERTS))
CT = -(-CAP // P)
CAPP = CT * P
HALF_T = -(-CT // 2)
LAST_M = -(-(CAP - (CT - 1) * P) // 32) * 32
HALF_COLS = (HALF_T * P, (CT - HALF_T - 1) * P + LAST_M)
FINISH_AT = (1, 4, 8)
W_AT = 1
RPAIRS = CT // 2
ROW = D + 2
NO_SLOT = EXPERTS * CAPP
NEG_INF = float("-inf")

SLOW_STEPS = 2 + TILES * 6

assert TILES % BATCH == 0 and GROUPS % (2 * HALF_GROUPS) == 0
assert FRONT + N == (BLOCKS - 1) * NODES_B + TAIL
assert 0 < LAST_E < GE and GROWS <= P and CT % 2 == 0 and RPAIRS <= 4 and HALF_T * P <= 512


def gnn_moe_program(nc, t, out):
    with ExitStack() as ctx:
        def sb(name, shape, dt=F32):
            return ctx.enter_context(nc.sbuf_tensor(name, shape, dt))

        def sem(name):
            return ctx.enter_context(nc.semaphore(name))

        h_dram = [nc.dram_tensor(f"h_dram{i}", (FRONT + NPAD, D), F32, kind="Internal").ap() for i in range(LAYERS)]
        dispatch_dram = nc.dram_tensor("dispatch_dram", (EXPERTS * CAPP, ROW), F32, kind="Internal").ap()
        x_dram = nc.dram_tensor("x_dram", (NPAD, D), F32, kind="Internal").ap()

        at_agg = -(-nc.sbuf_base // 32) * 32
        agg = sb("agg", [P, HALVES, COLS])
        at_x = -(-nc.sbuf_base // 32) * 32
        x_flat = sb("x_flat", [P, TILES * D])
        x_sb = x_flat[:, 0:TILES * D].rearrange("p (t d) -> p t d", d=D)
        at_arena = -(-nc.sbuf_base // 32) * 32
        arena = sb("arena", [P, ARENA])
        tokens = arena[:, 0:TILES * ROW].rearrange("p (t d) -> p t d", d=ROW)

        at = 0

        def carve(words):
            nonlocal at
            at += words
            assert at <= ARENA
            return arena[:, at - words:at]

        rows = carve(SLOTS * (D + 1)).rearrange("p (s d) -> p s d", d=D + 1)
        onehot = carve(2 * GE).rearrange("p (b c n) -> p b c n", b=2, c=CHUNKS)
        prep0 = at

        def carve_prep(dt=F32):
            return carve(2 * GE).bitcast(dt).rearrange("p (q e) -> p q e", q=2)

        src_i, dst_i = carve_prep(I32), carve_prep(I32)
        src_f, dst_f, key_f, rel_f = (carve_prep() for _ in range(4))
        deg_row = arena[0:1, prep0:prep0 + COLS]

        idx_cols = sb("idx_cols", [P, GROUPS * CHUNKS + SLOTS], I32)
        rel_cols = sb("rel_cols", [P, (GROUPS + 1) * CHUNKS])
        dst_cols = sb("dst_cols", [P, GROUPS * CHUNKS])
        idx_now = sb("idx_now", [P, 2, SLOTS], I32)
        base = sb("base", [P, 2])
        any_far = sb("any_far", [P, 1])
        base_row = sb("base_row", [1, GROUPS], I32)
        least_i = sb("least_i", [1, GROUPS], I32)
        late_row = sb("late_row", [1, 3, GROUPS])
        general_f = sb("general_f", [1, 3])
        general_flag = sb("general_flag", [1, 1], I32)
        c_row = sb("c_row", [1, D])
        slow_idx = sb("slow_idx", [P, 1], I32)
        slow_rel = sb("slow_rel", [P, 1])

        ident = sb("ident", [P, P])
        ones = sb("ones", [P, P])
        upto = sb("upto", [P, P])
        blank = sb("blank", [P, ROW])
        iota_i = agg[:, 0, FRONT:FRONT + P].bitcast(I32)
        iota = sb("iota", [P, P])
        eps_col = sb("eps_col", [P, 1])

        w_gnn = sb("w_gnn", [P, LAYERS, 2, HALVES, D])
        gate_w = sb("gate_w", [P, HALVES, EXPERTS])
        gate_b = sb("gate_b", [P, EXPERTS])
        VEC0 = EXPERTS * FC
        PARAMS = 1 + LAYERS * 6 + 2
        CONSTS = 14
        NVEC = VEC0 + LAYERS * 4 * HALVES
        vec_rows = arena[0:NVEC, ARENA - P:]
        assert prep0 + COLS <= ARENA - P and at <= ARENA - P
        vecs = sb("vecs", [P, NVEC])

        partial = sb("partial", [P, 2, D + 1])
        nm = sb("nm", [P, BATCH, D])
        fm = sb("fm", [P, BATCH, HALVES, P])
        hid = fm[:, 0:2].rearrange("p a m b -> p (a m b)").rearrange("p (m n) -> p m n", m=HALVES)
        u_stage = fm[:, 2:4].rearrange("p a m b -> p (a m b)").rearrange("p (m n) -> p m n", m=HALVES)
        assert BATCH >= 7
        short = [fm[:, 4], fm[:, 5]]
        bn_st = sb("bn_st", [P, HALVES, BLOCKS, 6])
        bn_mv = sb("bn_mv", [P, HALVES, 2])
        bn_w = sb("bn_w", [P, 6, HALVES])
        ln_st = sb("ln_st", [P, BATCH, 6])
        ln_w = sb("ln_w", [P, 10, BATCH])

        TE = TILES * EXPERTS
        tok_i = sb("tok_i", [P, TILES], I32)
        exp_i = sb("exp_i", [P, TE], I32)
        route = sb("route", [P, 12, TILES])
        queued = sb("queued", [P, EXPERTS])
        scatter_idx = sb("scatter_idx", [P, TILES], I32)
        numbers = sb("numbers", [P, 2, CT], I32)
        weights = sb("weights", [P, 2, CT])

        W = HALVES * FF
        HM = 2 * FC * HALF_T * P
        agg_flat = agg[:, :, :].rearrange("p m n -> p (m n)")
        w_exp = agg_flat[:, 0:4 * W].rearrange("p (w o n) -> p w o n", w=2, o=2)
        at_bufT, at_y = 4 * W, 4 * W + 2 * HALVES * CAPP

        def as_parts(name, shape, at_byte):
            return nc.alloc_sbuf_tensor_at(name, shape, F32R, offset=at_byte)

        w_parts = as_parts("w_parts", [P, 2, 2, W], at_agg)
        bufT_parts = as_parts("bufT_parts", [P, 2, HALVES, CAPP], at_agg + 4 * at_bufT)
        hmid_parts = [as_parts(f"hmid_parts{n}", [P, 2, FC, HALF_T * P], at) for n, at in enumerate((at_x, at_arena))]
        y_out = agg_flat[:, at_y:at_y + CT * D].rearrange("p (c d) -> p c d", c=CT)
        hmid = [flat[:, 0:HM].rearrange("p (o f n) -> p o f n", o=2, f=FC) for flat in (x_flat, arena)]
        buf = x_flat[:, HM:HM + 2 * CT * ROW].rearrange("p (s c d) -> p s c d", s=2, c=CT)
        xrows = arena[:, HM:HM + CT * D].rearrange("p (c d) -> p c d", c=CT)
        b2_rows = arena[:, HM + CT * D:HM + CT * D + 2 * D].rearrange("p (s d) -> p s d", s=2)
        safe = nm[:, 0:2, :].rearrange("p a b -> p (a b)")
        finite = fm[:, 0:2].rearrange("p a m b -> p (a m b)").bitcast(I32)
        assert W == FC * D

        def pair_tiles(p):
            return range(2 * p, min(2 * p + 2, BATCH))

        def tok_slot(p, n):
            q = p % 3
            assert FRONT >= 6 * P
            at = agg[:, q, 0:4 * P].rearrange("p (c w) -> p c w", w=D) if q < 2 else agg[:, :, 4 * P:6 * P]
            return at[:, 0:n, :]

        def pair_before(i, p):
            return PAIRS * i + (PAIRS if p == 0 else PAIRS + 1 if p == 3 else p + 1)

        nm_flat = nm[:, :, :].rearrange("p a b -> p (a b)")
        fm_flat = fm[:, :, :, :].rearrange("p a m b -> p (a m b)")


        def route_place(part, k):
            lo, hi = ROUTED[part]
            n = (hi - lo) * EXPERTS
            if part == 0:
                assert 7 * EXPERTS <= P
                return agg[:, 0, FRONT + k * n:FRONT + (k + 1) * n]
            return (nm_flat, fm_flat)[k // 4][:, k % 4 * n:(k % 4 + 1) * n]

        bank = [ctx.enter_context(nc.psum_tensor(f"bank{i}", [P, 512], F32)) for i in range(8)]

        cleared = sem("cleared")
        consts = sem("consts")
        edges_in = sem("edges_in")
        x_in = [sem(f"x_in{i}") for i in range(2)]
        params_in = sem("params_in")
        prep = sem("prep")
        edges_ready = sem("edges_ready")
        prep_turned = sem("prep_turned")
        vecs_turned = sem("vecs_turned")
        vecs_ready = sem("vecs_ready")
        tables_ready = sem("tables_ready")
        counts_set = sem("counts_set")
        gate_passed = sem("gate_passed")
        ln_steps = sem("ln_steps")
        ln_var = sem("ln_var")
        ln_std = sem("ln_std")
        ln_ready = sem("ln_ready")
        x_normed, x_turned = sem("x_normed"), sem("x_turned")
        x_in_agg = [sem(f"x_in_agg{i}") for i in range(2)]
        X_TILES = (range(0, 4), range(4, BATCH))
        stored = [sem(f"stored{i}") for i in range(BATCH)]
        h_normed, h_turned, h_read = sem("h_normed"), sem("h_turned"), sem("h_read")
        idx_staged = sem("idx_staged")
        landed = [sem(f"landed{i}") for i in range(SLOTS)]
        onehot_ready = sem("onehot_ready")
        summed = sem("summed")
        partial_copied = sem("partial_copied")
        sums_turned = sem("sums_turned")
        added = sem("added")
        turn = sem("turn")
        slow_landed = sem("slow_landed")
        hid_summed = sem("hid_summed")
        hid_ready = sem("hid_ready")
        out_summed = sem("out_summed")
        u_ready = sem("u_ready")
        u_kept = sem("u_kept")
        u_turned = sem("u_turned")
        u_read = sem("u_read")
        bn_var = sem("bn_var")
        bn_std = sem("bn_std")
        bn_ready = sem("bn_ready")
        c_summed = sem("c_summed")
        wa_scaled = sem("wa_scaled")
        tok_normed, tok_turned, tok_copied = sem("tok_normed"), sem("tok_turned"), sem("tok_copied")
        tok_kept = [sem(f"tok_kept{j}") for j in range(BATCH)]
        tok_scored = sem("tok_scored")
        exp_in = sem("exp_in")
        exp_done = sem("exp_done")
        chosen = sem("chosen")
        counted = sem("counted")
        scanned = sem("scanned")
        routed = sem("routed")
        front_filled = sem("front_filled")
        zero_filled = sem("zero_filled")
        scattered = sem("scattered")
        w_in = [sem(f"w_in{w}") for w in range(2)]
        w_hi = [sem(f"w_hi{w}") for w in range(2)]
        w_lo = [sem(f"w_lo{w}") for w in range(2)]
        b2_in = [sem(f"b2_in{i}") for i in range(2)]
        buf_in = [sem(f"buf_in{i}") for i in range(2)]
        bufT_turned = sem("bufT_turned")
        bufT_hi = sem("bufT_hi")
        bufT_copied = sem("bufT_copied")
        numbered = sem("numbered")
        f_summed = sem("f_summed")
        f_read = sem("f_read")
        f_split = sem("f_split")
        y_summed = sem("y_summed")
        y_added = sem("y_added")
        y_weighted = sem("y_weighted")
        fix = sem("fix")
        y_done = sem("y_done")
        y_cleared = sem("y_cleared")
        x_saved = sem("x_saved")
        xrow_in = [sem(f"xrow_in{c}") for c in range(CT)]
        out_prefilled = sem("out_prefilled")
        result_out = [sem(f"result_out{c}") for c in range(CT)]

        def gate(eng, semaphore, value):
            eng.wait_ge(semaphore, value)
            eng.sem_inc(gate_passed, 1)

        def queue_no(i, s):
            return (i, 1) if s == 0 else (i + 1, 0)

        def wgt(layer, which, k, m):
            return w_gnn[:, layer, which, k, m * P:(m + 1) * P]

        def vec(layer, which, m):
            c = VEC0 + (layer * 4 + which) * HALVES + m
            return vecs[:, c:c + 1]

        def places(is_short):
            if is_short:
                return short[0], short[1], nm[:, 2:3, :], bank[0:3]
            return hid, u_stage, nm[:, 0:2, :], bank[4:7]

        def x_into_agg(eng, copy, which, i):
            for j in X_TILES[which]:
                gate(eng, x_turned, i * BATCH + j + 1)
                copy(agg[:, :, bass.ds(FRONT + (i * BATCH + j) * P, P)],
                     bank[j][:, 0:D].rearrange("p (m n) -> p m n", m=HALVES)).then_inc(x_in_agg[which], 1)

        block = ctx.enter_context(nc.Block())

        @block.sync
        def _(sp):
            sp.wait_ge(cleared, 2)
            for flat, dst in ((t["dst"], dst_i), (t["src"], src_i)):
                sp.dma_start(dst[0:GROWS, 0, :],
                             flat[0:GROWS * GE].rearrange("(p e) -> p e", e=GE)).then_inc(edges_in, 16)
                sp.dma_start(dst[0:GROWS - 1, 1, :],
                             flat[GROWS * GE:(GROUPS - 1) * GE].rearrange("(p e) -> p e", e=GE)).then_inc(edges_in, 16)
                sp.dma_start(dst[GROWS - 1:GROWS, 1, 0:LAST_E],
                             flat[(GROUPS - 1) * GE:E_GNN].rearrange("(p e) -> p e", p=1)).then_inc(edges_in, 16)
            sp.wait_ge(cleared, 3)
            for i in range(BATCHES):
                lo, hi = i * BATCH, (i + 1) * BATCH if i < BATCHES - 1 else TILES - 1
                sp.dma_start(x_sb[:, lo:hi, :],
                             t["x"][lo * P:hi * P, :].rearrange("(t p) d -> p t d", p=P)).then_inc(x_in[min(i, 1)], 16)
            sp.dma_start(x_sb[0:TAIL, TILES - 1, :], t["x"][(TILES - 1) * P:N, :]).then_inc(x_in[1], 16)

            sp.wait_ge(consts, 2)
            sp.dma_start(h_dram[0][0:FRONT, :].rearrange("(p c) d -> p c d", p=P),
                         blank[:, 0:D].unsqueeze(1).to_broadcast([P, FRONT // P, D])).then_inc(front_filled, 16)
            with sp.Fori(0, BATCHES) as i:
                for j in range(BATCH):
                    sp.wait_ge(x_normed, i * BATCH + j + 1)
                    sp.dma_start(h_dram[0][bass.ds(FRONT + (i * BATCH + j) * P, P), :], nm[:, j, :]).then_inc(stored[j], 16)
            def store_block(layer, i):
                sp.wait_ge(u_read, layer * BLOCKS + i + 2)
                sp.dma_start(h_dram[layer + 1][bass.ds(i * NODES_B, NODES_B), :].rearrange("(c p) d -> p c d", p=P),
                             places(False)[2]).then_inc(stored[0], 16)

            for layer in range(LAYERS - 1):
                if layer == 0:
                    with sp.Fori(0, EXPERTS) as i:
                        store_block(layer, i)
                        sp.dma_start(dispatch_dram[bass.ds(i * CAPP, CAPP), :].rearrange("(p c) d -> p c d", p=P),
                                     blank[:, :].unsqueeze(1).to_broadcast([P, CT, ROW])).then_inc(zero_filled, 16)
                with sp.Fori(EXPERTS if layer == 0 else 0, BLOCKS - 1) as i:
                    store_block(layer, i)
                sp.wait_ge(u_read, (layer + 1) * BLOCKS + 1)
                sp.dma_start(h_dram[layer + 1][(BLOCKS - 1) * NODES_B:(BLOCKS - 1) * NODES_B + P, :],
                             places(True)[2].rearrange("p c d -> p (c d)")).then_inc(stored[1], 16)

            def keep_batch(i, whole):
                gate(sp, h_read, i * PAIRS + 2 * PAIRS)
                here = bass.ds(i * BATCH * P, BATCH * P)
                batch = x_sb[:, bass.ds(i * BATCH, BATCH), :]
                sp.dma_start(x_dram[here, :].rearrange("(t p) d -> p t d", p=P), batch).then_inc(x_saved, 16)
                if whole:
                    sp.dma_start(out[here, :].rearrange("(t p) d -> p t d", p=P), batch).then_inc(out_prefilled, 16)
                for j in range(BATCH):
                    sp.wait_ge(tok_normed, i * BATCH + j + 1)
                    sp.dma_start(tokens[:, bass.ds(i * BATCH + j, 1), 0:D], nm[:, j:j + 1, :]).then_inc(tok_kept[j], 16)

            with sp.Fori(0, BATCHES - 1) as i:
                keep_batch(i, True)
            keep_batch(BATCHES - 1, False)
            lo = (BATCHES - 1) * BATCH
            sp.dma_start(out[lo * P:(TILES - 1) * P, :].rearrange("(t p) d -> p t d", p=P),
                         x_sb[:, lo:TILES - 1, :]).then_inc(out_prefilled, 16)
            sp.dma_start(out[(TILES - 1) * P:N, :], x_sb[0:TAIL, TILES - 1, :]).then_inc(out_prefilled, 16)

            def load_weights(w, e):
                src = t["L0_ffn_w1" if w == 0 else "L0_ffn_w2"]
                src = src[bass.ds(e, 1)] if not isinstance(e, int) else src[e:e + 1]
                c = HALVES if w == 0 else FC
                sp.dma_start(w_exp[:, w, 1, :].rearrange("p (c n) -> p c n", c=c),
                             src.rearrange("o (c p) n -> (o p) c n", p=P)).then_inc(w_in[w], 16)

            def load_b2(e, s):
                src = t["L0_ffn_b2"][bass.ds(e, 1), :] if not isinstance(e, int) else t["L0_ffn_b2"][e:e + 1, :]
                sp.dma_start(b2_rows[:, s], src.rearrange("o d -> (o d)").partition_broadcast(P)).then_inc(b2_in[s], 16)

            def load_buf(e, s):
                sp.dma_start(buf[:, s], dispatch_dram[bass.ds(e * CAPP, CAPP), :].rearrange(
                    "(c p) d -> p c d", p=P)).then_inc(buf_in[s], 16)

            sp.wait_ge(h_normed, BATCHES)
            sp.wait_ge(tok_scored, PAIRS * (BATCHES + 1))
            load_weights(0, 0)
            load_weights(1, 0)
            sp.wait_ge(x_saved, 16 * BATCHES)
            sp.wait_ge(out_prefilled, 16 * (BATCHES + 1))
            sp.wait_ge(scattered, 16 * TILES)
            load_buf(0, 0)
            load_buf(1, 1)
            load_b2(0, 0)
            load_b2(1, 1)

            def load_next(i, s, more):
                e = 2 * i + s
                if more:
                    gate(sp, bufT_turned, (e + 1) * CT)
                    gate(sp, numbered, 2 * (e + 1))
                    load_buf(e + 2, s)
                sp.wait_ge(f_summed, (e + 1) * 2 * FC)
                load_weights(0, e + 1)
                sp.wait_ge(y_summed, (e + 1) * CT)
                load_weights(1, e + 1)
                if more:
                    sp.wait_ge(y_added, (e + 1) * CT + 2)
                    load_b2(e + 2, s)

            with sp.Fori(0, EXPERTS // 2 - 1) as i:
                for s in range(2):
                    load_next(i, s, True)
            load_next(EXPERTS // 2 - 1, 0, False)
            for c in range(CT):
                sp.wait_ge(result_out[c], 16 * EXPERTS)

        @block.gpsimd
        def _(pool):
            pool.memset(dst_i, -1).then_inc(cleared, 1)
            pool.memset(src_i, 0).then_inc(cleared, 1)
            pool.memset(x_sb[:, TILES - 1, :], 0.0).then_inc(cleared, 1)
            pool.memset(blank[:, :], 0.0).then_inc(consts, 1)
            pool.wait_ge(consts, 1)
            pool.memset(blank[:, D:D + 1].bitcast(I32), N).then_inc(consts, 1)
            pool.memset(ones[:, :], 1.0).then_inc(consts, 1)
            pool.memset(eps_col[:, :], EPS).then_inc(consts, 1)
            pool.memset(idx_cols[:, GROUPS * CHUNKS:], 0).then_inc(consts, 1)
            pool.memset(agg[:, :, 0:FRONT], 0.0).then_inc(consts, 1)
            pool.memset(agg[:, :, FRONT + NPAD:COLS], 0.0).then_inc(consts, 1)
            pool.memset(rows[:, :, D:D + 1], 1.0).then_inc(consts, 1)
            pool.iota(least_i[:, :], [[NODES_B, LOOPS], [0, 2 * HALF_GROUPS]], base=NODES_B - FRONT, channel_multiplier=0).then_inc(consts, 1)
            pool.iota(iota_i[:, :], [[1, P]], base=0, channel_multiplier=0).then_inc(consts, 1)
            pool.iota(tok_i[:, :], [[P, TILES]], base=0, channel_multiplier=1).then_inc(consts, 1)
            pool.iota(exp_i[:, :], [[0, TILES], [1, EXPERTS]], base=0, channel_multiplier=0).then_inc(consts, 1)
            for j in range(BATCH):
                pool.sem_inc(tok_kept[j], 16)
            pool.wait_ge(consts, CONSTS - 2)
            pool.affine_select(out=ident[:, :], in_=ones[:, :], pattern=[[-1, P]], compare_op=ALU.is_equal, fill=0.0,
                               base=0, channel_multiplier=1).then_inc(consts, 1)
            pool.affine_select(out=upto[:, :], in_=ones[:, :], pattern=[[1, P]], compare_op=ALU.is_ge, fill=0.0,
                               base=0, channel_multiplier=-1).then_inc(consts, 1)

            pool.wait_ge(tables_ready, 2)
            pool.memset(deg_row, 1.0).then_inc(counts_set, 1)
            general = pool.value_load(general_flag[0:1, 0:1], min_val=0, max_val=1)
            for layer in range(LAYERS):
                h = h_dram[layer]
                if layer == 0:
                    pool.wait_ge(front_filled, 16)
                    for j in range(BATCH):
                        pool.wait_ge(stored[j], 16 * BATCHES)
                else:
                    pool.wait_ge(stored[0], 16 * (BATCHES + layer * (BLOCKS - 1)))
                    pool.wait_ge(stored[1], 16 * (BATCHES + layer))
                with pool.If(general > 0):
                    with pool.Fori(0, GROUPS * CHUNKS) as c:
                        gate(pool, turn, (c + layer * GROUPS * CHUNKS) * SLOW_STEPS + 3)
                        pool.indirect_dma_start(
                            rows[:, 0, 0:D], None, h,
                            bass.IndirectOffsetOnAxis(ap=slow_idx[:, 0:1], axis=0)).then_inc(slow_landed, 16)
                with pool.Else():
                    with pool.Fori(0, LOOPS) as i:
                        for half in range(2):
                            gate(pool, idx_staged, layer * (2 * LOOPS + 1) + 2 * i + half + 1)
                            for k in range(HALF_GROUPS):
                                gate(pool, summed, layer * GROUPS + (2 * i + half) * HALF_GROUPS + k + 1)
                                for c in range(CHUNKS):
                                    s = k * CHUNKS + c
                                    pool.indirect_dma_start(
                                        rows[:, s, 0:D], None, h,
                                        bass.IndirectOffsetOnAxis(ap=idx_now[:, half, s:s + 1], axis=0),
                                    ).then_inc(landed[s], 16)
                pool.end_ifs()

            pool.wait_ge(zero_filled, 16 * EXPERTS)
            for part, (lo, hi) in enumerate(ROUTED):
                pool.wait_ge(routed, part + 1)
                for j in range(BATCH):
                    pool.wait_ge(tok_kept[j], 16 * (hi // BATCH + 1))
                for i in range(lo, hi):
                    pool.indirect_dma_start(
                        dispatch_dram, bass.IndirectOffsetOnAxis(ap=scatter_idx[:, i:i + 1], axis=0), tokens[:, i, :], None,
                        bounds_check=EXPERTS * CAPP - 1, oob_is_err=False).then_inc(scattered, 16)

            pool.memset(y_out[:, CT - 1, :], 0.0).then_inc(y_cleared, 1)

            pool.wait_ge(x_saved, 16 * BATCHES)
            pool.wait_ge(out_prefilled, 16 * (BATCHES + 1))
            pool.wait_ge(scattered, 16 * TILES)

            def serve(i, s):
                e = 2 * i + s
                gate(pool, numbered, 2 * (e + 1))
                for c in range(CT):
                    if not (isinstance(e, int) and e == 0):
                        gate(pool, result_out[c], 16 * e)
                    pool.indirect_dma_start(
                        xrows[:, c, :], None, x_dram,
                        bass.IndirectOffsetOnAxis(ap=numbers[:, s, c:c + 1], axis=0)).then_inc(xrow_in[c], 16)
                for c in range(CT):
                    if c % 2 == 0:
                        gate(pool, y_done, e * RPAIRS + c // 2 + 1)
                    pool.indirect_dma_start(
                        out, bass.IndirectOffsetOnAxis(ap=numbers[:, s, c:c + 1], axis=0), xrows[:, c, :], None,
                        bounds_check=N - 1, oob_is_err=False).then_inc(result_out[c], 16)

            serve(0, 0)
            serve(0, 1)
            with pool.Fori(1, EXPERTS // 2) as i:
                for s in range(2):
                    serve(i, s)

        @block.scalar
        def _(act):
            act.dma_start(vec_rows[0:VEC0, :], t["L0_ffn_b1"].rearrange("e (f p) -> (e f) p", p=P)).then_inc(params_in, 16)
            for layer in range(LAYERS):
                n = layer + 1
                for w, name in enumerate((f"b{n}a", f"b{n}b", f"g{n}", f"be{n}")):
                    r = VEC0 + (layer * 4 + w) * HALVES
                    act.dma_start(vec_rows[r:r + HALVES, :],
                                  t["L0_gnn_" + name].rearrange("(k p) -> k p", p=P)).then_inc(params_in, 16)
                for w, name in enumerate((f"W{n}a", f"W{n}b")):
                    act.dma_start(w_gnn[:, layer, w],
                                  t["L0_gnn_" + name].rearrange("(k p) n -> p k n", p=P)).then_inc(params_in, 16)
            act.dma_start(gate_w[:, :, :], t["L0_ffn_gate_w"].rearrange("(k p) e -> p k e", p=P)).then_inc(params_in, 16)
            act.dma_start(gate_b[:, :], t["L0_ffn_gate_b"].partition_broadcast(P)).then_inc(params_in, 16)

            act.sem_inc(x_in_agg[1], len(X_TILES[1]))
            act.sem_inc(partial_copied, 2)
            act.sem_inc(hid_ready, 1)
            act.sem_inc(u_ready, 1)
            act.sem_inc(f_read, 4)

            def layer_norm_batch(i, nth, source, slot_free, done):
                act.wait_ge(ln_var, nth * BATCHES + i + 1)
                nc.scalar.activation(ln_w[:, 6, :], ln_w[:, 5, :], ACT.Sqrt).then_inc(ln_std, 1)
                gate(act, ln_ready, nth * BATCHES + i + 1)
                for j in range(BATCH):
                    slot_free(j)
                    nc.scalar.activation(nm[:, j:j + 1, :], source[:, bass.ds(i * BATCH + j, 1), :], ACT.Identity,
                                         bias=ln_w[:, 8, j:j + 1], scale=ln_w[:, 7, j:j + 1]).then_inc(done, 1)

            layer_norm_batch(0, 0, x_sb, lambda j: None, x_normed)
            with act.Fori(1, BATCHES) as i:
                def slot_free(j):
                    gate(act, stored[j], 16 * i)
                    gate(act, x_turned, (i - 1) * BATCH + j + 1)
                layer_norm_batch(i, 0, x_sb, slot_free, x_normed)
                x_into_agg(act, nc.scalar.copy, 1, i - 1)
            x_into_agg(act, nc.scalar.copy, 1, BATCHES - 1)

            act.wait_ge(vecs_ready, 1)
            act.wait_ge(tables_ready, 2)
            general = act.value_load(general_flag[0:1, 0:1], min_val=0, max_val=1)
            for layer in range(LAYERS):
                width = D + 1 if layer == 0 else D

                def mlp_hid(b, size, is_short=False):
                    to, _, _, banks = places(is_short)
                    if not is_short:
                        gate(act, out_summed, b + 1)
                    gate(act, hid_summed, b + 1)
                    for m in range(HALVES):
                        ins = nc.scalar.activation(to[:, m, 0:size], banks[0][:, m * NODES_B:m * NODES_B + size], ACT.Relu,
                                                   bias=vec(layer, 0, m))
                    ins.then_inc(hid_ready, 1)

                def mlp_u(b, size, is_short=False):
                    _, to, _, banks = places(is_short)
                    if not is_short:
                        gate(act, u_kept, b + 1)
                        if layer < LAYERS - 1:
                            gate(act, u_turned, b + 1)
                    gate(act, out_summed, b + 2)
                    for m in range(HALVES):
                        ins = nc.scalar.activation(to[:, m, 0:size], banks[1][:, m * NODES_B:m * NODES_B + size], ACT.Relu,
                                                   bias=vec(layer, 1, m))
                    ins.then_inc(u_ready, 1)

                if layer > 0:
                    act.wait_ge(c_summed, layer)
                    nc.scalar.copy(c_row[:, :], bank[7][0:1, 0:D])
                    for k in range(HALVES):
                        w = w_gnn[:, layer, 0, k, :]
                        ins = nc.scalar.mul(w, w, bn_w[:, 3, k:k + 1])
                    ins.then_inc(wa_scaled, 1)
                if layer == LAYERS - 1:
                    act.wait_ge(u_turned, layer * BLOCKS + 1)

                with act.If(general > 0):
                    with act.Fori(0, GROUPS * CHUNKS) as c:
                        with act.Fori(0, TILES) as w:
                            act.wait_ge(turn, (c + layer * GROUPS * CHUNKS) * SLOW_STEPS + w * 6 + 5)
                            nc.scalar.copy(partial[:, 0, 0:width], bank[0][:, 0:width]).then_inc(turn, 1)
                    with act.Fori(0, LOOPS) as i:
                        mlp_hid(i + layer * BLOCKS, NODES_B)
                        mlp_u(i + layer * BLOCKS, NODES_B)
                with act.Else():
                    with act.Fori(0, LOOPS) as i:
                        for k in range(2 * HALF_GROUPS):
                            g = layer * GROUPS + i * 2 * HALF_GROUPS + k
                            gate(act, sums_turned, g + 1)
                            act.wait_ge(summed, g + 1 + 4)
                            nc.scalar.copy(partial[:, k % 2, 0:width], bank[k % 2][:, 0:width]).then_inc(partial_copied, 1)
                            if k == HID_AT:
                                mlp_hid(i + layer * BLOCKS, NODES_B)
                            if k == OUT_AT:
                                mlp_u(i + layer * BLOCKS, NODES_B)
                act.end_ifs()
                b = layer * BLOCKS + LOOPS
                for step in (mlp_hid, mlp_u):
                    step(b, NODES_B)
                    step(b + 1, P, True)

                act.wait_ge(bn_var, layer + 1)
                nc.scalar.activation(bn_w[:, 1, :], bn_w[:, 0, :], ACT.Sqrt).then_inc(bn_std, 1)

            act.wait_ge(bn_ready, LAYERS)
            act.wait_ge(u_kept, LAYERS * BLOCKS + 1)
            for j in range(BATCH):
                act.wait_ge(stored[j], 16 * (BATCHES + (LAYERS - 1) * (BLOCKS - 1 if j == 0 else 1 if j == 1 else 0)))
            def h_norm(i):
                for m in range(HALVES):
                    ins = nc.scalar.activation(fm[:, :, m, :],
                                               agg[:, m, bass.ds(FRONT + i * BATCH * P, BATCH * P)].rearrange("p (j n) -> p j n", n=P),
                                               ACT.Identity, bias=bn_w[:, 4, m:m + 1], scale=bn_w[:, 3, m:m + 1])
                ins.then_inc(h_normed, 1)

            def tok_norm(i):
                def slot_free(j):
                    gate(act, tok_turned, i * PAIRS + j // 2 + 1)
                    gate(act, tok_kept[j], i * 16 + 16)
                layer_norm_batch(i, 1, x_sb, slot_free, tok_normed)

            def exponentials(part):
                act.wait_ge(exp_in, part + 1)
                nc.scalar.activation(route_place(part, 2), route_place(part, 1), ACT.Exp).then_inc(exp_done, 1)

            h_norm(0)
            with act.Fori(0, BATCHES - 1) as i:
                gate(act, h_turned, (i + 1) * PAIRS)
                h_norm(i + 1)
                tok_norm(i)
            exponentials(0)
            tok_norm(BATCHES - 1)
            exponentials(1)

            def hi_weights(w, e):
                gate(act, w_in[w], 16 * (e + 1))
                nc.scalar.copy(w_parts[:, w, 0, :], w_exp[:, w, 1, :]).then_inc(w_hi[w], 1)

            def weigh(s, e, c):
                gate(act, y_added, e * CT + c + 1 + 2)
                nc.scalar.activation(y_out[:, c, :], y_out[:, c, :], ACT.Copy, scale=weights[:, s, c:c + 1]).then_inc(y_weighted, 1)

            def expert(i, s, last=False):
                e = 2 * i + s
                for q in range(2 * FC):
                    n, f = q // FC, q % FC
                    if q % FC == 0:
                        gate(act, y_summed, e * CT) if not (isinstance(e, int) and e == 0) else None
                    gate(act, f_summed, e * 2 * FC + q + 1)
                    cols = HALF_COLS[n]
                    bias = vecs[:, bass.ds(e * FC + f, 1)] if not isinstance(e, int) else vecs[:, e * FC + f:e * FC + f + 1]
                    nc.scalar.activation(hmid_parts[n][:, 0, f, 0:cols], bank[q % 4][:, 0:cols], ACT.Relu, bias=bias)
                    nc.scalar.activation(hmid[n][:, 1, f, 0:cols], bank[q % 4][:, 0:cols], ACT.Relu, bias=bias).then_inc(f_read, 1)
                    if q == FC - 1:
                        hi_weights(1, e)
                for c in range(CT):
                    weigh(s, e, c)
                    if c == W_AT and not last:
                        hi_weights(0, e + 1)

            hi_weights(0, 0)
            act.wait_ge(y_cleared, 1)
            with act.Fori(0, EXPERTS // 2 - 1) as i:
                for s in range(2):
                    expert(i, s)
            expert(EXPERTS // 2 - 1, 0)
            expert(EXPERTS // 2 - 1, 1, True)

        @block.tensor
        def _(pe):
            pe.sem_inc(summed, 4)
            pe.sem_inc(sums_turned, 2)
            pe.sem_inc(out_summed, 1)
            pe.sem_inc(u_turned, 1)
            pe.sem_inc(tok_turned, PAIRS)
            pe.sem_inc(tok_scored, PAIRS)

            pe.wait_ge(consts, CONSTS)
            pe.wait_ge(edges_ready, 1)
            for a, src in enumerate((src_f, rel_f, dst_f)):
                for q in range(2):
                    for c in range(CHUNKS):
                        ins = pe.transpose(bank[2 * a + q][:, c * GROWS:(c + 1) * GROWS],
                                           src[0:GROWS, q, c * P:(c + 1) * P], ident[0:GROWS, 0:GROWS])
                    ins.then_inc(prep_turned, 1)
            for n, col in enumerate((base[0:GROWS, 0:1], base[0:GROWS, 1:2], any_far[0:GROWS, :])):
                ins = pe.transpose(bank[6][0:1, n * GROWS:(n + 1) * GROWS], col, ident[0:GROWS, 0:GROWS])
            ins.then_inc(prep_turned, 1)
            pe.wait_ge(tables_ready, 2)

            def turn_tile(src, j, done):
                for m in range(HALVES):
                    ins = pe.transpose(bank[j][:, m * P:(m + 1) * P], src(m), ident[:, :])
                ins.then_inc(done, 1)

            with pe.Fori(0, BATCHES) as i:
                for j in range(BATCH):
                    which = 0 if j in X_TILES[0] else 1
                    pe.wait_ge(x_in_agg[which], i * len(X_TILES[which]) + X_TILES[which].index(j) + 1)
                    pe.sem_inc(gate_passed, 1)
                    pe.wait_ge(x_normed, i * BATCH + j + 1)
                    turn_tile(lambda m: nm[:, j, m * P:(m + 1) * P], j, x_turned)
            for which, tiles in enumerate(X_TILES):
                pe.wait_ge(x_in_agg[which], (BATCHES + 1) * len(tiles))
            pe.wait_ge(params_in, 16 * PARAMS)
            pe.transpose(bank[7][:, 0:NVEC], vec_rows[:, :], ident[0:NVEC, 0:NVEC]).then_inc(vecs_turned, 1)
            pe.wait_ge(vecs_ready, 1)

            general = pe.value_load(general_flag[0:1, 0:1], min_val=0, max_val=1)
            for layer in range(LAYERS):
                width = D + 1 if layer == 0 else D

                def turn_partial(par, done):
                    if layer == 0:
                        pe.transpose(bank[2 + par][0:1, D:D + P], partial[:, par, D:D + 1], ident[:, :])
                    for m in range(HALVES):
                        ins = pe.transpose(bank[2 + par][:, m * P:(m + 1) * P], partial[:, par, m * P:(m + 1) * P], ident[:, :])
                    ins.then_inc(done, 1)

                def turn_sums(g, par):
                    pe.wait_ge(partial_copied, g + 1 + 2)
                    pe.sem_inc(gate_passed, 1)
                    gate(pe, added, g + 1)
                    turn_partial(par, sums_turned)

                def mlp_first(idx, size, is_short=False):
                    b = layer * BLOCKS + idx
                    bank_1 = places(is_short)[3][0]
                    if not is_short:
                        pe.wait_ge(hid_ready, b + 1)
                    for m in range(HALVES):
                        to = bank_1[:, m * NODES_B:m * NODES_B + size]
                        for k in range(HALVES):
                            ins = pe.matmul(to, wgt(layer, 0, k, m), agg[:, k, bass.ds(idx * NODES_B, size)],
                                            start=(k == 0), stop=(layer == 0 and k == HALVES - 1))
                        if layer > 0:
                            ins = pe.matmul(to, c_row[0:1, m * P:(m + 1) * P], deg_row[0:1, bass.ds(idx * NODES_B, size)],
                                            start=False, stop=True)
                    ins.then_inc(hid_summed, 1)

                def mlp_second(idx, size, is_short=False):
                    b = layer * BLOCKS + idx
                    from_hid, _, _, banks = places(is_short)
                    gate(pe, hid_ready, b + 2)
                    if not is_short:
                        gate(pe, u_ready, b + 1)
                    for m in range(HALVES):
                        for k in range(HALVES):
                            ins = pe.matmul(banks[1][:, m * NODES_B:m * NODES_B + size], wgt(layer, 1, k, m), from_hid[:, k, 0:size],
                                            start=(k == 0), stop=(k == HALVES - 1))
                    ins.then_inc(out_summed, 1)

                def mlp_turn(idx, size, is_short=False):
                    b = layer * BLOCKS + idx
                    _, from_u, _, banks = places(is_short)
                    if layer < LAYERS - 1:
                        gate(pe, u_ready, b + 2)
                        if not is_short:
                            gate(pe, u_read, b + 1)
                        for c in range(size // P):
                            for m in range(HALVES):
                                ins = pe.transpose(banks[2][:, c * D + m * P:c * D + (m + 1) * P],
                                                   from_u[:, m, c * P:(c + 1) * P], ident[:, :])
                        ins.then_inc(u_turned, 1)

                if layer > 0:
                    pe.wait_ge(u_read, layer * BLOCKS + 1)
                    pe.wait_ge(bn_ready, layer)
                    for k in range(HALVES):
                        ins = pe.matmul(bank[7][0:1, 0:D], bn_w[:, 4, k:k + 1], w_gnn[:, layer, 0, k, :],
                                        start=(k == 0), stop=(k == HALVES - 1))
                    ins.then_inc(c_summed, 1)
                    pe.wait_ge(wa_scaled, layer)

                with pe.If(general > 0):
                    with pe.Fori(0, GROUPS * CHUNKS) as c:
                        step = (c + layer * GROUPS * CHUNKS) * SLOW_STEPS
                        gate(pe, slow_landed, 16 * (c + layer * GROUPS * CHUNKS + 1))
                        with pe.Fori(0, TILES) as w:
                            pe.wait_ge(turn, step + w * 6 + 4)
                            pe.matmul(bank[0][:, 0:width], onehot[:, 0, 0, :], rows[:, 0, 0:width], start=True, stop=True).then_inc(turn, 1)
                            gate(pe, turn, step + w * 6 + 6)
                            turn_partial(0, turn)
                    pe.wait_ge(turn, (layer + 1) * GROUPS * CHUNKS * SLOW_STEPS + 1)
                    with pe.Fori(0, LOOPS) as i:
                        mlp_first(i, NODES_B)
                        mlp_second(i, NODES_B)
                        mlp_turn(i, NODES_B)
                with pe.Else():
                    with pe.Fori(0, LOOPS) as i:
                        for k in range(2 * HALF_GROUPS):
                            g = layer * GROUPS + 2 * i * HALF_GROUPS + k
                            gate(pe, onehot_ready, g + 1)
                            gate(pe, partial_copied, g + 1)
                            for c in range(CHUNKS):
                                s = k % HALF_GROUPS * CHUNKS + c
                                pe.wait_ge(landed[s], 16 * (layer * 2 * LOOPS + 2 * i + k // HALF_GROUPS + 1))
                                ins = pe.matmul(bank[k % 2][:, 0:width], onehot[:, k % 2, c, :], rows[:, s, 0:width],
                                                start=(c == 0), stop=(c == CHUNKS - 1))
                            ins.then_inc(summed, 1)
                            if k > 0:
                                turn_sums(g - 1, (k - 1) % 2)
                            if k == HID_AT:
                                gate(pe, added, layer * GROUPS + i * 2 * HALF_GROUPS + 2)
                                mlp_first(i, NODES_B)
                            if k == OUT_AT:
                                mlp_second(i, NODES_B)
                            if k == TURN_AT:
                                mlp_turn(i, NODES_B)
                        turn_sums(g, k % 2)
                    pe.wait_ge(added, (layer + 1) * GROUPS + 2)
                    pe.sem_inc(gate_passed, 1)
                pe.end_ifs()
                for step in (mlp_first, mlp_second, mlp_turn):
                    step(LOOPS, NODES_B)
                    step(LOOPS + 1, P, True)

            pe.wait_ge(u_ready, LAYERS * BLOCKS + 1)
            pe.wait_ge(u_read, (LAYERS - 1) * BLOCKS + 1)
            pe.wait_ge(wa_scaled, LAYERS - 1)
            def turn_pair(p, to, src, done):
                for n, j in enumerate(pair_tiles(p)):
                    for m in range(HALVES):
                        ins = pe.transpose(to[:, n * D + m * P:n * D + (m + 1) * P], src(j, m), ident[:, :])
                ins.then_inc(done, 1)

            def h_turn(i):
                pe.wait_ge(h_normed, i + 1)
                pe.sem_inc(gate_passed, 1)
                for p in range(PAIRS):
                    gate(pe, h_read, i * PAIRS + p + 1)
                    turn_pair(p, bank[p], lambda j, m: fm[:, j, m, :], h_turned)

            def score(i, meanwhile=None):
                def scores(p):
                    pe.wait_ge(tok_copied, i * PAIRS + p + 1 + PAIRS)
                    pe.sem_inc(gate_passed, 1)
                    tiles = pair_tiles(p)
                    for n, j in enumerate(tiles):
                        for m in range(HALVES):
                            ins = pe.matmul(bank[7][:, bass.ds((i * BATCH + j) * EXPERTS, EXPERTS)],
                                            tok_slot(p, len(tiles))[:, n, m * P:(m + 1) * P], gate_w[:, m, :],
                                            start=(m == 0), stop=(m == HALVES - 1))
                    ins.then_inc(tok_scored, 1)

                def turn_tokens(p):
                    gate(pe, tok_normed, i * BATCH + pair_tiles(p)[-1] + 1)
                    gate(pe, tok_copied, pair_before(i, p))
                    turn_pair(p, bank[4 + p % 3], lambda j, m: nm[:, j, m * P:(m + 1) * P], tok_turned)

                for p in range(PAIRS - 1):
                    turn_tokens(p)
                scores(0)
                turn_tokens(PAIRS - 1)
                if meanwhile is not None:
                    h_turn(meanwhile)
                for p in range(1, PAIRS):
                    scores(p)

            def count(part):
                pe.wait_ge(chosen, part + 1)
                lo, hi = ROUTED[part]
                n = (hi - lo) * EXPERTS
                pe.matmul(bank[4][:, 0:n], upto[:, :], route_place(part, 4), start=True, stop=True).then_inc(counted, 1)
                pe.matmul(bank[5][:, 0:n], ones[:, :], route_place(part, 4), start=True, stop=True).then_inc(counted, 1)
                pe.wait_ge(routed, part + 1)

            h_turn(0)
            h_turn(1)
            with pe.Fori(0, SPLIT) as i:
                score(i, i + 2)
            count(0)
            score(BATCHES - 2)
            score(BATCHES - 1)
            count(1)

            def turn_buf(i, s, c):
                gate(pe, bufT_copied, (2 * i + s) * CT + c + 1)
                for k in range(HALVES):
                    ins = pe.transpose(bank[6 + c % 2][:, k * P:(k + 1) * P], buf[:, s, c, k * P:(k + 1) * P], ident[:, :])
                ins.then_inc(bufT_turned, 1)

            def expert(i, s, last=False):
                e = 2 * i + s
                gate(pe, w_lo[0], e + 1)
                for q in range(2 * FC):
                    n, f = q // FC, q % FC
                    cols = HALF_COLS[n]
                    if f == 0:
                        gate(pe, bufT_copied, e * CT + (CT if n else HALF_T) + 2)
                    gate(pe, f_read, e * 2 * FC + q + 1)
                    for k in range(HALVES):
                        for a, b in ((0, 0), (0, 1), (1, 0)):
                            ins = pe.matmul(bank[q % 4][:, 0:cols],
                                            w_parts[:, 0, a, k * FF + f * P:k * FF + (f + 1) * P],
                                            bufT_parts[:, b, k, n * HALF_T * P:n * HALF_T * P + cols],
                                            start=(k == 0 and a + b == 0), stop=(k == HALVES - 1 and a == 1))
                    ins.then_inc(f_summed, 1)
                gate(pe, w_lo[1], e + 1)
                if not last:
                    ni, ns = queue_no(i, s)
                    gate(pe, buf_in[ns], 16 * (ni + 1))
                for c in range(CT):
                    if not last:
                        turn_buf(ni, ns, c)
                    n, at = c // HALF_T, c % HALF_T * P
                    if at == 0:
                        gate(pe, f_split, e * 2 * FC + (n + 1) * FC)
                    m = LAST_M if c == CT - 1 else P
                    gate(pe, y_added, e * CT + c + 1)
                    for f in range(FC):
                        for a, b in ((0, 0), (0, 1), (1, 0)):
                            ins = pe.matmul(bank[4 + c % 2][0:m, 0:D], hmid_parts[n][:, a, f, at:at + m],
                                            w_parts[:, 1, b, f * D:(f + 1) * D],
                                            start=(f == 0 and a + b == 0), stop=(f == FC - 1 and a == 1))
                    ins.then_inc(y_summed, 1)

            pe.wait_ge(buf_in[0], 16)
            for c in range(CT):
                turn_buf(0, 0, c)
            with pe.Fori(0, EXPERTS // 2 - 1) as i:
                for s in range(2):
                    expert(i, s)
            expert(EXPERTS // 2 - 1, 0)
            expert(EXPERTS // 2 - 1, 1, True)

        @block.vector
        def _(dve):
            steps = 0

            def link(ins):
                nonlocal steps
                steps += 1
                ins.then_inc(prep, 1)
                dve.wait_ge(prep, steps)

            dve.sem_inc(added, 2)
            dve.sem_inc(u_kept, 1)
            dve.sem_inc(u_read, 1)
            dve.sem_inc(x_in_agg[0], len(X_TILES[0]))
            dve.sem_inc(tok_copied, PAIRS)
            dve.sem_inc(h_read, PAIRS)
            dve.sem_inc(bufT_copied, 2)
            dve.sem_inc(y_added, 2)

            G = slice(0, GROWS)
            dve.wait_ge(edges_in, 16 * 6)
            dve.tensor_copy(src_f[G], src_i[G])
            link(dve.tensor_copy(dst_f[G], dst_i[G]))
            link(dve.tensor_scalar(key_f[G], dst_f[G], 0.0, 65536.0, ALU.is_lt, ALU.mult))
            link(dve.tensor_tensor(key_f[G], key_f[G], dst_f[G], ALU.add))
            link(dve.tensor_reduce(base[G, :], key_f[G], AX.X, ALU.min))
            for q in range(2):
                link(dve.tensor_scalar(rel_f[G, q], dst_f[G, q], base[G, q:q + 1], None, ALU.subtract))
            link(dve.tensor_scalar(key_f[G], rel_f[G], float(P), None, ALU.is_ge))
            link(dve.tensor_reduce(any_far[G, :], key_f[G], AX.XY, ALU.max))
            dve.sem_inc(edges_ready, 1)
            dve.wait_ge(consts, CONSTS)
            link(dve.tensor_copy(iota[:, :], iota_i[:, :]))
            for a, cols in enumerate((idx_cols, rel_cols, dst_cols)):
                for q in range(2):
                    dve.wait_ge(prep_turned, 2 * a + q + 1)
                    to = cols[:, 0:GROUPS * CHUNKS].rearrange("p (g c) -> p c g", c=CHUNKS)[:, :, q * GROWS:(q + 1) * GROWS]
                    turned_edges = bank[2 * a + q][:, 0:CHUNKS * GROWS].rearrange("p (c g) -> p c g", c=CHUNKS)
                    link(dve.tensor_scalar(to, turned_edges, float(FRONT if a == 0 else 0), None, ALU.add))
            link(dve.tensor_copy(rel_cols[:, GROUPS * CHUNKS:], rel_cols[:, 0:CHUNKS]))
            dve.wait_ge(prep_turned, 7)
            dve.tensor_copy(base_row[:, :], bank[6][0:1, 0:GROUPS]).then_inc(tables_ready, 1)
            link(dve.tensor_copy(late_row[:, 0, :], least_i[:, :]))
            link(dve.tensor_copy(late_row[:, 1, :], bank[6][0:1, 0:GROUPS]))
            link(dve.tensor_tensor(late_row[:, 2, :], late_row[:, 1, :], late_row[:, 0, :], ALU.is_lt))
            link(dve.tensor_reduce(general_f[:, 0:1], late_row[:, 2, :], AX.X, ALU.max))
            link(dve.tensor_reduce(general_f[:, 1:2], bank[6][0:1, GROUPS:GROUPS + GROWS], AX.X, ALU.max))
            link(dve.tensor_tensor(general_f[:, 2:3], general_f[:, 0:1], general_f[:, 1:2], ALU.max))
            dve.tensor_copy(general_flag[:, :], general_f[:, 2:3]).then_inc(tables_ready, 1)
            dve.wait_ge(tables_ready, 2)

            LN_STEPS = BATCH + 6

            def ln_stats(nb, j, tile):
                dve.bn_stats(ln_st[:, j, :], tile).then_inc(ln_steps, 1)

            def ln_finish(nb):
                s0 = nb * LN_STEPS
                col = lambda c: ln_st[:, :, c]
                w = lambda r: ln_w[:, r, :]
                gate(dve, ln_steps, s0 + BATCH)
                dve.tensor_tensor(w(0), col(1), col(4), ALU.add).then_inc(ln_steps, 1)
                dve.tensor_tensor(w(1), col(1), col(4), ALU.subtract).then_inc(ln_steps, 1)
                dve.tensor_tensor(w(2), col(2), col(5), ALU.add).then_inc(ln_steps, 1)
                gate(dve, ln_steps, s0 + BATCH + 3)
                dve.tensor_tensor(w(3), w(1), w(1), ALU.mult).then_inc(ln_steps, 1)
                dve.tensor_scalar(w(4), w(2), 1.0 / D, EPS, ALU.mult, ALU.add).then_inc(ln_steps, 1)
                gate(dve, ln_steps, s0 + BATCH + 5)
                dve.scalar_tensor_tensor(out=w(5), in0=w(3), scalar=0.25, in1=w(4), op0=ALU.mult, op1=ALU.add).then_inc(ln_var, 1)
                gate(dve, ln_std, nb + 1)
                dve.reciprocal(w(7), w(6)).then_inc(ln_steps, 1)
                gate(dve, ln_steps, s0 + BATCH + 6)
                dve.scalar_tensor_tensor(out=w(8), in0=w(0), scalar=-0.5, in1=w(7), op0=ALU.mult, op1=ALU.mult).then_inc(ln_ready, 1)

            def x_scales(i):
                for j in range(BATCH):
                    ln_stats(i, j, x_sb[:, bass.ds(i * BATCH + j, 1), :].rearrange("p a d -> p (a d)"))
                ln_finish(i)

            dve.wait_ge(x_in[0], 16)
            x_scales(0)
            dve.wait_ge(x_in[1], 16 * BATCHES)
            with dve.Fori(1, BATCHES) as i:
                x_scales(i)
                x_into_agg(dve, dve.tensor_copy, 0, i - 1)
            x_into_agg(dve, dve.tensor_copy, 0, BATCHES - 1)
            dve.wait_ge(vecs_turned, 1)
            dve.tensor_copy(vecs[:, :], bank[7][:, 0:NVEC]).then_inc(vecs_ready, 1)
            dve.wait_ge(counts_set, 1)
            for which, tiles in enumerate(X_TILES):
                dve.wait_ge(x_in_agg[which], (BATCHES + 1) * len(tiles))

            general = dve.value_load(general_flag[0:1, 0:1], min_val=0, max_val=1)
            for j in range(3):
                dve.wait_ge(stored[j], 16 * BATCHES)
            for layer in range(LAYERS):
                def add_window(first, par, done):
                    if layer == 0:
                        counts = deg_row[0:1, bass.ds(first, P)]
                        dve.tensor_tensor(counts, counts, bank[2 + par][0:1, D:D + P], ALU.add)
                    window = agg[:, :, bass.ds(first, P)]
                    dve.tensor_tensor(window, window, bank[2 + par][:, 0:D].rearrange("p (m n) -> p m n", m=HALVES),
                                      ALU.add).then_inc(done, 1)

                def one_hots(g, gl, par):
                    dve.wait_ge(summed, g - 2 + 1 + 4)
                    dve.tensor_tensor(onehot[:, par], iota[:, :].unsqueeze(1).to_broadcast([P, CHUNKS, P]),
                                      rel_cols[:, bass.ds(gl * CHUNKS, CHUNKS)].unsqueeze(2).to_broadcast([P, CHUNKS, P]),
                                      ALU.is_equal).then_inc(onehot_ready, 1)

                def add_sums(g, gl, par):
                    first = dve.value_load(base_row[0:1, bass.ds(gl, 1)], min_val=0, max_val=N - 1)
                    gate(dve, added, g + 2)
                    gate(dve, sums_turned, g + 1 + 2)
                    add_window(FRONT + first, par, added)

                def mlp_keep(idx, size, real, is_short=False):
                    b = layer * BLOCKS + idx
                    u = places(is_short)[1]
                    gate(dve, u_ready, b + 2)
                    for m in range(HALVES):
                        dve.bn_stats(bn_st[:, m, bass.ds(idx, 1), :].rearrange("p a s -> p (a s)"), u[:, m, 0:real])
                    dve.tensor_copy(agg[:, :, bass.ds(idx * NODES_B, size)], u[:, :, 0:size]).then_inc(u_kept, 1)

                def mlp_rows(idx, size, is_short=False):
                    b = layer * BLOCKS + idx
                    _, _, to, banks = places(is_short)
                    if layer < LAYERS - 1:
                        if is_short:
                            gate(dve, stored[1], 16 * (BATCHES + layer))
                        else:
                            gate(dve, stored[0], 16 * (BATCHES + layer * (BLOCKS - 1) + idx))
                        gate(dve, u_turned, b + 2)
                        dve.tensor_copy(to.rearrange("p c d -> p (c d)"), banks[2][:, 0:size // P * D]).then_inc(u_read, 1)

                with dve.If(general > 0):
                    if layer == 0:
                        dve.sem_inc(turn, 1)
                    with dve.Fori(0, GROUPS * CHUNKS) as c:
                        step = (c + layer * GROUPS * CHUNKS) * SLOW_STEPS
                        gate(dve, turn, step + 1)
                        dve.tensor_copy(slow_idx[:, :], idx_cols[:, bass.ds(c, 1)]).then_inc(turn, 1)
                        dve.tensor_copy(slow_rel[:, :], dst_cols[:, bass.ds(c, 1)]).then_inc(turn, 1)
                        with dve.Fori(0, TILES) as w:
                            dve.wait_ge(turn, step + w * 6 + 3)
                            dve.tensor_scalar(onehot[:, 0, 0, :], iota[:, :], slow_rel[:, 0:1], None, ALU.is_equal).then_inc(turn, 1)
                            gate(dve, turn, step + w * 6 + 7)
                            add_window(FRONT + w * P, 0, turn)
                            dve.wait_ge(turn, step + w * 6 + 8)
                            dve.tensor_scalar(slow_rel[:, :], slow_rel[:, :], float(P), None, ALU.subtract).then_inc(turn, 1)
                    dve.wait_ge(turn, (layer + 1) * GROUPS * CHUNKS * SLOW_STEPS + 1)
                    with dve.Fori(0, LOOPS) as i:
                        mlp_keep(i, NODES_B, NODES_B)
                        mlp_rows(i, NODES_B)
                with dve.Else():
                    dve.tensor_copy(idx_now[:, 0, :], idx_cols[:, 0:SLOTS]).then_inc(idx_staged, 1)
                    if layer == 0:
                        one_hots(0, 0, 0)
                    with dve.Fori(0, LOOPS) as i:
                        for k in range(2 * HALF_GROUPS):
                            gl = 2 * i * HALF_GROUPS + k
                            if k == 0:
                                dve.tensor_copy(idx_now[:, 1, :],
                                                idx_cols[:, bass.ds((2 * i + 1) * SLOTS, SLOTS)]).then_inc(idx_staged, 1)
                            one_hots(layer * GROUPS + gl + 1, gl + 1, (k + 1) % 2)
                            if k > 0:
                                add_sums(layer * GROUPS + gl - 1, gl - 1, (k - 1) % 2)
                            if k == HALF_GROUPS:
                                dve.tensor_copy(idx_now[:, 0, :],
                                                idx_cols[:, bass.ds((2 * i + 2) * SLOTS, SLOTS)]).then_inc(idx_staged, 1)
                            if k == KEEP_AT:
                                mlp_keep(i, NODES_B, NODES_B)
                            if k == ROWS_AT:
                                mlp_rows(i, NODES_B)
                        add_sums(layer * GROUPS + gl, gl, k % 2)
                dve.end_ifs()
                mlp_rows(LOOPS, NODES_B)
                mlp_rows(LOOPS + 1, P, True)
                mlp_keep(LOOPS, NODES_B, NODES_B)
                mlp_keep(LOOPS + 1, P, TAIL, True)

                dve.wait_ge(u_kept, (layer + 1) * BLOCKS + 1)
                for m in range(HALVES):
                    link(dve.bn_aggr(bn_mv[:, m, :], bn_st[:, m, LAG:, :].rearrange("p b s -> p (b s)")))
                c = VEC0 + (layer * 4 + 2) * HALVES
                gamma, beta = vecs[:, c:c + HALVES], vecs[:, c + HALVES:c + 2 * HALVES]
                if layer > 0:
                    dve.wait_ge(wa_scaled, layer)
                dve.tensor_scalar(bn_w[:, 0, :], bn_mv[:, :, 1], EPS, None, ALU.add).then_inc(bn_var, 1)
                dve.wait_ge(bn_std, layer + 1)
                link(dve.reciprocal(bn_w[:, 2, :], bn_w[:, 1, :]))
                link(dve.tensor_tensor(bn_w[:, 3, :], bn_w[:, 2, :], gamma, ALU.mult))
                link(dve.tensor_tensor(bn_w[:, 5, :], bn_mv[:, :, 0], bn_w[:, 3, :], ALU.mult))
                dve.tensor_tensor(bn_w[:, 4, :], beta, bn_w[:, 5, :], ALU.subtract).then_inc(bn_ready, 1)

            def add_h(i):
                for p in range(PAIRS):
                    n = len(pair_tiles(p))
                    x_pair = x_sb[:, bass.ds(i * BATCH + 2 * p, n), :].rearrange("p a d -> p (a d)")
                    gate(dve, h_turned, i * PAIRS + p + 1)
                    dve.tensor_tensor(x_pair, x_pair, bank[p][:, 0:n * D], ALU.add).then_inc(h_read, 1)
                for j in range(BATCH):
                    gate(dve, h_read, i * PAIRS + j // 2 + 1 + PAIRS)
                    ln_stats(i + BATCHES, j, x_sb[:, bass.ds(i * BATCH + j, 1), :].rearrange("p a d -> p (a d)"))
                ln_finish(i + BATCHES)

            def copy_tokens(i):
                for p in range(PAIRS):
                    n = len(pair_tiles(p))
                    gate(dve, tok_turned, i * PAIRS + p + 1 + PAIRS)
                    gate(dve, tok_scored, pair_before(i, p))
                    dve.tensor_copy(tok_slot(p, n), bank[4 + p % 3][:, 0:n * D].rearrange("p (c w) -> p c w", w=D)).then_inc(tok_copied, 1)

            def by_tile(flat):
                return flat.rearrange("p (t e) -> p t e", e=EXPERTS)

            SHIFTED_MAX, SUM, INV, PROB, CHOICE_8, CHOICE, REAL, PLACE, KEPT, SENT, ROW_S, ROW_T = range(12)

            def route_part(part):
                lo, hi = ROUTED[part]
                n = (hi - lo) * EXPERTS
                r_a, r_b, r_c, r_d, r_e, r_f, r_g = (route_place(part, k) for k in range(7))

                def row(r):
                    return route[:, r, lo:hi]

                def wide(r):
                    return row(r).unsqueeze(2).to_broadcast([P, hi - lo, EXPERTS])

                dve.wait_ge(tok_scored, PAIRS * (hi // BATCH + 1))
                if part == 1:
                    for j in range(BATCH):
                        dve.wait_ge(tok_kept[j], 16 * (BATCHES + 1))
                link(dve.tensor_tensor(by_tile(r_a), by_tile(bank[7][:, lo * EXPERTS:hi * EXPERTS]),
                                       gate_b[:, :].unsqueeze(1).to_broadcast([P, hi - lo, EXPERTS]), ALU.add))
                link(dve.tensor_reduce(row(SHIFTED_MAX), by_tile(r_a), AX.X, ALU.max))
                dve.tensor_tensor(by_tile(r_b), by_tile(r_a), wide(SHIFTED_MAX), ALU.subtract).then_inc(exp_in, 1)
                dve.wait_ge(exp_done, part + 1)
                link(dve.tensor_reduce(row(SUM), by_tile(r_c), AX.X, ALU.add))
                link(dve.reciprocal(row(INV), row(SUM)))
                link(dve.tensor_tensor(by_tile(r_a), by_tile(r_c), wide(INV), ALU.mult))
                link(dve.tensor_reduce(row(PROB), by_tile(r_a), AX.X, ALU.max))
                link(dve.tensor_tensor(by_tile(r_b), by_tile(r_a), wide(PROB), ALU.is_equal))
                link(dve.tensor_copy(r_g, exp_i[:, lo * EXPERTS:hi * EXPERTS]))
                link(dve.scalar_tensor_tensor(out=r_d, in0=r_b, scalar=-float(EXPERTS), in1=r_g, op0=ALU.mult, op1=ALU.add))
                link(dve.tensor_reduce(row(CHOICE_8), by_tile(r_d), AX.X, ALU.min))
                link(dve.tensor_scalar(row(CHOICE), row(CHOICE_8), float(EXPERTS), None, ALU.add))
                link(dve.tensor_copy(row(ROW_S), tok_i[:, lo:hi]))
                link(dve.tensor_scalar(row(REAL), row(ROW_S), float(N), None, ALU.is_lt))
                link(dve.tensor_tensor(by_tile(r_d), by_tile(r_g), wide(CHOICE), ALU.is_equal))
                dve.tensor_tensor(by_tile(r_e), by_tile(r_d), wide(REAL), ALU.mult).then_inc(chosen, 1)
                dve.wait_ge(counted, 2 * (part + 1))
                link(dve.tensor_copy(r_f, bank[5][:, 0:n]))
                for e in range(EXPERTS):
                    dve.tensor_tensor_scan(r_a[:, e:n:EXPERTS], ones[:, 0:hi - lo], r_f[:, e:n:EXPERTS], 0.0, ALU.mult, ALU.add).then_inc(scanned, 1)
                dve.wait_ge(scanned, (part + 1) * EXPERTS)
                if part == 0:
                    link(dve.tensor_copy(queued[:, :], r_a[:, n - EXPERTS:n]))
                else:
                    link(dve.tensor_tensor(by_tile(r_a), by_tile(r_a), queued[:, :].unsqueeze(1).to_broadcast([P, hi - lo, EXPERTS]), ALU.add))
                link(dve.tensor_tensor(r_a, r_a, r_f, ALU.subtract))
                link(dve.tensor_tensor(r_a, r_a, bank[4][:, 0:n], ALU.add))
                link(dve.tensor_tensor(r_a, r_a, r_e, ALU.mult))
                link(dve.tensor_reduce(row(PLACE), by_tile(r_a), AX.X, ALU.add))
                link(dve.tensor_scalar(row(KEPT), row(PLACE), float(CAP), None, ALU.is_le))
                link(dve.tensor_tensor(row(SENT), row(KEPT), row(REAL), ALU.mult))
                link(dve.scalar_tensor_tensor(out=row(ROW_S), in0=row(CHOICE), scalar=float(CAPP), in1=row(PLACE), op0=ALU.mult, op1=ALU.add))
                link(dve.scalar_tensor_tensor(out=row(ROW_T), in0=row(ROW_S), scalar=-float(NO_SLOT + 1), in1=row(SENT), op0=ALU.add, op1=ALU.mult))
                link(dve.tensor_scalar(scatter_idx[:, lo:hi], row(ROW_T), float(NO_SLOT), None, ALU.add))
                link(dve.tensor_copy(tokens[:, lo:hi, D:D + 1].bitcast(I32), tok_i[:, lo:hi].unsqueeze(2)))
                dve.tensor_copy(tokens[:, lo:hi, D + 1:D + 2], row(PROB).unsqueeze(2)).then_inc(routed, 1)

            add_h(0)
            with dve.Fori(1, SPLIT + 1) as i:
                add_h(i)
                copy_tokens(i - 1)
            route_part(0)
            add_h(BATCHES - 1)
            copy_tokens(BATCHES - 2)
            copy_tokens(BATCHES - 1)
            route_part(1)

            def lo_weights(w, e):
                gate(dve, w_hi[w], e + 1)
                dve.tensor_tensor(w_parts[:, w, 1, :], w_exp[:, w, 1, :], w_parts[:, w, 0, :].bitcast(F32), ALU.subtract).then_inc(w_lo[w], 1)

            def split_buf(i, s, c):
                t_no = (2 * i + s) * CT + c + 1
                turned_tile = bank[6 + c % 2][:, 0:D].rearrange("p (k n) -> p k n", k=HALVES)
                hi, lo = (bufT_parts[:, o, :, c * P:(c + 1) * P] for o in range(2))
                gate(dve, bufT_turned, t_no)
                dve.tensor_copy(hi, turned_tile).then_inc(bufT_hi, 1)
                gate(dve, bufT_hi, t_no)
                dve.tensor_tensor(lo, turned_tile, hi.bitcast(F32), ALU.subtract).then_inc(bufT_copied, 1)

            def finish_pair(i, s, r):
                e = 2 * i + s
                y2 = y_out[:, 2 * r:2 * r + 2, :].rearrange("p c d -> p (c d)")
                x2 = xrows[:, 2 * r:2 * r + 2, :].rearrange("p c d -> p (c d)")
                step = (e * RPAIRS + r) * 3
                gate(dve, y_weighted, e * CT + 2 * r + 2)
                if isinstance(e, int) and step == 0:
                    pass
                else:
                    gate(dve, y_done, e * RPAIRS + r)
                dve.tensor_scalar(finite, y2, 0.0, 0.0, ALU.mult, ALU.is_equal)
                dve.tensor_scalar(safe, y2, 1e4, -1e4, ALU.min, ALU.max).then_inc(fix, 1)
                gate(dve, fix, step + 1)
                dve.scalar_tensor_tensor(out=safe, in0=y2, scalar=NEG_INF, in1=safe, op0=ALU.is_ge, op1=ALU.mult).then_inc(fix, 1)
                gate(dve, fix, step + 2)
                dve.copy_predicated(safe, finite, y2).then_inc(fix, 1)
                gate(dve, fix, step + 3)
                for c in (2 * r, 2 * r + 1):
                    gate(dve, xrow_in[c], 16 * (e + 1))
                dve.tensor_tensor(x2, x2, safe, ALU.add).then_inc(y_done, 1)

            def expert(i, s, first=False, last=False):
                e = 2 * i + s
                pi, ps = (i, 0) if s == 1 else (i - 1, 1)
                ni, ns = queue_no(i, s)
                for q in range(2 * FC):
                    n, f = q // FC, q % FC
                    cols = HALF_COLS[n]
                    gate(dve, f_read, e * 2 * FC + q + 1 + 4)
                    whole = hmid[n][:, 1, f, 0:cols]
                    dve.tensor_tensor(hmid_parts[n][:, 1, f, 0:cols], whole, hmid_parts[n][:, 0, f, 0:cols].bitcast(F32), ALU.subtract).then_inc(f_split, 1)
                    if q == FC - 1:
                        lo_weights(1, e)
                    if not first and q in FINISH_AT[:RPAIRS - 1]:
                        finish_pair(pi, ps, FINISH_AT.index(q) + 1)
                gate(dve, b2_in[s], 16 * (i + 1))
                for c in range(CT):
                    if not last:
                        if c == 0:
                            take_numbers(ni, ns)
                        split_buf(ni, ns, c)
                    gate(dve, y_summed, e * CT + c + 1)
                    if not first and c % 2 == 0:
                        gate(dve, y_done, (e - 1) * RPAIRS + c // 2 + 1)
                    m = LAST_M if c == CT - 1 else P
                    dve.tensor_tensor(y_out[0:m, c, :], bank[4 + c % 2][0:m, 0:D], b2_rows[0:m, s], ALU.add).then_inc(y_added, 1)
                    if c == W_AT + 1 and not last:
                        lo_weights(0, e + 1)
                    if last and c % 2 == 1 and c > 1:
                        finish_pair(i, s, c // 2 - 1)
                if not last:
                    finish_pair(i, s, 0)

            def take_numbers(i, s):
                e = 2 * i + s
                gate(dve, buf_in[s], 16 * (i + 1))
                if not (isinstance(e, int) and e < 2):
                    for c in range(CT):
                        gate(dve, result_out[c], 16 * (e - 1))
                dve.tensor_copy(numbers[:, s, :], buf[:, s, :, D:D + 1].bitcast(I32).rearrange("p c o -> p (c o)")).then_inc(numbered, 1)
                dve.tensor_copy(weights[:, s, :], buf[:, s, :, D + 1:D + 2].rearrange("p c o -> p (c o)")).then_inc(numbered, 1)

            lo_weights(0, 0)
            dve.wait_ge(y_cleared, 1)
            take_numbers(0, 0)
            for c in range(CT):
                split_buf(0, 0, c)
            expert(0, 0, first=True)
            expert(0, 1)
            with dve.Fori(1, EXPERTS // 2 - 1) as i:
                for s in range(2):
                    expert(i, s)
            expert(EXPERTS // 2 - 1, 0)
            expert(EXPERTS // 2 - 1, 1, last=True)
            finish_pair(EXPERTS // 2 - 1, 1, RPAIRS - 1)


_INS = ["x", "src", "dst"] + [f"L0_gnn_{n}" for l in (1, 2, 3) for n in
                              (f"W{l}a", f"b{l}a", f"W{l}b", f"b{l}b", f"g{l}", f"be{l}")] + \
       [f"L0_ffn_{n}" for n in ("gate_w", "gate_b", "w1", "b1", "w2", "b2")]


def kernel(**inputs):
    import numpy as _np
    import concourse.bacc as _bacc
    from concourse import mybir as _mybir
    from concourse.bass_utils import run_bass_kernel_spmd as _run

    nc = _bacc.Bacc("TRN2", target_bir_lowering=False, num_devices=1)
    arrays, args = {}, {}
    for name in _INS:
        a = _np.ascontiguousarray(inputs[name])
        arrays[f"in_{name}_dram"] = a
        args[name] = nc.dram_tensor(f"in_{name}_dram", a.shape, _mybir.dt.from_np(a.dtype), kind="ExternalInput").ap()
    out = nc.dram_tensor("out_dram", (N, D), _mybir.dt.float32, kind="ExternalOutput").ap()
    gnn_moe_program(nc, args, out)
    r = _run(nc, [arrays], core_ids=[0])
    return r.results[0]["out_dram"]
```
